# Optimizing a Trainium2 kernel written in Bass

```python
import numpy as np
import jax
import jax.numpy as jnp

def _softmax(x, axis=-1):
    return jax.nn.softmax(x, axis=axis)

def _gelu(x):
    return jax.nn.gelu(x, approximate=True)

def _silu(x):
    return jax.nn.silu(x)

def _sigmoid(x):
    return jax.nn.sigmoid(x)

def _layernorm(x, axis=-1, eps=1e-05):
    m = jnp.mean(x, axis=axis, keepdims=True)
    v = jnp.var(x, axis=axis, keepdims=True)
    return (x - m) / jnp.sqrt(v + eps)

def _scatter_add(tgt, idx, src, axis=0):
    return tgt.at[idx].add(src)

def _segment_sum(src, seg, n):
    return jax.ops.segment_sum(src, seg, n)
kernel_name = 'mk_gnn_ffn_d2_gnn_r8_d41df2'

def setup_inputs(seed: int=0):
    np.random.seed(seed)
    _w = jnp.asarray

    def _rec_inputs():
        import jax
        import jax.numpy as jnp
        _gk = jax.random.key(seed)
        x = -0.0003713 + 1 * jax.random.normal(jax.random.fold_in(_gk, 1), (6250, 256), jnp.float32)
        src = jax.random.randint(jax.random.fold_in(_gk, 2), (100000,), 0, 6250, jnp.int32)
        dst = jnp.minimum((6250 * jax.random.uniform(jax.random.fold_in(_gk, 3), (100000,)) ** 2.0).astype(jnp.int32), 49999)
        _o = jnp.argsort(dst, stable=True)
        src = src[_o]
        dst = dst[_o]
        edge_weight = jax.random.uniform(jax.random.fold_in(_gk, 13), (100000,), jnp.float32, 0.0, 0.03125)
        return (x, src, dst, edge_weight)
    x, src, dst, edge_weight = _rec_inputs()

    def _L0_gnn_setup():
        import jax, jax.numpy as jnp
        import numpy as np
        N_NODES = 6250
        N_EDGES = 100000
        IN_FEATS = 256
        HID = 64
        HEADS = 4
        OUT = 64

        def _gat_layer(x, src, dst, W, a_s, a_d, b, num_nodes):
            H, F = a_s.shape
            h = (x @ W).reshape(num_nodes, H, F)
            al_s = jnp.einsum('nhf,hf->nh', h, a_s)
            al_d = jnp.einsum('nhf,hf->nh', h, a_d)
            e = jax.nn.leaky_relu(al_s[src] + al_d[dst], 0.2)
            emax = jax.ops.segment_max(e, dst, num_segments=num_nodes)
            emax = jnp.where(jnp.isfinite(emax), emax, 0.0)
            ee = jnp.exp(e - emax[dst])
            denom = jax.ops.segment_sum(ee, dst, num_segments=num_nodes)
            alpha = ee / (denom[dst] + 1e-16)
            out = jax.ops.segment_sum(alpha[:, :, None] * h[src], dst, num_segments=num_nodes)
            return out.reshape(num_nodes, H * F) + b
        key = jax.random.key(seed)
        ks = jax.random.split(key, 16)
        p = lambda k, shape: jax.random.normal(k, shape, dtype=jnp.float32) * 0.05
        return {'x': jax.random.normal(ks[0], (N_NODES, IN_FEATS), dtype=jnp.float32), 'edge_index': jax.random.randint(ks[1], (2, N_EDGES), 0, N_NODES), 'W0': p(ks[2], (IN_FEATS, HEADS * HID)), 'as0': p(ks[3], (HEADS, HID)), 'ad0': p(ks[4], (HEADS, HID)), 'b0': jnp.zeros((HEADS * HID,), jnp.float32), 'W1': p(ks[5], (HEADS * HID, HEADS * HID)), 'as1': p(ks[6], (HEADS, HID)), 'ad1': p(ks[7], (HEADS, HID)), 'b1': jnp.zeros((HEADS * HID,), jnp.float32), 'W2': p(ks[8], (HEADS * HID, HEADS * OUT)), 'as2': p(ks[9], (HEADS, OUT)), 'ad2': p(ks[10], (HEADS, OUT)), 'b2': jnp.zeros((HEADS * OUT,), jnp.float32)}
    _L0_gnn_all = _L0_gnn_setup()
    _L0_gnn_in = {k: v for k, v in _L0_gnn_all.items() if k in ('W0', 'as0', 'ad0', 'b0', 'W1', 'as1', 'ad1', 'b1', 'W2', 'as2', 'ad2', 'b2')}
    del _L0_gnn_all

    def _L0_ffn_setup():
        import jax, jax.numpy as jnp
        import numpy as np
        B, S, D, F, E, K = (8, 256, 256, 1024, 8, 2)
        key = jax.random.key(seed)
        ks = jax.random.split(key, 10)
        s = 0.02
        return {'x': jax.random.normal(ks[0], (B, S, D), dtype=jnp.float32), 'Wr': jax.random.normal(ks[1], (D, E), dtype=jnp.float32) * s, 'W1s': jax.random.normal(ks[2], (D, F), dtype=jnp.float32) * s, 'b1s': jnp.zeros((F,), dtype=jnp.float32), 'W2s': jax.random.normal(ks[3], (F, D), dtype=jnp.float32) * s, 'b2s': jnp.zeros((D,), dtype=jnp.float32), 'W1p': jax.random.normal(ks[4], (E, D, F), dtype=jnp.float32) * s, 'b1p': jnp.zeros((E, F), dtype=jnp.float32), 'W2p': jax.random.normal(ks[5], (E, F, D), dtype=jnp.float32) * s, 'b2p': jnp.zeros((E, D), dtype=jnp.float32)}
    _L0_ffn_all = _L0_ffn_setup()
    _L0_ffn_in = {k: v for k, v in _L0_ffn_all.items() if k in ('Wr', 'W1s', 'b1s', 'W2s', 'b2s', 'W1p', 'b1p', 'W2p', 'b2p')}
    del _L0_ffn_all

    def _L1_gnn_setup():
        import jax, jax.numpy as jnp
        import numpy as np
        N_NODES = 12500
        N_EDGES = 400000
        DIM = 256
        LEAKY_SLOPE = 0.2
        EPS = 1e-12
        key = jax.random.key(seed)
        ks = jax.random.split(key, 8)
        embeddings = jax.random.normal(ks[0], (N_NODES, DIM), dtype=jnp.float32)
        edge_src = jax.random.randint(ks[1], (N_EDGES,), 0, N_NODES, dtype=jnp.int32)
        edge_dst = jax.random.randint(ks[2], (N_EDGES,), 0, N_NODES, dtype=jnp.int32)
        edge_val = jax.random.uniform(ks[3], (N_EDGES,), dtype=jnp.float32) / 32.0
        scale = 1.0 / np.sqrt(DIM)
        W1 = jax.random.normal(ks[4], (DIM, DIM), dtype=jnp.float32) * scale
        b1 = jax.random.normal(ks[5], (DIM,), dtype=jnp.float32) * 0.01
        W2 = jax.random.normal(ks[6], (DIM, DIM), dtype=jnp.float32) * scale
        b2 = jax.random.normal(ks[7], (DIM,), dtype=jnp.float32) * 0.01
        return {'embeddings': embeddings, 'edge_src': edge_src, 'edge_dst': edge_dst, 'edge_val': edge_val, 'W1': W1, 'b1': b1, 'W2': W2, 'b2': b2}
    _L1_gnn_all = _L1_gnn_setup()
    _L1_gnn_in = {k: v for k, v in _L1_gnn_all.items() if k in ('W1', 'b1', 'W2', 'b2')}
    del _L1_gnn_all

    def _L1_ffn_setup():
        import jax, jax.numpy as jnp
        import numpy as np
        B, A = (512, 8)
        IN, OUT = (256, 256)
        SH1, SH2 = (256, 128)
        EH1, EH2 = (128, 64)
        E, TOPK = (4, 2)

        def _shared_mlp(x, W1, b1, W2, b2, W3, b3):
            h = jax.nn.relu(x @ W1 + b1)
            h = jax.nn.relu(h @ W2 + b2)
            return h @ W3 + b3

        def _experts_mlp(x, eW1, eb1, eW2, eb2, eW3, eb3):
            h = jax.nn.relu(jnp.einsum('baf,efh->ebah', x, eW1) + eb1[:, None, None, :])
            h = jax.nn.relu(jnp.einsum('ebah,ehg->ebag', h, eW2) + eb2[:, None, None, :])
            o = jnp.einsum('ebag,ego->ebao', h, eW3) + eb3[:, None, None, :]
            return jnp.moveaxis(o, 0, -1)
        key = jax.random.key(seed)
        ks = jax.random.split(key, 16)
        s = 0.05
        return {'x': jax.random.normal(ks[0], (B, A, IN), jnp.float32), 'sW1': jax.random.normal(ks[1], (IN, SH1), jnp.float32) * s, 'sb1': jnp.zeros((SH1,), jnp.float32), 'sW2': jax.random.normal(ks[2], (SH1, SH2), jnp.float32) * s, 'sb2': jnp.zeros((SH2,), jnp.float32), 'sW3': jax.random.normal(ks[3], (SH2, OUT), jnp.float32) * s, 'sb3': jnp.zeros((OUT,), jnp.float32), 'eW1': jax.random.normal(ks[4], (E, IN, EH1), jnp.float32) * s, 'eb1': jnp.zeros((E, EH1), jnp.float32), 'eW2': jax.random.normal(ks[5], (E, EH1, EH2), jnp.float32) * s, 'eb2': jnp.zeros((E, EH2), jnp.float32), 'eW3': jax.random.normal(ks[6], (E, EH2, OUT), jnp.float32) * s, 'eb3': jnp.zeros((E, OUT), jnp.float32), 'gW': jax.random.normal(ks[7], (IN, E), jnp.float32) * s, 'gb': jnp.zeros((E,), jnp.float32)}
    _L1_ffn_all = _L1_ffn_setup()
    _L1_ffn_in = {k: v for k, v in _L1_ffn_all.items() if k in ('sW1', 'sb1', 'sW2', 'sb2', 'sW3', 'sb3', 'eW1', 'eb1', 'eW2', 'eb2', 'eW3', 'eb3', 'gW', 'gb')}
    del _L1_ffn_all
    return {'x': x, 'src': src, 'dst': dst, 'edge_weight': edge_weight, 'L0_gnn_W0': _L0_gnn_in['W0'], 'L0_gnn_as0': _L0_gnn_in['as0'], 'L0_gnn_ad0': _L0_gnn_in['ad0'], 'L0_gnn_b0': _L0_gnn_in['b0'], 'L0_gnn_W1': _L0_gnn_in['W1'], 'L0_gnn_as1': _L0_gnn_in['as1'], 'L0_gnn_ad1': _L0_gnn_in['ad1'], 'L0_gnn_b1': _L0_gnn_in['b1'], 'L0_gnn_W2': _L0_gnn_in['W2'], 'L0_gnn_as2': _L0_gnn_in['as2'], 'L0_gnn_ad2': _L0_gnn_in['ad2'], 'L0_gnn_b2': _L0_gnn_in['b2'], 'L0_ffn_Wr': _L0_ffn_in['Wr'], 'L0_ffn_W1s': _L0_ffn_in['W1s'], 'L0_ffn_b1s': _L0_ffn_in['b1s'], 'L0_ffn_W2s': _L0_ffn_in['W2s'], 'L0_ffn_b2s': _L0_ffn_in['b2s'], 'L0_ffn_W1p': _L0_ffn_in['W1p'], 'L0_ffn_b1p': _L0_ffn_in['b1p'], 'L0_ffn_W2p': _L0_ffn_in['W2p'], 'L0_ffn_b2p': _L0_ffn_in['b2p'], 'L1_gnn_W1': _L1_gnn_in['W1'], 'L1_gnn_b1': _L1_gnn_in['b1'], 'L1_gnn_W2': _L1_gnn_in['W2'], 'L1_gnn_b2': _L1_gnn_in['b2'], 'L1_ffn_sW1': _L1_ffn_in['sW1'], 'L1_ffn_sb1': _L1_ffn_in['sb1'], 'L1_ffn_sW2': _L1_ffn_in['sW2'], 'L1_ffn_sb2': _L1_ffn_in['sb2'], 'L1_ffn_sW3': _L1_ffn_in['sW3'], 'L1_ffn_sb3': _L1_ffn_in['sb3'], 'L1_ffn_eW1': _L1_ffn_in['eW1'], 'L1_ffn_eb1': _L1_ffn_in['eb1'], 'L1_ffn_eW2': _L1_ffn_in['eW2'], 'L1_ffn_eb2': _L1_ffn_in['eb2'], 'L1_ffn_eW3': _L1_ffn_in['eW3'], 'L1_ffn_eb3': _L1_ffn_in['eb3'], 'L1_ffn_gW': _L1_ffn_in['gW'], 'L1_ffn_gb': _L1_ffn_in['gb']}

def reference(x, src, dst, edge_weight, L0_gnn_W0, L0_gnn_as0, L0_gnn_ad0, L0_gnn_b0, L0_gnn_W1, L0_gnn_as1, L0_gnn_ad1, L0_gnn_b1, L0_gnn_W2, L0_gnn_as2, L0_gnn_ad2, L0_gnn_b2, L0_ffn_Wr, L0_ffn_W1s, L0_ffn_b1s, L0_ffn_W2s, L0_ffn_b2s, L0_ffn_W1p, L0_ffn_b1p, L0_ffn_W2p, L0_ffn_b2p, L1_gnn_W1, L1_gnn_b1, L1_gnn_W2, L1_gnn_b2, L1_ffn_sW1, L1_ffn_sb1, L1_ffn_sW2, L1_ffn_sb2, L1_ffn_sW3, L1_ffn_sb3, L1_ffn_eW1, L1_ffn_eb1, L1_ffn_eW2, L1_ffn_eb2, L1_ffn_eW3, L1_ffn_eb3, L1_ffn_gW, L1_ffn_gb):
    import jax
    import jax.numpy as jnp

    def _L0_gnn_ref(x, edge_index, W0, as0, ad0, b0, W1, as1, ad1, b1, W2, as2, ad2, b2):
        import jax, jax.numpy as jnp
        import numpy as np
        N_NODES = 6250
        N_EDGES = 100000
        IN_FEATS = 256
        HID = 64
        HEADS = 4
        OUT = 64

        def _gat_layer(x, src, dst, W, a_s, a_d, b, num_nodes):
            H, F = a_s.shape
            h = (x @ W).reshape(num_nodes, H, F)
            al_s = jnp.einsum('nhf,hf->nh', h, a_s)
            al_d = jnp.einsum('nhf,hf->nh', h, a_d)
            e = jax.nn.leaky_relu(al_s[src] + al_d[dst], 0.2)
            emax = jax.ops.segment_max(e, dst, num_segments=num_nodes)
            emax = jnp.where(jnp.isfinite(emax), emax, 0.0)
            ee = jnp.exp(e - emax[dst])
            denom = jax.ops.segment_sum(ee, dst, num_segments=num_nodes)
            alpha = ee / (denom[dst] + 1e-16)
            out = jax.ops.segment_sum(alpha[:, :, None] * h[src], dst, num_segments=num_nodes)
            return out.reshape(num_nodes, H * F) + b
        n = x.shape[0]
        loop = jnp.arange(n, dtype=edge_index.dtype)
        src = jnp.concatenate([edge_index[0], loop])
        dst = jnp.concatenate([edge_index[1], loop])
        h = _gat_layer(x, src, dst, W0, as0, ad0, b0, n)
        h = _gat_layer(h, src, dst, W1, as1, ad1, b1, n)
        h = _gat_layer(h, src, dst, W2, as2, ad2, b2, n)
        return h

    def _L0_ffn_ref(x, Wr, W1s, b1s, W2s, b2s, W1p, b1p, W2p, b2p):
        import jax, jax.numpy as jnp
        import numpy as np
        B, S, D, F, E, K = (8, 256, 256, 1024, 8, 2)
        gelu = lambda t: jax.nn.gelu(t, approximate=False)
        shared = gelu(x @ W1s + b1s) @ W2s + b2s
        rw = jax.nn.softmax(x @ Wr, axis=-1)
        topw, topi = jax.lax.top_k(rw, K)
        topw = topw / jnp.sum(topw, axis=-1, keepdims=True)
        mask = jnp.sum(jax.nn.one_hot(topi, E, dtype=topw.dtype) * topw[..., None], axis=-2)
        h = gelu(jnp.einsum('bsd,edf->bsef', x, W1p) + b1p)
        priv = jnp.einsum('bsef,efd->bsed', h, W2p) + b2p
        routed = jnp.einsum('bsed,bse->bsd', priv, mask)
        return shared + routed

    def _L1_gnn_ref(embeddings, edge_src, edge_dst, edge_val, W1, b1, W2, b2):
        import jax, jax.numpy as jnp
        import numpy as np
        N_NODES = 12500
        N_EDGES = 400000
        DIM = 256
        LEAKY_SLOPE = 0.2
        EPS = 1e-12
        ego_emb = embeddings @ W1.T + b1
        messages = edge_val[:, None] * embeddings[edge_src]
        neighbor_emb = jax.ops.segment_sum(messages, edge_dst, num_segments=embeddings.shape[0])
        interaction_emb = neighbor_emb * embeddings
        side_emb = (neighbor_emb + interaction_emb) @ W2.T + b2
        out = ego_emb + side_emb
        out = jnp.where(out >= 0, out, LEAKY_SLOPE * out)
        norm = jnp.sqrt(jnp.sum(out * out, axis=1, keepdims=True))
        return out / jnp.maximum(norm, EPS)

    def _L1_ffn_ref(x, sW1, sb1, sW2, sb2, sW3, sb3, eW1, eb1, eW2, eb2, eW3, eb3, gW, gb):
        import jax, jax.numpy as jnp
        import numpy as np
        B, A = (512, 8)
        IN, OUT = (256, 256)
        SH1, SH2 = (256, 128)
        EH1, EH2 = (128, 64)
        E, TOPK = (4, 2)

        def _shared_mlp(x, W1, b1, W2, b2, W3, b3):
            h = jax.nn.relu(x @ W1 + b1)
            h = jax.nn.relu(h @ W2 + b2)
            return h @ W3 + b3

        def _experts_mlp(x, eW1, eb1, eW2, eb2, eW3, eb3):
            h = jax.nn.relu(jnp.einsum('baf,efh->ebah', x, eW1) + eb1[:, None, None, :])
            h = jax.nn.relu(jnp.einsum('ebah,ehg->ebag', h, eW2) + eb2[:, None, None, :])
            o = jnp.einsum('ebag,ego->ebao', h, eW3) + eb3[:, None, None, :]
            return jnp.moveaxis(o, 0, -1)
        all_out = _experts_mlp(x, eW1, eb1, eW2, eb2, eW3, eb3)
        shared = _shared_mlp(x, sW1, sb1, sW2, sb2, sW3, sb3)
        gates = jax.nn.softmax(x @ gW + gb, axis=-1)
        topv, topi = jax.lax.top_k(gates, TOPK)
        topw = jax.nn.softmax(topv, axis=-1)
        sel = jnp.take_along_axis(all_out, topi[:, :, None, :], axis=-1)
        gated = jnp.sum(sel * topw[:, :, None, :], axis=-1)
        return shared + gated
    edge_index = jnp.stack([src, dst])
    x = x + _L0_gnn_ref(_layernorm(x, axis=-1), edge_index, L0_gnn_W0, L0_gnn_as0, L0_gnn_ad0, L0_gnn_b0, L0_gnn_W1, L0_gnn_as1, L0_gnn_ad1, L0_gnn_b1, L0_gnn_W2, L0_gnn_as2, L0_gnn_ad2, L0_gnn_b2)
    x = x + _L0_ffn_ref(_layernorm(x, axis=-1)[None], L0_ffn_Wr, L0_ffn_W1s, L0_ffn_b1s, L0_ffn_W2s, L0_ffn_b2s, L0_ffn_W1p, L0_ffn_b1p, L0_ffn_W2p, L0_ffn_b2p)[0]
    x = x + _L1_gnn_ref(_layernorm(x, axis=-1), src, dst, edge_weight, L1_gnn_W1, L1_gnn_b1, L1_gnn_W2, L1_gnn_b2)
    x = x + _L1_ffn_ref(_layernorm(x, axis=-1)[None], L1_ffn_sW1, L1_ffn_sb1, L1_ffn_sW2, L1_ffn_sb2, L1_ffn_sW3, L1_ffn_sb3, L1_ffn_eW1, L1_ffn_eb1, L1_ffn_eW2, L1_ffn_eb2, L1_ffn_eW3, L1_ffn_eb3, L1_ffn_gW, L1_ffn_gb)[0]
    return x

_drawn_inputs = setup_inputs


def setup_inputs(seed=0):
    import zlib

    import numpy as np

    out = dict(_drawn_inputs(seed))
    spreads = {'L0_gnn_b0': (0.0, 0.1),
     'L0_gnn_b1': (0.0, 0.1),
     'L0_gnn_b2': (0.0, 0.1),
     'L0_ffn_b1s': (0.0, 0.1),
     'L0_ffn_b2s': (0.0, 0.1),
     'L0_ffn_b1p': (0.0, 0.308),
     'L0_ffn_b2p': (0.0, 0.1),
     'L1_ffn_sb1': (0.0, 0.393),
     'L1_ffn_sb2': (0.0, 0.1),
     'L1_ffn_sb3': (0.0, 0.1),
     'L1_ffn_eb1': (0.0, 0.8),
     'L1_ffn_eb2': (0.0, 0.475),
     'L1_ffn_eb3': (0.0, 0.1),
     'L1_ffn_gb': (0.0, 0.386)}
    factors = {'edge_weight': 8.0,
     'L0_gnn_as0': 3.598,
     'L0_gnn_ad0': 30.295,
     'L0_gnn_as1': 8.0,
     'L0_gnn_ad1': 46.017,
     'L0_gnn_as2': 45.434,
     'L0_gnn_ad2': 64.0,
     'L1_gnn_b1': 64.0,
     'L1_gnn_W2': 6.323,
     'L1_gnn_b2': 64.0,
     'L1_gnn_W1': 3.613}
    for name, (base, spread) in spreads.items():
        noise = np.random.default_rng([zlib.crc32(name.encode()), seed]).standard_normal(out[name].shape)
        drawn = base * np.exp(spread * noise) if base else spread * noise
        out[name] = jnp.asarray(drawn.astype(out[name].dtype))
    for name, factor in factors.items():
        out[name] = (out[name] * factor).astype(out[name].dtype)
    return out
```

```python
from contextlib import ExitStack

import numpy as np

import concourse.bass as bass
from concourse import mybir

F32 = mybir.dt.float32
I32 = mybir.dt.int32
U32 = mybir.dt.uint32
BF16 = mybir.dt.bfloat16
ALU = mybir.AluOpType
ACT = mybir.ActivationFunctionType
AX = mybir.AxisListType

P = 128
D = 256
NN = 6250
NE = 100000
NT = -(-NN // P)
NP = NT * P
EC = -(-NE // P)
EP = EC * P
H = 4
HD = D // H
SLOPE = 0.2
LN_EPS = 1e-5
BIG = 1e30
FAR = 1 << 22

SELF0 = EC + 2
TROWS = 896
GMAX = 1024
assert EC + 4 * NT <= GMAX and SELF0 + NT <= TROWS
GC = GMAX // P

SLOTS = 8
RW = D + H
UT = 7
NB = NT // UT
CH = UT * P // 2
assert UT * NB == NT and CH <= 512

E0, F0 = 8, 1024
E1 = 4
FT0 = F0 // P


class Kit:

    def __init__(self, nc):
        self.nc, self.n = nc, 0

    def stage(self):
        return Stage(self)


class Stage(ExitStack):
    def __init__(self, kit):
        super().__init__()
        self.kit, self.sems = kit, []

    def sb(self, name, shape, dt=F32):
        self.kit.n += 1
        return self.enter_context(self.kit.nc.sbuf_tensor(f"{name}_{self.kit.n}", shape, dt))

    def ps(self, name, shape, dt=F32):
        self.kit.n += 1
        n = int(np.prod(shape[1:]))
        whole = self.enter_context(self.kit.nc.psum_tensor(f"{name}_{self.kit.n}", [P, -(-n // 512) * 512], dt))
        view = whole[0:shape[0], 0:n]
        if len(shape) == 2:
            return view
        names = "abcd"[:len(shape) - 1]
        return view.rearrange(f"p ({' '.join(names)}) -> p {' '.join(names)}", **dict(zip(names, shape[1:])))

    def sem(self, name):
        self.kit.n += 1
        if not self.sems:
            self.callback(self.zero_sems)
        s = self.kit.nc.alloc_semaphore(f"{name}_{self.kit.n}")
        self.sems.append(s)
        return s

    def pool_sem(self, name):
        self.kit.n += 1
        return self.kit.nc.alloc_semaphore(f"{name}_{self.kit.n}")

    def zero_sems(self):
        nc = self.kit.nc
        with nc.Block() as block:
            @block.gpsimd
            def _(pool):
                for s in self.sems:
                    pool.sem_clear(s)
        for s in self.sems:
            nc.release_semaphore(s)


class Chain:

    def __init__(self, eng, sem):
        self.eng, self.sem, self.n = eng, sem, 0

    def link(self, ins):
        self.n += 1
        ins.then_inc(self.sem, 1)
        self.eng.wait_ge(self.sem, self.n)


def ds(start, size=1):
    return bass.ds(start, size)



def constants(nc, kit, c):
    with kit.stage() as st:
        zeroed = st.sem("zeroed")
        made = st.sem("made")
        counted = st.sem("counted")
        iota_i = st.sb("iota_i", [P, P + 1], I32)
        with nc.Block() as block:
            @block.gpsimd
            def _(pool):
                nc.gpsimd.memset(c.ident[:, :], 0.0).then_inc(zeroed, 1)
                nc.gpsimd.memset(c.ones[:, :], 1.0).then_inc(made, 1)
                pool.wait_ge(zeroed, 1)
                nc.gpsimd.affine_select(out=c.ident[:, :], in_=c.ident[:, :], compare_op=ALU.not_equal,
                                        fill=1.0, base=0, pattern=[[-1, P]], channel_multiplier=1
                                        ).then_inc(made, 1)
                nc.gpsimd.iota(iota_i[:, :], pattern=[[1, P + 1]], base=0, channel_multiplier=0
                               ).then_inc(counted, 1)

            @block.vector
            def _(dve):
                dve.wait_ge(counted, 1)
                nc.vector.tensor_copy(c.iota[:, :], iota_i[:, :]).then_inc(made, 1)


def step_tables(nc, kit, c, a):
    with kit.stage() as st:
        sb, ps, sem = st.sb, st.ps, st.sem
        dst_i = sb("dst_i", [P, EC], I32)
        prev_i = sb("prev_i", [P, EC], I32)
        next_i = sb("next_i", [P, EC], I32)
        dst_f = sb("dst_f", [P, EC])
        oth_f = sb("oth_f", [P, EC])
        junk = sb("junk", [P, EC])
        below = sb("below", [P, NT + 1])
        bound_i = sb("bound_i", [P, NT + 1], I32)
        blk_i = sb("blk_i", [P, 2 * (NT + 1)], I32)
        blk_f = sb("blk_f", [P, 2 * (NT + 1)])
        cnt = sb("cnt", [P, NT])
        has = sb("has", [P, NT])
        cnt_i = sb("cnt_i", [P, NT], I32)
        gs = sb("gs", [P, NT + 1])
        off = sb("off", [P, NT])
        d_off = sb("d_off", [P, NT])
        gnum_i = sb("gnum_i", [P, GC], I32)
        gnum = sb("gnum", [P, GC])
        le = sb("le", [P, NT])
        tn = sb("tn", [P, GC])
        te = sb("te", [P, GC])
        slf = sb("slf", [P, GC])
        tmp = sb("tmp", [P, GC])
        tmp2 = sb("tmp2", [P, GC])
        self_i = sb("self_i", [NT, P], I32)
        zrow = sb("zrow", [P, P])
        zsp = sb("zsp", [P, EC * 8])
        rows_i = sb("rows_i", [P, GC, P], I32)
        rows_d = sb("rows_d", [P, GC, P], I32)
        rows_w = sb("rows_w", [P, GC, P])
        rows_s = sb("rows_s", [P, GC, P])
        rows_r = sb("rows_r", [P, GC, P])
        psum = ps("psum", [P, 3, 4, P])
        pcol = ps("pcol", [P, NT + 1])
        loaded = sem("loaded")
        dve_own = sem("dve_own")
        numbered = sem("numbered")
        table = sem("table")
        counted = sem("counted")
        summed = sem("summed")
        chosen = sem("chosen")
        fetched = st.pool_sem("fetched")
        laid = sem("laid")
        turned = sem("turned")
        kept = sem("kept")
        sel = sb("sel", [P, GC, NT])
        with nc.Block() as block:
            @block.sync
            def _(sp):
                sp.dma_start(dst_i[:, :], a["dst"][1:1 + EP].rearrange("(p j) -> p j", p=P)).then_inc(loaded, 16)
                sp.dma_start(prev_i[:, :], a["dst"][0:EP].rearrange("(p j) -> p j", p=P)).then_inc(loaded, 16)
                sp.dma_start(next_i[:, :], a["dst"][2:2 + EP].rearrange("(p j) -> p j", p=P)).then_inc(loaded, 16)
                e = a["dst"][1:1 + EP].rearrange("(t q) -> t q", q=P)
                sp.dma_start(c.t_dst[0:EC, :], e).then_inc(table, 16)
                sp.dma_start(c.t_src[0:EC, :], a["src"][0:EP].rearrange("(t q) -> t q", q=P)).then_inc(table, 16)
                sp.dma_start(c.t_w[0:EC, :], a["edge_weight"][0:EP].rearrange("(t q) -> t q", q=P)).then_inc(table, 16)
                sp.wait_ge(numbered, 4)
                far_i = c.far_i[0:TROWS - EC, :]
                sp.dma_start(c.t_dst[EC:SELF0, :], far_i[0:SELF0 - EC, :]).then_inc(table, 16)
                sp.dma_start(c.t_dst[SELF0 + NT:TROWS, :], far_i[0:TROWS - SELF0 - NT, :]).then_inc(table, 16)
                sp.dma_start(c.t_dst[SELF0:SELF0 + NT, :], self_i[:, :]).then_inc(table, 16)
                sp.dma_start(c.t_src[SELF0:SELF0 + NT, :], self_i[:, :]).then_inc(table, 16)
                zi = zrow[:, :].bitcast(I32)
                sp.dma_start(c.t_src[EC:SELF0, :], zi[0:SELF0 - EC, :]).then_inc(table, 16)
                sp.dma_start(c.t_src[SELF0 + NT:TROWS, :], zi[0:TROWS - SELF0 - NT, :]).then_inc(table, 16)
                sp.dma_start(c.t_w[EC:TROWS, :], zrow[0:TROWS - EC, :]).then_inc(table, 16)
                sp.dma_start(c.spread.rearrange("(p j) c -> p (j c)", p=P), zsp[:, :]).then_inc(table, 16)
                for r in (slice(EC, SELF0), slice(SELF0 + NT, TROWS)):
                    sp.dma_start(c.pay[r, :], zsp[0:r.stop - r.start, 0:H * P]).then_inc(table, 16)
                sp.wait_ge(table, 13 * 16)

            @block.gpsimd
            def _(pool):
                nc.gpsimd.iota(self_i[:, :], pattern=[[1, P]], base=0, channel_multiplier=P).then_inc(numbered, 1)
                nc.gpsimd.iota(gnum_i[:, :], pattern=[[P, GC]], base=0, channel_multiplier=1).then_inc(numbered, 1)
                nc.gpsimd.iota(c.far_i[:, :], pattern=[[0, P]], base=FAR, channel_multiplier=0).then_inc(numbered, 1)
                pool.wait_ge(chosen, 1)
                pool.wait_ge(table, 13 * 16)
                for k in range(GC):
                    at = bass.IndirectOffsetOnAxis(ap=c.te_i[:, k:k + 1], axis=0)
                    pool.indirect_dma_start(rows_i[:, k, :], None, c.t_src, at).then_inc(fetched, 16)
                    pool.indirect_dma_start(rows_d[:, k, :], None, c.t_dst, at).then_inc(fetched, 16)
                    pool.indirect_dma_start(rows_w[:, k, :], None, c.t_w, at).then_inc(fetched, 16)

            @block.vector
            def _(dve):
                ch = Chain(dve, dve_own)
                v = nc.vector
                v.memset(zsp[:, :], 0.0)
                v.memset(zrow[:, :], 0.0).then_inc(numbered, 1)
                v.memset(off[:, :], 0.0)
                dve.wait_ge(loaded, 48)
                ch.link(v.tensor_copy(dst_f[:, :], dst_i[:, :]))
                ch.link(v.tensor_copy(oth_f[:, :], prev_i[:, :]))
                ch.link(v.tensor_tensor(c.goes_on[:, :], dst_f[:, :], oth_f[:, :], ALU.is_equal))
                ch.link(v.tensor_scalar(c.pen_fwd[:, :], c.goes_on[:, :], 1.0, BIG, ALU.subtract, ALU.mult))
                ch.link(v.tensor_copy(oth_f[:, :], next_i[:, :]))
                ch.link(v.tensor_tensor(junk[:, :], dst_f[:, :], oth_f[:, :], ALU.is_equal))
                ch.link(v.tensor_scalar(c.pen_bwd[:, :], junk[:, :], 1.0, BIG, ALU.subtract, ALU.mult))
                ch.link(v.tensor_reduce(c.edge_pen[:, 0:1], c.goes_on[:, :], AX.X, ALU.min))
                ch.link(v.tensor_reduce(c.edge_pen[:, 1:2], c.pen_fwd[:, :], AX.X, ALU.min))
                ch.link(v.tensor_reduce(c.edge_pen[:, 2:3], c.pen_bwd[:, :], AX.X, ALU.min))
                for n in range(NT + 1):
                    ch.link(v.tensor_scalar(junk[:, :], dst_f[:, :], float(P * n), None, ALU.is_lt, ALU.add,
                                            accum_out=below[:, n:n + 1]))
                v.nop().then_inc(counted, 1)
                dve.wait_ge(summed, 1)
                ch.link(v.tensor_copy(bound_i[:, :], pcol[:, :]))
                ch.link(v.tensor_scalar(blk_i[:, 0:NT + 1], bound_i[:, :], 7, None, ALU.arith_shift_right))
                ch.link(v.tensor_copy(blk_f[:, 0:NT + 1], blk_i[:, 0:NT + 1]))
                ch.link(v.tensor_scalar(bound_i[:, :], bound_i[:, :], -1.0, None, ALU.add))
                ch.link(v.tensor_scalar(blk_i[:, NT + 1:], bound_i[:, :], 7, None, ALU.arith_shift_right))
                ch.link(v.tensor_copy(blk_f[:, NT + 1:], blk_i[:, NT + 1:]))
                ch.link(v.tensor_copy(below[:, :], pcol[:, :]))
                ch.link(v.tensor_tensor(has[:, :], below[:, 1:NT + 1], below[:, 0:NT], ALU.is_gt))
                ch.link(v.tensor_tensor(cnt[:, :], blk_f[:, NT + 2:], blk_f[:, 0:NT], ALU.subtract))
                ch.link(v.tensor_scalar(cnt[:, :], cnt[:, :], 1.0, None, ALU.add))
                ch.link(v.tensor_tensor(cnt[:, :], cnt[:, :], has[:, :], ALU.mult))
                ch.link(v.tensor_scalar(cnt[:, :], cnt[:, :], 2.0, None, ALU.add))
                ch.link(v.tensor_copy(cnt_i[:, :], cnt[:, :]))
                ch.link(v.tensor_scalar(cnt_i[:, :], cnt_i[:, :], 1, 1, ALU.arith_shift_right,
                                        ALU.logical_shift_left))
                ch.link(v.tensor_copy(cnt[:, :], cnt_i[:, :]))
                ch.link(v.memset(gs[:, :], 0.0))
                ch.link(v.tensor_tensor_scan(gs[:, 1:NT + 1], cnt[:, :], off[:, :], 0.0, ALU.add, ALU.add))
                ch.link(v.tensor_copy(c.first_step[:, :], gs[0:1, :]))
                ch.link(v.tensor_tensor(off[:, :], blk_f[:, 0:NT], gs[:, 0:NT], ALU.subtract))
                ch.link(v.tensor_scalar(off[:, :], off[:, :], 1.0, None, ALU.subtract))
                ch.link(v.tensor_copy(d_off[:, 0:1], off[:, 0:1]))
                ch.link(v.tensor_tensor(d_off[:, 1:NT], off[:, 1:NT], off[:, 0:NT - 1], ALU.subtract))
                dve.wait_ge(numbered, 3)
                ch.link(v.tensor_copy(gnum[:, :], gnum_i[:, :]))
                for k in range(GC):
                    g = gnum[:, k:k + 1]
                    ch.link(v.tensor_scalar(le[:, :], gs[:, 0:NT], g, None, ALU.is_equal, ALU.add,
                                            accum_out=slf[:, k:k + 1]))
                    ch.link(v.tensor_scalar(le[:, :], gs[:, 0:NT], g, None, ALU.is_le, ALU.add,
                                            accum_out=tn[:, k:k + 1]))
                    ch.link(v.tensor_tensor_reduce(le[:, :], le[:, :], d_off[:, :], 1.0, 0.0, ALU.mult,
                                                   ALU.add, te[:, k:k + 1]))
                ch.link(v.tensor_tensor(te[:, :], te[:, :], gnum[:, :], ALU.add))
                ch.link(v.tensor_scalar(te[:, :], te[:, :], float(EC), None, ALU.min))
                ch.link(v.tensor_scalar(tn[:, :], tn[:, :], 1.0, None, ALU.subtract))
                ch.link(v.tensor_scalar(tmp[:, :], tn[:, :], float(SELF0), None, ALU.add))
                ch.link(v.tensor_tensor(tmp[:, :], tmp[:, :], te[:, :], ALU.subtract))
                ch.link(v.tensor_tensor(tmp[:, :], tmp[:, :], slf[:, :], ALU.mult))
                ch.link(v.tensor_tensor(te[:, :], te[:, :], tmp[:, :], ALU.add))
                v.tensor_copy(c.te_i[:, :], te[:, :]).then_inc(chosen, 1)
                ch.link(v.tensor_scalar(tmp2[:, :], slf[:, :], -BIG, None, ALU.mult))
                ch.link(v.tensor_tensor(tmp2[:, :], tmp2[:, :], tn[:, :], ALU.add))
                for k in range(GC):
                    v.tensor_scalar(sel[:, k, :], c.iota[:, 0:NT], tmp2[:, k:k + 1], None, ALU.is_equal)
                ch.link(v.tensor_scalar(tmp[:, :], tn[:, :], float(P), None, ALU.mult))
                dve.wait_ge(fetched, 3 * GC * 16)
                ch.link(v.tensor_copy(rows_s[:, :, :], rows_i[:, :, :]))
                ch.link(v.tensor_copy(rows_r[:, :, :], rows_d[:, :, :]))
                for k in range(GC):
                    ins = v.tensor_scalar(rows_r[:, k, :], rows_r[:, k, :], tmp[:, k:k + 1], None, ALU.subtract)
                ch.link(ins)
                v.nop().then_inc(laid, 1)
                for b in range(GC // 4):
                    s = slice(b * 4 * P, (b + 1) * 4 * P)
                    dve.wait_ge(turned, b + 1)
                    v.tensor_copy(c.idx[:, s], psum[:, 0, :, :].rearrange("p a b -> p (a b)"))
                    v.tensor_copy(c.drel[:, s], psum[:, 1, :, :].rearrange("p a b -> p (a b)"))
                    v.tensor_copy(c.ew[:, s], psum[:, 2, :, :].rearrange("p a b -> p (a b)")).then_inc(kept, 1)

            @block.tensor
            def _(pe):
                pe.wait_ge(counted, 1)
                nc.tensor.matmul(pcol[:, :], c.ones[:, :], below[:, :], start=True, stop=True).then_inc(summed, 1)
                pe.wait_ge(laid, 1)
                for b in range(GC // 4):
                    if b:
                        pe.wait_ge(kept, b)
                    for m, rows in enumerate((rows_s, rows_r, rows_w)):
                        for k in range(4):
                            ins = nc.tensor.transpose(psum[:, m, k, :], rows[:, 4 * b + k, :], c.ident[:, :])
                    ins.then_inc(turned, 1)

        step_cols = st.sb("step_cols", [P, 2, GMAX])
        lt = st.sb("lt", [P, 8, P + 1], BF16)
        ones_h = st.sb("ones_h", [P, 1], BF16)
        iota_h = st.sb("iota_h", [P, P + 1], BF16)
        rel = st.sb("rel", [P, GMAX])
        tcol = st.sb("tcol", [P, P])
        at_f = st.sb("at_f", [P, 2, NT])
        pcnt = st.ps("pcnt", [P, 2, 16])
        pfirst = st.ps("pfirst", [P, 2, NT])
        pt = st.ps("pt", [P, P])
        setup = st.sem("setup")
        compared = st.sem("compared")
        colsum = st.sem("colsum")
        moved = st.sem("moved")
        own2 = st.sem("own2")
        tposed = st.sem("tposed")
        tkept = st.sem("tkept")
        found = st.sem("found")
        NGB = GMAX // 8
        with nc.Block() as block:
            @block.vector
            def _(dve):
                v = nc.vector
                ch = Chain(dve, own2)
                ch.link(v.memset(ones_h[:, :], 1.0))
                ch.link(v.tensor_copy(iota_h[:, :], c.iota[:, :]))
                with dve.Fori(0, NGB) as i:
                    dve.wait_ge(colsum, i)
                    for k in range(8):
                        ins = v.tensor_scalar(lt[:, k, :], iota_h[:, :], c.drel[:, ds(i * 8 + k)], None, ALU.is_gt)
                    ins.then_inc(compared, 1)
                    dve.wait_ge(colsum, i + 1)
                    v.tensor_copy(step_cols[:, :, ds(i * 8, 8)], pcnt[:, :, 0:8]).then_inc(moved, 1)
                n = 0
                for m in range(2):
                    for k in range(GC):
                        n += 1
                        dve.wait_ge(tposed, n)
                        v.tensor_copy(tcol[:, :], pt[:, :]).then_inc(tkept, 1)
                dve.wait_ge(found, 1)
                ch.link(v.tensor_copy(at_f[:, :, :], pfirst[:, :, :]))
                ch.link(v.tensor_tensor(at_f[:, 1, :], at_f[:, 1, :], at_f[:, 0, :], ALU.is_equal))
                ch.link(v.tensor_scalar(at_f[:, 1, :], at_f[:, 1, :], float(FAR), None, ALU.mult))
                ch.link(v.tensor_scalar(blk_f[:, 0:NT], blk_f[:, 0:NT], float(P), None, ALU.mult))
                ch.link(v.tensor_tensor(at_f[:, 0, :], at_f[:, 0, :], blk_f[:, 0:NT], ALU.add))
                ch.link(v.tensor_tensor(at_f[:, 0, :], at_f[:, 0, :], at_f[:, 1, :], ALU.add))
                ch.link(v.tensor_copy(c.first_edge[:, :], at_f[:, 0, :]))

            @block.tensor
            def _(pe):
                with pe.Fori(0, NGB) as i:
                    pe.wait_ge(compared, i + 1)
                    pe.wait_ge(moved, i)
                    for k in range(8):
                        nc.tensor.matmul(pcnt[:, 0, k:k + 1], lt[:, k, 0:P], ones_h[:, :], start=True, stop=True)
                        ins = nc.tensor.matmul(pcnt[:, 1, k:k + 1], lt[:, k, 1:P + 1], ones_h[:, :],
                                               start=True, stop=True)
                    ins.then_inc(colsum, 1)
                pe.wait_ge(moved, NGB)
                n = 0
                for m in range(2):
                    for k in range(GC):
                        if n:
                            pe.wait_ge(tkept, n)
                        nc.tensor.transpose(pt[:, :], step_cols[:, m, k * P:(k + 1) * P], c.ident[:, :]
                                            ).then_inc(tposed, 1)
                        n += 1
                        pe.wait_ge(tkept, n)
                        ins = nc.tensor.matmul(pfirst[:, m, :], tcol[:, :], sel[:, k, :],
                                               start=(k == 0), stop=(k == GC - 1))
                ins.then_inc(found, 1)



def norm_stage(nc, kit, c, a, X, add, outs, want):
    with kit.stage() as st:
        sb, ps, sem = st.sb, st.ps, st.sem
        xin = sb("xin", [P, UT, D])
        xs = sb("xs", [P, UT, D])
        stats = sb("stats", [P, UT, 6])
        mv = sb("mv", [P, UT, 2])
        std = sb("std", [P, UT])
        rstd = sb("rstd", [P, UT])
        pT = [ps(f"pT{k}", [P, 2, P]) for k in range(2)]
        loaded, own, varied, rooted = sem("loaded"), sem("own"), sem("varied"), sem("rooted")
        normed, used, turned, kept, stored = sem("normed"), sem("used"), sem("turned"), sem("kept"), sem("stored")
        read, passed = sem("read"), sem("passed")
        eps = sb("eps", [P, 1])
        if want == "project":
            xt = sb("xt", [P, 2, 2, P])
            hs = sb("hs", [P, UT, D + 2 * H])
            pH = [ps(f"pH{k}", [P, D + 2 * H]) for k in range(2)]
            prod, hkept, hstored = sem("prod"), sem("hkept"), sem("hstored")
        with nc.Block() as block:
            if add == "input":
                @block.sync
                def _(sp):
                    with sp.Fori(0, NB) as i:
                        sp.wait_ge(read, i)
                        sp.dma_start(xin[:, :, :], a["x"][ds(i * UT * P, UT * P), :].rearrange(
                            "(k p) d -> p k d", p=P)).then_inc(loaded, 16)
                        if want == "project":
                            sp.wait_ge(hkept, i * UT + UT)
                            r = ds(i * UT * P, UT * P)
                            sp.dma_start(outs["rows"][r, :].rearrange("(k p) d -> p k d", p=P),
                                         hs[:, :, 0:D]).then_inc(hstored, 16)
                            sp.dma_start(outs["logits"][r, :].rearrange("(k p) d -> p k d", p=P),
                                         hs[:, :, D:D + H]).then_inc(hstored, 16)
                    if want == "project":
                        sp.wait_ge(hstored, 32 * NB)
            elif want == "rows":
                @block.sync
                def _(sp):
                    with sp.Fori(0, NB) as i:
                        sp.wait_ge(normed, (i + 1) * UT)
                        sp.dma_start(outs["rows"][ds(i * UT * P, UT * P), :].rearrange("(k p) d -> p k d", p=P),
                                     outs["sbuf"][:, ds(i * UT, UT), :]).then_inc(stored, 16)
                    sp.wait_ge(stored, 16 * NB)

            @block.vector
            def _(dve):
                v = nc.vector
                v.memset(eps[:, :], LN_EPS).then_inc(own, 1)
                dve.wait_ge(own, 1)
                L = 2 if add == "none" or want == "project" else 3
                with dve.Fori(0, NB) as i:
                    o = i * L + 1
                    tiles = ds(i * UT, UT)
                    if want == "project":
                        src = xin
                        dve.wait_ge(loaded, (i + 1) * 16)
                    else:
                        if add == "input":
                            dve.wait_ge(loaded, (i + 1) * 16)
                            v.tensor_tensor(X[:, tiles, :], X[:, tiles, :], xin[:, :, :], ALU.add).then_inc(own, 1)
                            dve.wait_ge(own, o + 1)
                            o = o + 1
                        elif add == "scaled":
                            for k in range(UT):
                                t = ds(i * UT + k)
                                ins = v.scalar_tensor_tensor(out=X[:, t, :], in0=outs["adds"][:, t, :],
                                                             scalar=outs["scale"][:, t], in1=X[:, t, :],
                                                             op0=ALU.mult, op1=ALU.add)
                            ins.then_inc(own, 1)
                            dve.wait_ge(own, o + 1)
                            o = o + 1
                    def tile(k):
                        return xin[:, k, :] if want == "project" else X[:, ds(i * UT + k), :]
                    dve.sem_inc(passed, 1)
                    for k in range(UT):
                        ins = v.bn_stats(stats[:, k, :], tile(k))
                    ins.then_inc(own, 1)
                    dve.wait_ge(own, o + 1)
                    dve.sem_inc(passed, 1)
                    for k in range(UT):
                        ins = v.bn_aggr(mv[:, k, :], stats[:, k, :])
                    ins.then_inc(varied, 1)
                    dve.wait_ge(rooted, i + 1)
                    v.reciprocal(rstd[:, :], std[:, :]).then_inc(own, 1)
                    dve.wait_ge(own, o + 2)
                    if want != "rows":
                        dve.wait_ge(used, i * UT)
                    for k in range(UT):
                        out = outs["sbuf"][:, ds(i * UT + k), :] if want == "rows" else xs[:, k, :]
                        ins = v.tensor_scalar(out, tile(k), mv[:, k, 0:1], rstd[:, k:k + 1],
                                              ALU.subtract, ALU.mult)
                        ins.then_inc(normed, 1)
                    dve.wait_ge(normed, (i + 1) * UT)
                    if add == "input":
                        dve.sem_inc(read, 1)
                    if want == "project":
                        for k in range(UT):
                            dve.wait_ge(prod, i * UT + k + 1)
                            if k == 0:
                                dve.wait_ge(hstored, i * 32)
                            v.tensor_copy(c.logit[:, ds(i * UT + k), :], pH[k % 2][:, D:D + 2 * H])
                            v.tensor_copy(hs[:, k, :], pH[k % 2][:, :]).then_inc(hkept, 1)

            @block.scalar
            def _(act):
                with act.Fori(0, NB) as i:
                    act.wait_ge(varied, i + 1)
                    nc.scalar.activation(std[:, :], mv[:, :, 1], ACT.Sqrt, bias=eps[:, :]).then_inc(rooted, 1)
                    if want != "rows":
                        for k in range(UT):
                            act.wait_ge(turned, i * UT + k + 1)
                            if want == "project":
                                if k >= 2:
                                    act.wait_ge(prod, i * UT + k - 1)
                                else:
                                    act.wait_ge(prod, i * UT)
                                to = xt[:, k % 2, :, :]
                            else:
                                to = outs["sbuf"][:, :, ds((i * UT + k) * P, P)]
                            nc.scalar.activation(to, pT[k % 2][:, :, :], ACT.Copy).then_inc(kept, 1)

            if want != "rows":
                @block.tensor
                def _(pe):
                    with pe.Fori(0, NB) as i:
                        for k in range(UT):
                            pe.wait_ge(normed, i * UT + k + 1)
                            if k >= 2:
                                pe.wait_ge(kept, i * UT + k - 1)
                            else:
                                pe.wait_ge(kept, i * UT)
                            for h in range(2):
                                ins = nc.tensor.transpose(pT[k % 2][:, h, :], xs[:, k, h * P:(h + 1) * P],
                                                          c.ident[:, :])
                            ins.then_inc(turned, 1)
                            if want == "project":
                                pe.wait_ge(kept, i * UT + k + 1)
                                if k >= 2:
                                    pe.wait_ge(hkept, i * UT + k - 1)
                                else:
                                    pe.wait_ge(hkept, i * UT)
                                for h in range(2):
                                    ins = nc.tensor.matmul(pH[k % 2][:, :], xt[:, k % 2, h, :], c.wp[:, h, :],
                                                           start=(h == 0), stop=(h == 1))
                                ins.then_inc(prod, 1)
                        pe.wait_ge(turned, i * UT + UT)
                        pe.sem_inc(used, UT)


def attention_weights(nc, kit, c, a, layer):
    with kit.stage() as st:
        sb, ps, sem = st.sb, st.ps, st.sem
        avec = sb("avec", [P, 2, 2 * H])
        wt = sb("wt", [P, 2, D])
        pw = ps("pw", [P, 2, 2, P])
        pa = ps("pa", [P, 2, 2 * H])
        clear, loaded, turned, kept, prod = sem("clear"), sem("loaded"), sem("turned"), sem("kept"), sem("prod")
        done = sem("done")
        with nc.Block() as block:
            @block.sync
            def _(sp):
                sp.dma_start(c.wp[:, :, 0:D], a[f"L0_gnn_W{layer}"].rearrange("(k p) n -> p k n", p=P)
                             ).then_inc(loaded, 16)
                sp.dma_start(c.gbias[:, :], a[f"L0_gnn_b{layer}"].rearrange("(a n) -> a n", a=1)
                             .to_broadcast([P, D])).then_inc(loaded, 16)
                sp.wait_ge(clear, 1)
                for j, s in enumerate((a[f"L0_gnn_as{layer}"], a[f"L0_gnn_ad{layer}"])):
                    for h in range(H):
                        r = h * HD % P
                        sp.dma_start(avec[r:r + HD, h * HD // P, j * H + h:j * H + h + 1],
                                     s[h, :].rearrange("(n a) -> n a", a=1)).then_inc(loaded, 16)

            @block.vector
            def _(dve):
                nc.vector.memset(avec[:, :, :], 0.0).then_inc(clear, 1)
                dve.wait_ge(turned, 1)
                nc.vector.tensor_copy(wt[:, :, :].rearrange("p a (b n) -> p a b n", b=2), pw[:, :, :, :]).then_inc(kept, 1)
                dve.wait_ge(prod, 1)
                nc.vector.tensor_copy(c.wp[:, :, D:D + 2 * H], pa[:, :, :]).then_inc(done, 1)

            @block.tensor
            def _(pe):
                pe.wait_ge(loaded, (2 + 2 * H) * 16)
                for j in range(2):
                    for k in range(2):
                        ins = nc.tensor.transpose(pw[:, j, k, :], c.wp[:, k, j * P:(j + 1) * P], c.ident[:, :])
                ins.then_inc(turned, 1)
                pe.wait_ge(kept, 1)
                for k in range(2):
                    for j in range(2):
                        ins = nc.tensor.matmul(pa[:, k, :], wt[:, j, k * P:(k + 1) * P], avec[:, j, :],
                                               start=(j == 0), stop=(j == 1))
                ins.then_inc(prod, 1)



def edge_softmax(nc, kit, c, a, layer):
    with kit.stage() as st:
        sb, ps, sem = st.sb, st.ps, st.sem
        src_i = sb("src_i", [P, EC], I32)
        e = sb("e", [P, EC, H])
        own8 = sb("own8", [P, EC, 2 * H])
        node = sb("node", [P, EC, 2 * H])
        mx = sb("mx", [P, EC, H])
        ns = sb("ns", [P, NT, 2 * H])
        nmax = sb("nmax", [P, NT, H])
        t4 = sb("t4", [P, NT, H])
        ends = sb("ends", [P, 2 * H + 1])
        rows = sb("rows", [2 * H, 2, P + 2])
        carry = sb("carry", [P, 2 * H])
        prow = ps("prow", [2 * H, P])
        pflag = ps("pflag", [2 * H, P])
        pcar = ps("pcar", [P, 2 * H])
        pturn = [ps(f"pturn{k}", [P, 4, P]) for k in range(2)]
        prows = sb("prows", [P, GC, H * P])
        idx8 = sb("idx8", [P, 2, 8], I32)
        gat, own, ld, self_done, spread_done = st.pool_sem("gat"), sem("own"), sem("ld"), sem("selfd"), st.pool_sem("spread")
        re_read, ended, rowed, rkept, carried = sem("reread"), sem("ended"), sem("rowed"), sem("rkept"), sem("carried")
        exped, wrote, maxed, mgot, wexp = sem("exped"), sem("wrote"), sem("maxed"), st.pool_sem("mgot"), sem("wexp")
        fetched, turned, kept = st.pool_sem("fetched"), sem("turned"), sem("kept")
        idx_put, issued, prefill = sem("idxput"), sem("issued"), sem("prefill")
        raw1, raw2, wrote_max = sem("raw1"), sem("raw2"), sem("wrote_max")
        NGB = -(-EC // 8)
        GB2 = NGB // 2
        with nc.Block() as block:
            @block.sync
            def _(sp):
                sp.dma_start(src_i[:, :], a["src"][0:EP].rearrange("(p j) -> p j", p=P)).then_inc(ld, 16)
                sp.wait_ge(spread_done, 16 * NT)
                sp.dma_start(own8[:, :, :], c.spread.rearrange("(p j) c -> p j c", p=P)).then_inc(re_read, 16)
                sp.wait_ge(maxed, 1)
                sp.dma_start(c.emax.rearrange("(p j) c -> p j c", p=P), mx[:, :, :]).then_inc(wrote_max, 16)
                sp.wait_ge(exped, 1)
                sp.dma_start(c.pay[0:EC, :].rearrange("t (q h) -> (t q) h", h=H).rearrange(
                    "(p j) h -> p j h", p=P), e[:, :, :]).then_inc(wrote, 16)
                sp.wait_ge(wexp, 1)
                for t in range(NT):
                    sp.dma_start(c.pay[SELF0 + t, :].rearrange("(q h) -> q h", h=H), nmax[:, t, :]
                                 ).then_inc(wrote, 16)

            @block.gpsimd
            def _(pool):
                pool.wait_ge(self_done, 1)
                for t in range(NT):
                    pool.indirect_dma_start(c.spread, bass.IndirectOffsetOnAxis(ap=c.first_edge[:, t:t + 1], axis=0),
                                            ns[:, t, :], None, bounds_check=EP - 1, oob_is_err=False
                                            ).then_inc(spread_done, 16)
                pool.wait_ge(ld, 16)
                for j in range(EC):
                    pool.indirect_dma_start(e[:, j, :], None, c.src_logit,
                                            bass.IndirectOffsetOnAxis(ap=src_i[:, j:j + 1], axis=0)
                                            ).then_inc(gat, 16)
                pool.wait_ge(wrote_max, 16)
                pool.wait_ge(prefill, 1)
                for t in range(NT):
                    pool.indirect_dma_start(nmax[:, t, :], None, c.emax,
                                            bass.IndirectOffsetOnAxis(ap=c.first_edge[:, t:t + 1], axis=0),
                                            bounds_check=EP - 1, oob_is_err=False).then_inc(mgot, 16)
                pool.wait_ge(wrote, 16 * (1 + NT))
                for k in range(GC):
                    pool.indirect_dma_start(prows[:, k, :], None, c.pay,
                                            bass.IndirectOffsetOnAxis(ap=c.te_i[:, k:k + 1], axis=0)
                                            ).then_inc(fetched, 16)

            @block.vector
            def _(dve):
                v = nc.vector
                ch = Chain(dve, own)
                ch.link(v.tensor_copy(ns[:, :, 0:H], c.logit[:, :, H:2 * H]))
                ch.link(v.tensor_tensor(t4[:, :, :], c.logit[:, :, 0:H], c.logit[:, :, H:2 * H], ALU.add))
                v.scalar_tensor_tensor(out=ns[:, :, H:2 * H], in0=t4[:, :, :], scalar=SLOPE, in1=t4[:, :, :],
                                       op0=ALU.mult, op1=ALU.max).then_inc(self_done, 1)
                dve.wait_ge(self_done, 1)
                v.tensor_copy(nmax[:, :, :], ns[:, :, H:2 * H]).then_inc(prefill, 1)

                def scan(out, flags, vals, ncol, op0, op1, init, back, flag_end, n):
                    s = slice(None, None, -1) if back else slice(None)
                    last = 0 if back else EC - 1
                    for h in range(ncol):
                        ins = v.tensor_tensor_scan(out[:, s, h], flags[:, s], vals[:, s, h], init, op0, op1)
                    ch.link(ins)
                    ch.link(v.tensor_copy(ends[:, 0:ncol], out[:, last, 0:ncol]))
                    ch.link(v.tensor_copy(carry[:, 0:ncol], flag_end.to_broadcast([P, ncol])))
                    v.nop().then_inc(ended, 1)
                    dve.wait_ge(rowed, n)
                    ch.link(v.memset(rows[:, 1, :], init))
                    ch.link(v.tensor_copy(rows[0:ncol, 0, 0:P], pflag[0:ncol, :]))
                    row_out = rows[0:ncol, 1, P - 1::-1] if back else rows[0:ncol, 1, 1:P + 1]
                    row_s = slice(None, None, -1) if back else slice(None)
                    if back:
                        ch.link(v.tensor_tensor_scan(rows[0:ncol, 1, P - 2::-1], rows[0:ncol, 0, P - 1:0:-1],
                                                     prow[0:ncol, P - 1:0:-1], init, op0, op1))
                    else:
                        ch.link(v.tensor_tensor_scan(rows[0:ncol, 1, 1:P], rows[0:ncol, 0, 0:P - 1],
                                                     prow[0:ncol, 0:P - 1], init, op0, op1))
                    v.nop().then_inc(rkept, 1)
                    dve.wait_ge(carried, n)
                    ch.link(v.tensor_copy(carry[:, 0:ncol], pcar[:, 0:ncol]))
                    for h in range(ncol):
                        ins = v.tensor_tensor_scan(out[:, s, h], flags[:, s], vals[:, s, h],
                                                   carry[:, h:h + 1], op0, op1)
                    ch.link(ins)

                dve.wait_ge(re_read, 16)
                ch.link(v.tensor_scalar(mx[:, :, 0], c.goes_on[:, :], -1.0, 1.0, ALU.mult, ALU.add))
                ch.link(v.tensor_tensor(own8[:, :, :], own8[:, :, :],
                                        mx[:, :, 0:1].to_broadcast([P, EC, 2 * H]), ALU.mult))
                scan(node, c.goes_on, own8, 2 * H, ALU.mult, ALU.add, 0.0, False, c.edge_pen[:, 0:1], 1)
                dve.wait_ge(gat, 16 * EC)
                ch.link(v.tensor_tensor(e[:, :, :], e[:, :, :], node[:, :, 0:H], ALU.add))
                ch.link(v.scalar_tensor_tensor(out=e[:, :, :], in0=e[:, :, :], scalar=SLOPE, in1=e[:, :, :],
                                               op0=ALU.mult, op1=ALU.max))
                scan(own8, c.pen_fwd, e, H, ALU.add, ALU.max, -BIG, False, c.edge_pen[:, 1:2], 2)
                scan(mx, c.pen_bwd, own8, H, ALU.add, ALU.max, -BIG, True, c.edge_pen[:, 2:3], 3)
                ch.link(v.tensor_tensor(mx[:, :, :], mx[:, :, :], node[:, :, H:2 * H], ALU.max))
                v.nop().then_inc(maxed, 1)
                v.tensor_tensor(e[:, :, :], e[:, :, :], mx[:, :, :], ALU.subtract).then_inc(raw1, 1)
                dve.wait_ge(mgot, 16 * NT)
                v.tensor_tensor(nmax[:, :, :], ns[:, :, H:2 * H], nmax[:, :, :], ALU.subtract).then_inc(raw2, 1)
                for k in range(GC):
                    dve.wait_ge(turned, k + 1)
                    v.tensor_copy(c.paid[:, :, k * P:(k + 1) * P], pturn[k % 2][:, :, :]).then_inc(kept, 1)

            @block.scalar
            def _(act):
                act.wait_ge(raw1, 1)
                nc.scalar.activation(e[:, :, :], e[:, :, :], ACT.Exp).then_inc(exped, 1)
                act.wait_ge(raw2, 1)
                nc.scalar.activation(nmax[:, :, :], nmax[:, :, :], ACT.Exp).then_inc(wexp, 1)

            @block.tensor
            def _(pe):
                for n, ncol in ((1, 2 * H), (2, H), (3, H)):
                    pe.wait_ge(ended, n)
                    nc.tensor.transpose(prow[0:ncol, :], ends[:, 0:ncol], c.ident[:, :])
                    nc.tensor.transpose(pflag[0:ncol, :], carry[:, 0:ncol], c.ident[:, :]).then_inc(rowed, 1)
                    pe.wait_ge(rkept, n)
                    nc.tensor.transpose(pcar[:, 0:ncol], rows[0:ncol, 1, 0:P], c.ident[0:ncol, 0:ncol]
                                        ).then_inc(carried, 1)
                pe.wait_ge(fetched, 16 * GC)
                for k in range(GC):
                    if k >= 2:
                        pe.wait_ge(kept, k - 1)
                    for h in range(H):
                        ins = nc.tensor.transpose(pturn[k % 2][:, h, :], prows[:, k, h::H], c.ident[:, :])
                    ins.then_inc(turned, 1)


def edge_pass(nc, kit, c, a, table, kind, outs):
    att = kind != "mix"
    with kit.stage() as st:
        sb, ps, sem = st.sb, st.ps, st.sem
        rows = sb("rows", [P, SLOTS, RW])
        hot = [sb(f"hot{b}", [P, P]) for b in range(2)]
        ix = sb("ix", [P, SLOTS], I32)
        den = sb("den", [P, H])
        rden = sb("rden", [P, H])
        NF = 4 if kind == "mix" else 2
        fin = sb("fin", [P, NF * P])
        xt = sb("xt", [P, NF, P])
        hs = sb("hs", [P, D + 2 * H])
        zero = sb("zero", [P, P])
        sq = sb("sq", [P, 1])
        acc = ps("acc", [P, RW])
        pT = ps("pT", [P, NF, P])
        pH = ps("pH", [P, D + 2 * H])
        total_i = st.sb("total_i", [1, 1], I32)
        landed = [st.pool_sem(f"landed{k}") for k in range(SLOTS)]
        passed = sem("passed")
        index_put = sem("index_put")
        paid_put = sem("paid_put")
        freed = sem("freed")
        hot_made, weighed = sem("hot_made"), sem("weighed")
        cleared, summed, own = sem("cleared"), sem("summed"), sem("own")
        fin_made, turned, kept, prod, hkept, stored = (sem(x) for x in
                                                       ("fin", "turned", "kept", "prod", "hkept", "stored"))
        with nc.Block() as block:
            def bodies(eng):
                total = eng.value_load(c.first_step[0:1, NT:NT + 1], min_val=2 * NT, max_val=GMAX - 2 * SLOTS)
                return eng.snap((total + (SLOTS - 1)) >> 3)

            @block.gpsimd
            def _(pool):
                nb = bodies(pool)
                with pool.Fori(0, nb) as i:
                    for k in range(SLOTS):
                        pool.wait_ge(freed, i * SLOTS + (k + 1))
                        pool.wait_ge(index_put, i * SLOTS + k + SLOTS)
                        pool.sem_inc(passed, 1)
                        pool.indirect_dma_start(rows[:, k, 0:D], None, table,
                                                bass.IndirectOffsetOnAxis(ap=ix[:, k:k + 1], axis=0)
                                                ).then_inc(landed[k], 16)

            @block.scalar
            def _(act):
                nb = bodies(act)
                for k in range(SLOTS):
                    nc.scalar.activation(ix[:, k:k + 1], c.idx[:, k:k + 1], ACT.Copy).then_inc(index_put, 1)
                with act.Fori(0, nb) as i:
                    for k in range(SLOTS):
                        act.wait_ge(landed[k], i * 16 + 16)
                        if att:
                            nc.scalar.activation(rows[:, k, D:RW], c.paid[:, :, ds(i * SLOTS + k)].rearrange(
                                "p h o -> p (h o)"), ACT.Copy).then_inc(paid_put, 1)
                        nc.scalar.activation(ix[:, k:k + 1], c.idx[:, ds(i * SLOTS + (k + SLOTS))],
                                             ACT.Copy).then_inc(index_put, 1)

            @block.vector
            def _(dve):
                v = nc.vector
                v.memset(zero[:, :], 0.0).then_inc(cleared, 1)
                K = 3 if att else 5
                with dve.Fori(0, NT) as n:
                    g0 = dve.value_load(c.first_step[0:1, ds(n)], min_val=0, max_val=GMAX - SLOTS)
                    g1 = dve.value_load(c.first_step[0:1, ds(n + 1)], min_val=0, max_val=GMAX - SLOTS)
                    with dve.Fori(g0, g1, 2) as g:
                        for b in range(2):
                            dve.wait_ge(freed, g + (b + SLOTS - 2 + 1))
                            if att:
                                v.tensor_scalar(hot[b][:, :], c.iota[:, 0:P], c.drel[:, ds(g + b)], None,
                                                ALU.is_equal).then_inc(hot_made, 1)
                                dve.wait_ge(index_put, g + (b + 1 + SLOTS))
                                row = rows[:, ds((g + b) & (SLOTS - 1)), 0:D].rearrange("p o (h f) -> p (o h) f", h=H)
                                v.tensor_tensor(row, row, c.paid[:, :, ds(g + b)].to_broadcast([P, H, HD]),
                                                ALU.mult).then_inc(weighed, 1)
                            else:
                                v.tensor_scalar(hot[b][:, :], c.iota[:, 0:P], c.drel[:, ds(g + b)],
                                                c.ew[:, ds(g + b)], ALU.is_equal, ALU.mult).then_inc(hot_made, 1)
                    dve.wait_ge(summed, n + 1)
                    if att:
                        v.tensor_scalar(den[:, :], acc[:, D:RW], 1e-16, None, ALU.add).then_inc(own, 1)
                        dve.wait_ge(own, n * K + 1)
                        v.reciprocal(rden[:, :], den[:, :]).then_inc(own, 1)
                        dve.wait_ge(own, n * K + 2)
                        v.tensor_tensor(fin[:, :].rearrange("p (h f) -> p h f", h=H),
                                        acc[:, 0:D].rearrange("p (h f) -> p h f", h=H),
                                        rden[:, :].rearrange("p (h o) -> p h o", o=1).to_broadcast([P, H, HD]),
                                        ALU.mult).then_inc(own, 1)
                        dve.wait_ge(own, n * K + 3)
                        if kind == "last":
                            v.tensor_tensor(outs["sbuf"][:, ds(n), :].rearrange("p o d -> p (o d)"),
                                            fin[:, :], c.gbias[:, :], ALU.add).then_inc(fin_made, 1)
                        else:
                            v.tensor_tensor(fin[:, :], fin[:, :], c.gbias[:, :], ALU.add).then_inc(fin_made, 1)
                            dve.wait_ge(turned, n + 1)
                            v.tensor_copy(xt[:, :, :], pT[:, :, :]).then_inc(kept, 1)
                            dve.wait_ge(prod, n + 1)
                            dve.wait_ge(stored, n * 32)
                            v.tensor_copy(c.logit[:, ds(n), :].rearrange("p o d -> p (o d)"), pH[:, D:D + 2 * H])
                            v.tensor_copy(hs[:, :], pH[:, :]).then_inc(hkept, 1)
                    else:
                        emb = outs["sbuf"][:, ds(n), :].rearrange("p o d -> p (o d)")
                        v.tensor_copy(fin[:, 0:D], emb).then_inc(own, 1)
                        v.tensor_tensor(fin[:, D:2 * D], acc[:, 0:D], emb, ALU.mult).then_inc(own, 1)
                        dve.wait_ge(own, n * K + 2)
                        v.tensor_tensor(fin[:, D:2 * D], fin[:, D:2 * D], acc[:, 0:D], ALU.add).then_inc(fin_made, 1)
                        dve.wait_ge(turned, n + 1)
                        v.tensor_copy(xt[:, :, :], pT[:, :, :]).then_inc(kept, 1)
                        dve.wait_ge(prod, n + 1)
                        v.tensor_tensor(hs[:, 0:D], pH[:, 0:D], c.gbias[:, :], ALU.add).then_inc(own, 1)
                        dve.wait_ge(own, n * K + 3)
                        v.scalar_tensor_tensor(out=fin[:, 0:D], in0=hs[:, 0:D], scalar=SLOPE, in1=hs[:, 0:D],
                                               op0=ALU.mult, op1=ALU.max).then_inc(own, 1)
                        dve.wait_ge(own, n * K + 4)
                        dve.sem_inc(passed, 1)
                        v.tensor_copy(emb, fin[:, 0:D])
                        v.tensor_tensor_reduce(fin[:, D:2 * D], fin[:, 0:D], fin[:, 0:D], 1.0, 0.0, ALU.mult,
                                               ALU.add, sq[:, :]).then_inc(own, 1)
                        dve.wait_ge(own, n * K + 5)
                        dve.sem_inc(passed, 1)
                        v.tensor_copy(outs["sumsq"][:, ds(n)], sq[:, :]).then_inc(hkept, 1)
                        dve.wait_ge(hkept, n + 1)

            @block.tensor
            def _(pe):
                pe.sem_inc(freed, SLOTS)
                pe.wait_ge(cleared, 1)
                with pe.Fori(0, NT) as n:
                    g0 = pe.value_load(c.first_step[0:1, ds(n)], min_val=0, max_val=GMAX - SLOTS)
                    g1 = pe.value_load(c.first_step[0:1, ds(n + 1)], min_val=0, max_val=GMAX - SLOTS)
                    pe.wait_ge(fin_made, n)
                    A = acc[:, :] if att else acc[:, 0:D]
                    W = RW if att else D
                    nc.tensor.matmul(A, zero[0:1, :], c.zero_row[0:1, 0:W], start=True, stop=False,
                                     skip_group_check=True)
                    with pe.Fori(g0, g1, 2) as g:
                        for b in range(2):
                            if att:
                                pe.wait_ge(paid_put, g + (b + 1))
                                pe.wait_ge(weighed, g + (b + 1))
                            else:
                                pe.wait_ge(index_put, g + (b + 1 + SLOTS))
                                pe.wait_ge(hot_made, g + (b + 1))
                            row = rows[:, ds((g + b) & (SLOTS - 1)), 0:W].rearrange("p o d -> p (o d)")
                            nc.tensor.matmul(A, hot[b][:, :], row, start=False, stop=False,
                                             skip_group_check=True).then_inc(freed, 1)
                    nc.tensor.matmul(A, zero[0:1, :], c.zero_row[0:1, 0:W], start=False, stop=True,
                                     skip_group_check=True).then_inc(summed, 1)
                    if kind != "last":
                        pe.wait_ge(fin_made, n + 1)
                        for f in range(NF):
                            ins = nc.tensor.transpose(pT[:, f, :], fin[:, f * P:(f + 1) * P], c.ident[:, :])
                        ins.then_inc(turned, 1)
                        pe.wait_ge(kept, n + 1)
                        for f in range(NF):
                            if kind == "mix":
                                ins = nc.tensor.matmul(pH[:, 0:D], xt[:, f, :], outs["w"][:, f, :],
                                                       start=(f == 0), stop=(f == NF - 1))
                            else:
                                ins = nc.tensor.matmul(pH[:, :], xt[:, f, :], c.wp[:, f, :],
                                                       start=(f == 0), stop=(f == NF - 1))
                        ins.then_inc(prod, 1)
                        pe.wait_ge(hkept, n + 1)

            if kind == "project":
                @block.sync
                def _(sp):
                    with sp.Fori(0, NT) as n:
                        sp.wait_ge(hkept, n + 1)
                        sp.dma_start(outs["rows"][ds(n * P, P), :], hs[:, 0:D]).then_inc(stored, 16)
                        sp.dma_start(outs["logits"][ds(n * P, P), :], hs[:, D:D + H]).then_inc(stored, 16)
                    sp.wait_ge(stored, NT * 32)



def router(nc, kit, c, xT, wr, E, gbias, gate):
    with kit.stage() as st:
        sb, ps, sem = st.sb, st.ps, st.sem
        lt = sb("lt", [E, UT * P])
        logits = sb("logits", [P, NT, 8])
        best = sb("best", [P, NT, 8])
        at = sb("at", [P, NT, 8], U32)
        at_f = sb("at_f", [P, NT, 2])
        ex = sb("ex", [P, NT, 8])
        z = sb("z", [P, NT, 1])
        w1 = sb("w1", [P, NT, 1])
        w2 = sb("w2", [P, NT, 1])
        dd = sb("dd", [P, NT, 1])
        hit = sb("hit", [P, NT, 8])
        pL = [ps(f"pL{k}", [E, CH]) for k in range(2)]
        pG = ps("pG", [P, UT, E])
        prod, kept, turned, put, own = sem("prod"), sem("kept"), sem("turned"), sem("put"), sem("own")
        asked, given, passed = sem("asked"), sem("given"), sem("passed")
        with nc.Block() as block:
            @block.tensor
            def _(pe):
                with pe.Fori(0, NB) as i:
                    pe.wait_ge(kept, i)
                    for m in range(2):
                        for k in range(2):
                            ins = nc.tensor.matmul(pL[m][:, :], wr[:, k, :], xT[:, k, ds(i * UT * P + m * CH, CH)],
                                                   start=(k == 0), stop=(k == 1))
                    ins.then_inc(prod, 1)
                    pe.wait_ge(kept, i + 1)
                    pe.wait_ge(put, i)
                    pe.sem_inc(passed, 1)
                    for k in range(UT):
                        ins = nc.tensor.transpose(pG[:, k, :], lt[:, k * P:(k + 1) * P], c.ident[0:E, 0:E])
                    ins.then_inc(turned, 1)

            @block.vector
            def _(dve):
                v = nc.vector
                v.memset(logits[:, :, :], -BIG).then_inc(own, 1)
                dve.wait_ge(own, 1)
                with dve.Fori(0, NB) as i:
                    dve.wait_ge(prod, i + 1)
                    dve.wait_ge(turned, i)
                    for m in range(2):
                        to = lt[:, m * CH:(m + 1) * CH]
                        if gbias is None:
                            ins = v.tensor_copy(to, pL[m][:, :])
                        else:
                            ins = v.tensor_scalar(to, pL[m][:, :], gbias[:, :], None, ALU.add)
                    ins.then_inc(kept, 1)
                    dve.wait_ge(turned, i + 1)
                    v.tensor_copy(logits[:, ds(i * UT, UT), 0:E], pG[:, :, :]).then_inc(put, 1)
                ch = Chain(dve, own)
                ch.n = 1
                dve.wait_ge(put, NB)
                for t in range(NT):
                    ins = v.max(best[:, t, :], logits[:, t, :])
                ch.link(ins)
                for t in range(NT):
                    ins = v.max_index(at[:, t, :], best[:, t, :], logits[:, t, :])
                ch.link(ins)
                ch.link(v.tensor_copy(at_f[:, :, :], at[:, :, 0:2]))
                v.tensor_tensor(ex[:, :, :], logits[:, :, :], best[:, :, 0:1].to_broadcast([P, NT, 8]),
                                ALU.subtract).then_inc(asked, 1)
                dve.wait_ge(given, 1)
                ch.link(v.tensor_reduce(z[:, :, 0], ex[:, :, :], AX.X, ALU.add))
                ch.link(v.reciprocal(z[:, :, :], z[:, :, :]))
                ch.link(v.tensor_tensor(dd[:, :, :], best[:, :, 1:2], best[:, :, 0:1], ALU.subtract))
                v.nop().then_inc(asked, 1)
                dve.wait_ge(given, 2)
                ch.link(v.tensor_tensor(w2[:, :, :], dd[:, :, :], z[:, :, :], ALU.mult))
                ch.link(v.tensor_copy(w1[:, :, :], z[:, :, :]))
                if gbias is not None:
                    v.tensor_tensor(w2[:, :, :], w2[:, :, :], w1[:, :, :], ALU.subtract).then_inc(asked, 1)
                    dve.wait_ge(given, 3)
                    ch.link(v.memset(w1[:, :, :], 1.0))
                ch.link(v.tensor_tensor(z[:, :, :], w1[:, :, :], w2[:, :, :], ALU.add))
                ch.link(v.reciprocal(z[:, :, :], z[:, :, :]))
                ch.link(v.tensor_tensor(w1[:, :, :], w1[:, :, :], z[:, :, :], ALU.mult))
                ch.link(v.tensor_tensor(w2[:, :, :], w2[:, :, :], z[:, :, :], ALU.mult))
                iota = c.iota[:, 0:E].rearrange("p (o e) -> p o e", o=1).to_broadcast([P, NT, E])
                h = hit[:, :, 0:E]
                ch.link(v.tensor_tensor(h, iota, at_f[:, :, 0:1].to_broadcast([P, NT, E]), ALU.is_equal))
                ch.link(v.tensor_tensor(gate[:, :, :], h, w1[:, :, :].to_broadcast([P, NT, E]), ALU.mult))
                ch.link(v.tensor_tensor(h, iota, at_f[:, :, 1:2].to_broadcast([P, NT, E]), ALU.is_equal))
                ch.link(v.tensor_tensor(h, h, w2[:, :, :].to_broadcast([P, NT, E]), ALU.mult))
                ch.link(v.tensor_tensor(gate[:, :, :], gate[:, :, :], h, ALU.add))

            @block.scalar
            def _(act):
                act.wait_ge(asked, 1)
                nc.scalar.activation(ex[:, :, :], ex[:, :, :], ACT.Exp).then_inc(given, 1)
                act.wait_ge(asked, 2)
                nc.scalar.activation(dd[:, :, :], dd[:, :, :], ACT.Exp).then_inc(given, 1)
                if gbias is not None:
                    act.wait_ge(asked, 3)
                    nc.scalar.activation(w2[:, :, :], w2[:, :, :], ACT.Exp).then_inc(given, 1)


def experts_gelu(nc, kit, c, a, xT, gate9, X):
    NE9 = E0 + 1
    with kit.stage() as st:
        sb, ps, sem = st.sb, st.ps, st.sem
        w1n = sb("w1n", [P, 2, F0])
        w1 = sb("w1", [P, 2, F0])
        w2 = sb("w2", [P, FT0, D])
        b1 = sb("b1", [P, FT0])
        b2 = sb("b2", [P, D])
        hT = sb("hT", [P, FT0, UT * P])
        tmp = sb("tmp", [P, 2, D])
        p1 = [ps(f"p1{k}", [P, 512]) for k in range(4)]
        p2 = [ps(f"p2{k}", [P, 512]) for k in range(3)]
        w1_loaded, w1_put, w2_loaded = sem("w1_loaded"), sem("w1_put"), sem("w2_loaded")
        up, bent, down, tmp_made, added = sem("up"), sem("bent"), sem("down"), sem("tmpm"), sem("added")
        passed = [sem(f"passed{k}") for k in range(3)]
        UPS = 2 * FT0
        with nc.Block() as block:
            @block.sync
            def _(sp):
                with sp.Fori(0, NE9) as e:
                    sp.wait_ge(w1_put, e)
                    sp.dma_start(w1n[:, :, :], a["W1all"][ds(e), :, :].rearrange("o (k p) f -> p (o k) f", p=P)
                                 ).then_inc(w1_loaded, 16)
                    sp.wait_ge(added, e * NT)
                    sp.wait_ge(bent, e * NB * UPS)
                    sp.dma_start(w2[:, :, :], a["W2all"][ds(e), :, :].rearrange("o (f p) d -> p (o f) d", p=P)
                                 ).then_inc(w2_loaded, 16)
                    sp.dma_start(b1[:, :], a["b1all"][ds(e), :, :].rearrange("o p f -> p (o f)")
                                 ).then_inc(w2_loaded, 16)
                    sp.dma_start(b2[:, :], a["b2all"][ds(e), :].to_broadcast([P, D])).then_inc(w2_loaded, 16)

            @block.gpsimd
            def _(pool):
                with pool.Fori(0, NE9) as e:
                    pool.wait_ge(w1_loaded, (e + 1) * 16)
                    pool.wait_ge(up, e * NB * UPS)
                    pool.sem_inc(passed[0], 1)
                    nc.gpsimd.tensor_copy(w1[:, :, :], w1n[:, :, :]).then_inc(w1_put, 1)

            @block.tensor
            def _(pe):
                with pe.Fori(0, NE9) as e:
                    pe.wait_ge(w1_put, e + 1)
                    pe.sem_inc(passed[1], 1)
                    with pe.Fori(0, NB) as i:
                        o = e * (NB * UPS) + i * UPS
                        t0 = e * NT + i * UT
                        for m in range(2):
                            for f in range(FT0):
                                u = m * FT0 + f
                                if u >= 4:
                                    pe.wait_ge(bent, o + (u - 3))
                                else:
                                    pe.wait_ge(bent, o)
                                for k in range(2):
                                    ins = nc.tensor.matmul(p1[u % 4][:, 0:CH], w1[:, k, f * P:(f + 1) * P],
                                                           xT[:, k, ds(i * UT * P + m * CH, CH)],
                                                           start=(k == 0), stop=(k == 1))
                                ins.then_inc(up, 1)
                        pe.wait_ge(w2_loaded, (e + 1) * 48)
                        for t in range(UT):
                            pe.wait_ge(bent, o + (FT0 if (t + 1) * P <= CH else UPS))
                            pe.wait_ge(tmp_made, t0 + (t - 2) if t >= 3 else t0)
                            for f in range(FT0):
                                ins = nc.tensor.matmul(p2[t % 3][:, 0:D], hT[:, f, t * P:(t + 1) * P], w2[:, f, :],
                                                       start=(f == 0), stop=(f == FT0 - 1))
                            ins.then_inc(down, 1)

            @block.scalar
            def _(act):
                with act.Fori(0, NE9) as e:
                    act.wait_ge(w2_loaded, (e + 1) * 48)
                    with act.Fori(0, NB) as i:
                        o = e * (NB * UPS) + i * UPS
                        t0 = e * NT + i * UT
                        act.wait_ge(down, t0)
                        for m in range(2):
                            for f in range(FT0):
                                u = m * FT0 + f
                                act.wait_ge(up, o + (u + 1))
                                nc.scalar.activation(hT[:, f, m * CH:(m + 1) * CH], p1[u % 4][:, 0:CH], ACT.Gelu,
                                                     bias=b1[:, f:f + 1]).then_inc(bent, 1)

            @block.vector
            def _(dve):
                v = nc.vector
                with dve.Fori(0, NE9) as e:
                    dve.wait_ge(w2_loaded, (e + 1) * 48)
                    dve.sem_inc(passed[2], 1)
                    with dve.Fori(0, NB) as i:
                        for t in range(UT):
                            T = e * NT + i * UT + t
                            n = ds(i * UT + t)
                            dve.wait_ge(added, T - 1 if t else T)
                            dve.sem_inc(passed[2], 1)
                            dve.wait_ge(down, T + 1)
                            v.tensor_tensor(tmp[:, t % 2, :], p2[t % 3][:, 0:D], b2[:, :], ALU.add
                                            ).then_inc(tmp_made, 1)
                            dve.wait_ge(tmp_made, T + 1)
                            x = X[:, n, :].rearrange("p o d -> p (o d)")
                            v.scalar_tensor_tensor(out=x, in0=tmp[:, t % 2, :],
                                                   scalar=gate9[:, n, ds(e)].rearrange("p o e -> p (o e)"),
                                                   in1=x, op0=ALU.mult, op1=ALU.add).then_inc(added, 1)


def experts_relu(nc, kit, c, a, xT, gate, X, out):
    with kit.stage() as st:
        sb, ps, sem = st.sb, st.ps, st.sem
        sw1, sw2, sw3 = sb("sw1", [P, 2, D]), sb("sw2", [P, 2, P]), sb("sw3", [P, D])
        ew1, ew2, ew3 = sb("ew1", [P, E1, 2, P]), sb("ew2", [P, E1, 64]), sb("ew3", [64, E1, D])
        sb1, sb2, sb3 = sb("sb1", [P, 2]), sb("sb2", [P, 1]), sb("sb3", [P, D])
        eb1, eb2, eb3 = sb("eb1", [P, E1]), sb("eb2", [64, E1]), sb("eb3", [P, E1, D])
        h1 = sb("h1", [P, 6, UT * P])
        h2 = sb("h2", [P, UT * P])
        g2 = sb("g2", [64, E1, UT * P])
        tmp = sb("tmp", [P, 5, D])
        p1 = [ps(f"p1{k}", [P, 512]) for k in range(4)]
        p3 = [ps(f"p3{k}", [P, 512]) for k in range(4)]
        loaded, up, bent, down, tmp_made, added, stored = (sem(x) for x in (
            "loaded", "up", "bent", "down", "tmpm", "added", "stored"))
        UPS = 2 * (6 + 5)
        NL = 12
        with nc.Block() as block:
            @block.sync
            def _(sp):
                for to, fr in (
                        (sw1[:, :, :], a["L1_ffn_sW1"].rearrange("(k p) f -> p k f", p=P)),
                        (sw2[:, :, :], a["L1_ffn_sW2"].rearrange("(k p) f -> p k f", p=P)),
                        (sw3[:, :], a["L1_ffn_sW3"]),
                        (ew1[:, :, :, :].rearrange("p e k f -> p (e k) f"),
                         a["L1_ffn_eW1"].rearrange("e (k p) f -> p (e k) f", p=P)),
                        (ew2[:, :, :], a["L1_ffn_eW2"].rearrange("e p f -> p e f")),
                        (ew3[:, :, :], a["L1_ffn_eW3"].rearrange("e p f -> p e f")),
                        (sb1[:, :], a["L1_ffn_sb1"]),
                        (sb2[:, :], a["L1_ffn_sb2"]),
                        (sb3[:, :], a["L1_ffn_sb3"].rearrange("(o d) -> o d", o=1).to_broadcast([P, D])),
                        (eb1[:, :], a["L1_ffn_eb1"]),
                        (eb2[:, :], a["L1_ffn_eb2"]),
                        (eb3[:, :, :].rearrange("p e d -> p (e d)"),
                         a["L1_ffn_eb3"].rearrange("(o e) d -> o (e d)", o=1).to_broadcast([P, E1 * D]))):
                    sp.dma_start(to, fr).then_inc(loaded, 16)
                with sp.Fori(0, NB) as i:
                    sp.wait_ge(added, (i + 1) * UT * 5)
                    sp.dma_start(out[ds(i * UT * P, UT * P), :].rearrange("(k p) d -> p k d", p=P),
                                 X[:, ds(i * UT, UT), :]).then_inc(stored, 16)
                sp.wait_ge(stored, 16 * NB)

            @block.tensor
            def _(pe):
                pe.wait_ge(loaded, NL * 16)
                with pe.Fori(0, NB) as i:
                    o = i * UPS
                    def bank(u):
                        pe.wait_ge(bent, o + (u - 3) if u >= 4 else o)
                        return p1[u % 4]
                    for m in range(2):
                        cols = slice(m * CH, (m + 1) * CH)
                        for f in range(6):
                            pb = bank(m * 11 + f)
                            for k in range(2):
                                w = sw1[:, k, f * P:(f + 1) * P] if f < 2 else ew1[:, f - 2, k, :]
                                ins = nc.tensor.matmul(pb[:, 0:CH], w, xT[:, k, ds(i * UT * P + m * CH, CH)],
                                                       start=(k == 0), stop=(k == 1))
                            ins.then_inc(up, 1)
                        pb = bank(m * 11 + 6)
                        pe.wait_ge(bent, o + (m * 11 + 6))
                        for k in range(2):
                            ins = nc.tensor.matmul(pb[:, 0:CH], sw2[:, k, :], h1[:, k, cols],
                                                   start=(k == 0), stop=(k == 1))
                        ins.then_inc(up, 1)
                        for e in range(E1):
                            pb = bank(m * 11 + 7 + e)
                            nc.tensor.matmul(pb[0:64, 0:CH], ew2[:, e, :], h1[:, 2 + e, cols],
                                             start=True, stop=True).then_inc(up, 1)
                    for t in range(UT):
                        pe.wait_ge(bent, o + (11 if (t + 1) * P <= CH else 22))
                        for e in range(5):
                            j = t * 5 + e
                            pe.wait_ge(tmp_made, i * (5 * UT) + (j - 3 if j >= 4 else 0))
                            lhs = h2[:, t * P:(t + 1) * P] if e == 0 else g2[:, e - 1, t * P:(t + 1) * P]
                            rhs = sw3[:, :] if e == 0 else ew3[:, e - 1, :]
                            nc.tensor.matmul(p3[j % 4][:, 0:D], lhs, rhs, start=True, stop=True).then_inc(down, 1)

            @block.scalar
            def _(act):
                act.wait_ge(loaded, NL * 16)
                with act.Fori(0, NB) as i:
                    act.wait_ge(down, i * (5 * UT))
                    for m in range(2):
                        cols = slice(m * CH, (m + 1) * CH)
                        for j in range(11):
                            u = m * 11 + j
                            act.wait_ge(up, i * UPS + (u + 1))
                            pb = p1[u % 4]
                            if j < 6:
                                to, fr = h1[:, j, cols], pb[:, 0:CH]
                                bias = sb1[:, j:j + 1] if j < 2 else eb1[:, j - 2:j - 1]
                            elif j == 6:
                                to, fr, bias = h2[:, cols], pb[:, 0:CH], sb2[:, :]
                            else:
                                to, fr, bias = g2[:, j - 7, cols], pb[0:64, 0:CH], eb2[:, j - 7:j - 6]
                            nc.scalar.activation(to, fr, ACT.Relu, bias=bias).then_inc(bent, 1)

            @block.vector
            def _(dve):
                v = nc.vector
                dve.wait_ge(loaded, NL * 16)
                with dve.Fori(0, NB) as i:
                    for t in range(UT):
                        n = ds(i * UT + t)
                        x = X[:, n, :].rearrange("p o d -> p (o d)")
                        for e in range(5):
                            j = t * 5 + e
                            dve.wait_ge(down, i * (5 * UT) + (j + 1))
                            b = sb3[:, :] if e == 0 else eb3[:, e - 1, :]
                            v.tensor_tensor(tmp[:, e, :], p3[j % 4][:, 0:D], b, ALU.add).then_inc(tmp_made, 1)
                            dve.wait_ge(tmp_made, i * (5 * UT) + (j + 1))
                            if j:
                                dve.wait_ge(added, i * (5 * UT) + j)
                            if e == 0:
                                ins = v.tensor_tensor(x, x, tmp[:, e, :], ALU.add)
                            else:
                                ins = v.scalar_tensor_tensor(out=x, in0=tmp[:, e, :],
                                                             scalar=gate[:, n, e - 1:e].rearrange("p o e -> p (o e)"),
                                                             in1=x, op0=ALU.mult, op1=ALU.add)
                            ins.then_inc(added, 1)


class Consts:
    pass


def loads(nc, kit, pairs):
    with kit.stage() as st:
        loaded = st.sem("loaded")
        with nc.Block() as block:
            @block.sync
            def _(sp):
                for to, fr in pairs:
                    sp.dma_start(to, fr).then_inc(loaded, 16)
                sp.wait_ge(loaded, 16 * len(pairs))


def program(nc, a, out):
    kit = Kit(nc)
    c = Consts()

    def dram(name, shape, dt=F32):
        return nc.dram_tensor(name, shape, dt).ap()

    c.t_src, c.t_dst = dram("t_src", [TROWS, P], I32), dram("t_dst", [TROWS, P], I32)
    c.t_w = dram("t_w", [TROWS, P])
    c.pay = dram("pay", [TROWS, P * H])
    c.spread = dram("spread", [EP, 2 * H])
    c.emax = dram("emax", [EP, H])
    table = [dram(f"table{k}", [NP, D]) for k in range(2)]
    c.src_logit = dram("src_logit", [NP, H])

    with kit.stage() as whole:
        c.ident, c.ones = whole.sb("ident", [P, P]), whole.sb("ones", [P, P])
        c.iota = whole.sb("iota", [P, P + 1])
        c.far_i = whole.sb("far_i", [P, P], I32)
        c.idx = whole.sb("idx", [P, GMAX], I32)
        c.drel, c.ew = whole.sb("drel", [P, GMAX]), whole.sb("ew", [P, GMAX])
        c.first_step = whole.sb("first_step", [1, NT + 1], I32)
        c.gbias = whole.sb("gbias", [P, D])
        c.zero_row = whole.sb("zero_row", [1, RW])
        X = whole.sb("X", [P, NT, D])
        with kit.stage() as gat:
            c.te_i = gat.sb("te_i", [P, GC], I32)
            c.first_edge = gat.sb("first_edge", [P, NT], I32)
            c.goes_on = gat.sb("goes_on", [P, EC])
            c.pen_fwd = gat.sb("pen_fwd", [P, EC])
            c.pen_bwd = gat.sb("pen_bwd", [P, EC])
            c.edge_pen = gat.sb("edge_pen", [P, 3])
            c.wp = gat.sb("wp", [P, 2, D + 2 * H])
            c.logit = gat.sb("logit", [P, NT, 2 * H])
            constants(nc, kit, c)
            step_tables(nc, kit, c, a)
            attention_weights(nc, kit, c, a, 0)
            norm_stage(nc, kit, c, a, None, "input", {"rows": table[0], "logits": c.src_logit}, "project")
            for layer in range(3):
                edge_paid = gat.sb("paid", [P, H, GMAX]) if layer == 0 else c.paid
                c.paid = edge_paid
                edge_softmax(nc, kit, c, a, layer)
                if layer < 2:
                    next_weights(nc, kit, c, a, layer)
                    edge_pass(nc, kit, c, a, table[layer % 2], "project",
                              {"rows": table[(layer + 1) % 2], "logits": c.src_logit})
                else:
                    next_weights(nc, kit, c, a, layer)
                    edge_pass(nc, kit, c, a, table[layer % 2], "last", {"sbuf": X})
        with kit.stage() as moe:
            xT = moe.sb("xT", [P, 2, NP])
            gate9 = moe.sb("gate9", [P, NT, E0 + 1])
            wr = moe.sb("wr", [P, 2, E0])
            norm_stage(nc, kit, c, a, X, "input", {"sbuf": xT}, "turned")
            loads(nc, kit, [(wr[:, :, :], a["L0_ffn_Wr"].rearrange("(k p) e -> p k e", p=P))])
            router(nc, kit, c, xT, wr, E0, None, gate9[:, :, 1:E0 + 1])
            fill(nc, kit, gate9[:, :, 0:1], 1.0)
            experts_gelu(nc, kit, c, a, xT, gate9, X)
        with kit.stage() as mix:
            xT = mix.sb("xT2", [P, 2, NP])
            gate = mix.sb("gate4", [P, NT, E1])
            gw, gb = mix.sb("gw", [P, 2, E1]), mix.sb("gb", [E1, 1])
            with kit.stage() as st:
                emb = st.sb("emb", [P, NT, D])
                sumsq = st.sb("sumsq", [P, NT])
                w = st.sb("w", [P, 4, D])
                b = st.sb("b", [P, D])
                norm_stage(nc, kit, c, a, X, "none", {"sbuf": emb, "rows": table[0]}, "rows")
                loads(nc, kit, [
                    (w[:, 0:2, :], a["W1T"].rearrange("(k p) n -> p k n", p=P)),
                    (w[:, 2:4, :], a["W2T"].rearrange("(k p) n -> p k n", p=P)),
                    (c.gbias[:, :], a["L1_gnn_b1"].rearrange("(o n) -> o n", o=1).to_broadcast([P, D])),
                    (b[:, :], a["L1_gnn_b2"].rearrange("(o n) -> o n", o=1).to_broadcast([P, D]))])
                add_into(nc, kit, c.gbias[:, :], b[:, :])
                edge_pass(nc, kit, c, a, table[0], "mix", {"sbuf": emb, "w": w, "sumsq": sumsq})
                inverse_norms(nc, kit, sumsq)
                norm_stage(nc, kit, c, a, X, "scaled", {"sbuf": xT, "adds": emb, "scale": sumsq}, "turned")
            loads(nc, kit, [(gw[:, :, :], a["L1_ffn_gW"].rearrange("(k p) e -> p k e", p=P)),
                            (gb[:, :], a["L1_ffn_gb"])])
            router(nc, kit, c, xT, gw, E1, gb, gate[:, :, :])
            experts_relu(nc, kit, c, a, xT, gate, X, out)


def next_weights(nc, kit, c, a, layer):
    if layer < 2:
        attention_weights(nc, kit, c, a, layer + 1)
    with kit.stage() as st:
        loaded, cleared = st.sem("loaded"), st.sem("cleared")
        with nc.Block() as block:
            @block.sync
            def _(sp):
                sp.dma_start(c.gbias[:, :], a[f"L0_gnn_b{layer}"].rearrange("(a n) -> a n", a=1)
                             .to_broadcast([P, D])).then_inc(loaded, 16)
                sp.wait_ge(loaded, 16)

            @block.vector
            def _(dve):
                nc.vector.memset(c.zero_row[:, :], 0.0).then_inc(cleared, 1)


def fill(nc, kit, ap, value):
    with kit.stage() as st:
        done = st.sem("done")
        with nc.Block() as block:
            @block.vector
            def _(dve):
                nc.vector.memset(ap, value).then_inc(done, 1)


def add_into(nc, kit, to, ap):
    with kit.stage() as st:
        done = st.sem("done")
        with nc.Block() as block:
            @block.vector
            def _(dve):
                nc.vector.tensor_tensor(to, to, ap, ALU.add).then_inc(done, 1)


def inverse_norms(nc, kit, s):
    with kit.stage() as st:
        rooted, own = st.sem("rooted"), st.sem("own")
        with nc.Block() as block:
            @block.scalar
            def _(act):
                nc.scalar.activation(s[:, :], s[:, :], ACT.Sqrt).then_inc(rooted, 1)

            @block.vector
            def _(dve):
                dve.wait_ge(rooted, 1)
                nc.vector.tensor_scalar(s[:, :], s[:, :], 1e-12, None, ALU.max).then_inc(own, 1)
                dve.wait_ge(own, 1)
                nc.vector.reciprocal(s[:, :], s[:, :]).then_inc(own, 1)



def kernel(**inputs):
    import concourse.bacc as bacc
    from concourse.bass_utils import run_bass_kernel_spmd

    nc = bacc.Bacc("TRN2", target_bir_lowering=False, num_devices=1)
    v = {k: np.asarray(x) for k, x in inputs.items()}
    v["x"] = np.concatenate([v["x"], np.zeros((NP - NN, D), v["x"].dtype)])
    v["src"] = np.concatenate([v["src"], np.zeros(EP - NE, v["src"].dtype)])
    v["dst"] = np.concatenate([np.full(1, -1, v["dst"].dtype), v["dst"],
                               np.full(EP - NE + 1, FAR, v["dst"].dtype)])
    v["edge_weight"] = np.concatenate([v["edge_weight"], np.zeros(EP - NE, v["edge_weight"].dtype)])
    v["W1all"] = np.concatenate([v.pop("L0_ffn_W1s")[None], v.pop("L0_ffn_W1p")])
    v["b1all"] = np.concatenate([v.pop("L0_ffn_b1s")[None], v.pop("L0_ffn_b1p")])
    v["b1all"] = v["b1all"].reshape(E0 + 1, FT0, P).transpose(0, 2, 1)
    v["L1_ffn_sb1"] = v["L1_ffn_sb1"].reshape(2, P).T
    v["L1_ffn_sb2"] = v["L1_ffn_sb2"].reshape(P, 1)
    v["L1_ffn_eb1"], v["L1_ffn_eb2"] = v["L1_ffn_eb1"].T, v["L1_ffn_eb2"].T
    v["L1_ffn_gb"] = v["L1_ffn_gb"].reshape(E1, 1)
    v["W2all"] = np.concatenate([v.pop("L0_ffn_W2s")[None], v.pop("L0_ffn_W2p")])
    v["b2all"] = np.concatenate([v.pop("L0_ffn_b2s")[None], v.pop("L0_ffn_b2p")])
    v["W1T"] = v.pop("L1_gnn_W1").T
    v["W2T"] = v.pop("L1_gnn_W2").T
    arrays, aps = {}, {}
    for name, x in v.items():
        arrays[f"in_{name}"] = np.ascontiguousarray(x)
        aps[name] = nc.dram_tensor(f"in_{name}", x.shape, mybir.dt.from_np(x.dtype), kind="ExternalInput").ap()
    out = nc.dram_tensor("out_x", (NP, D), F32, kind="ExternalOutput").ap()
    program(nc, aps, out)
    r = run_bass_kernel_spmd(nc, [arrays], core_ids=[0])
    return r.results[0]["out_x"][0:NN]
```

```python
from contextlib import ExitStack

import numpy as np

import concourse.bass as bass
from concourse import mybir

F32 = mybir.dt.float32
I32 = mybir.dt.int32
U32 = mybir.dt.uint32
BF16 = mybir.dt.bfloat16
ALU = mybir.AluOpType
ACT = mybir.ActivationFunctionType
AX = mybir.AxisListType

P = 128
D = 256
NN = 6250
NE = 100000
NT = -(-NN // P)
NP = NT * P
EC = -(-NE // P)
EP = EC * P
H = 4
HD = D // H
SLOPE = 0.2
LN_EPS = 1e-5
BIG = 1e30
FAR = 1 << 22

RING = 16
QUAD = 4
TROWS = EC + 2
GMAX = 1024
assert EC + 4 * NT <= GMAX - RING
GC = GMAX // P

RW = D + H
UT = 7
NB = NT // UT
CH = UT * P // 2
assert UT * NB == NT and CH <= 512

E0, F0 = 8, 1024
E1 = 4
FT0 = F0 // P


class Kit:

    def __init__(self, nc):
        self.nc, self.n = nc, 0

    def stage(self):
        return Stage(self)


class Stage(ExitStack):
    def __init__(self, kit):
        super().__init__()
        self.kit, self.sems = kit, []

    def sb(self, name, shape, dt=F32):
        self.kit.n += 1
        return self.enter_context(self.kit.nc.sbuf_tensor(f"{name}_{self.kit.n}", shape, dt))

    def ps(self, name, shape, dt=F32):
        self.kit.n += 1
        n = int(np.prod(shape[1:]))
        whole = self.enter_context(self.kit.nc.psum_tensor(f"{name}_{self.kit.n}", [P, -(-n // 512) * 512], dt))
        view = whole[0:shape[0], 0:n]
        if len(shape) == 2:
            return view
        names = "abcd"[:len(shape) - 1]
        return view.rearrange(f"p ({' '.join(names)}) -> p {' '.join(names)}", **dict(zip(names, shape[1:])))

    def sem(self, name):
        self.kit.n += 1
        if not self.sems:
            self.callback(self.zero_sems)
        s = self.kit.nc.alloc_semaphore(f"{name}_{self.kit.n}")
        self.sems.append(s)
        return s

    def pool_sem(self, name):
        self.kit.n += 1
        return self.kit.nc.alloc_semaphore(f"{name}_{self.kit.n}")

    def zero_sems(self):
        nc = self.kit.nc
        with nc.Block() as block:
            @block.gpsimd
            def _(pool):
                for s in self.sems:
                    pool.sem_clear(s)
        for s in self.sems:
            nc.release_semaphore(s)


class Chain:

    def __init__(self, eng, sem):
        self.eng, self.sem, self.n = eng, sem, 0

    def link(self, ins):
        self.n += 1
        ins.then_inc(self.sem, 1)
        self.eng.wait_ge(self.sem, self.n)


def ds(start, size=1):
    return bass.ds(start, size)



def constants(nc, kit, c):
    with kit.stage() as st:
        zeroed = st.sem("zeroed")
        made = st.sem("made")
        counted = st.sem("counted")
        iota_i = st.sb("iota_i", [P, P + 1], I32)
        with nc.Block() as block:
            @block.gpsimd
            def _(pool):
                nc.gpsimd.memset(c.ident[:, :], 0.0).then_inc(zeroed, 1)
                nc.gpsimd.memset(c.ones[:, :], 1.0).then_inc(made, 1)
                pool.wait_ge(zeroed, 1)
                nc.gpsimd.affine_select(out=c.ident[:, :], in_=c.ident[:, :], compare_op=ALU.not_equal,
                                        fill=1.0, base=0, pattern=[[-1, P]], channel_multiplier=1
                                        ).then_inc(made, 1)
                nc.gpsimd.iota(iota_i[:, :], pattern=[[1, P + 1]], base=0, channel_multiplier=0
                               ).then_inc(counted, 1)

            @block.vector
            def _(dve):
                dve.wait_ge(counted, 1)
                nc.vector.tensor_copy(c.iota[:, :], iota_i[:, :]).then_inc(made, 1)


def step_tables(nc, kit, c, a):
    with kit.stage() as st:
        sb, ps, sem = st.sb, st.ps, st.sem
        dst_i = sb("dst_i", [P, EC], I32)
        prev_i = sb("prev_i", [P, EC], I32)
        next_i = sb("next_i", [P, EC], I32)
        dst_f = sb("dst_f", [P, EC])
        oth_f = sb("oth_f", [P, EC])
        junk = sb("junk", [P, EC])
        below = sb("below", [P, NT + 1])
        bound_i = sb("bound_i", [P, NT + 1], I32)
        blk_i = sb("blk_i", [P, 2 * (NT + 1)], I32)
        blk_f = sb("blk_f", [P, 2 * (NT + 1)])
        cnt = sb("cnt", [P, NT])
        has = sb("has", [P, NT])
        cnt_i = sb("cnt_i", [P, NT], I32)
        gs = sb("gs", [P, NT + 1])
        off = sb("off", [P, NT])
        d_off = sb("d_off", [P, NT])
        gnum_i = sb("gnum_i", [P, GC], I32)
        gnum = sb("gnum", [P, GC])
        le = sb("le", [P, NT])
        tn = sb("tn", [P, GC])
        te = sb("te", [P, GC])
        tmp = sb("tmp", [P, GC])
        zrow = sb("zrow", [P, P])
        zsp = sb("zsp", [P, EC * 8])
        rows_i = sb("rows_i", [P, GC, P], I32)
        rows_d = sb("rows_d", [P, GC, P], I32)
        rows_w = sb("rows_w", [P, GC, P])
        rows_s = sb("rows_s", [P, GC, P])
        rows_r = sb("rows_r", [P, GC, P])
        psum = ps("psum", [P, 3, 4, P])
        pcol = ps("pcol", [P, NT + 1])
        loaded = sem("loaded")
        dve_own = sem("dve_own")
        numbered = sem("numbered")
        table = sem("table")
        counted = sem("counted")
        summed = sem("summed")
        chosen = sem("chosen")
        fetched = st.pool_sem("fetched")
        laid = sem("laid")
        turned = sem("turned")
        kept = sem("kept")
        sel = sb("sel", [P, GC, NT])
        with nc.Block() as block:
            @block.sync
            def _(sp):
                sp.dma_start(dst_i[:, :], a["dst"][1:1 + EP].rearrange("(p j) -> p j", p=P)).then_inc(loaded, 16)
                sp.dma_start(prev_i[:, :], a["dst"][0:EP].rearrange("(p j) -> p j", p=P)).then_inc(loaded, 16)
                sp.dma_start(next_i[:, :], a["dst"][2:2 + EP].rearrange("(p j) -> p j", p=P)).then_inc(loaded, 16)
                e = a["dst"][1:1 + EP].rearrange("(t q) -> t q", q=P)
                sp.dma_start(c.t_dst[0:EC, :], e).then_inc(table, 16)
                sp.dma_start(c.t_src[0:EC, :], a["src"][0:EP].rearrange("(t q) -> t q", q=P)).then_inc(table, 16)
                sp.dma_start(c.t_w[0:EC, :], a["edge_weight"][0:EP].rearrange("(t q) -> t q", q=P)).then_inc(table, 16)
                sp.wait_ge(numbered, 3)
                sp.dma_start(c.t_dst[EC:TROWS, :], c.far_i[0:TROWS - EC, :]).then_inc(table, 16)
                sp.dma_start(c.t_src[EC:TROWS, :], zrow[:, :].bitcast(I32)[0:TROWS - EC, :]).then_inc(table, 16)
                sp.dma_start(c.t_w[EC:TROWS, :], zrow[0:TROWS - EC, :]).then_inc(table, 16)
                sp.dma_start(c.spread.rearrange("(p j) c -> p (j c)", p=P), zsp[:, :]).then_inc(table, 16)
                sp.dma_start(c.pay[EC:TROWS, :], zsp[0:TROWS - EC, 0:H * P]).then_inc(table, 16)
                sp.wait_ge(table, 8 * 16)

            @block.gpsimd
            def _(pool):
                nc.gpsimd.iota(gnum_i[:, :], pattern=[[P, GC]], base=0, channel_multiplier=1).then_inc(numbered, 1)
                nc.gpsimd.iota(c.far_i[:, :], pattern=[[0, P]], base=FAR, channel_multiplier=0).then_inc(numbered, 1)
                pool.wait_ge(chosen, 1)
                pool.wait_ge(table, 8 * 16)
                for k in range(GC):
                    at = bass.IndirectOffsetOnAxis(ap=c.te_i[:, k:k + 1], axis=0)
                    pool.indirect_dma_start(rows_i[:, k, :], None, c.t_src, at).then_inc(fetched, 16)
                    pool.indirect_dma_start(rows_d[:, k, :], None, c.t_dst, at).then_inc(fetched, 16)
                    pool.indirect_dma_start(rows_w[:, k, :], None, c.t_w, at).then_inc(fetched, 16)

            @block.vector
            def _(dve):
                ch = Chain(dve, dve_own)
                v = nc.vector
                v.memset(zsp[:, :], 0.0)
                v.memset(zrow[:, :], 0.0).then_inc(numbered, 1)
                v.memset(off[:, :], 0.0)
                dve.wait_ge(loaded, 48)
                ch.link(v.tensor_copy(dst_f[:, :], dst_i[:, :]))
                ch.link(v.tensor_copy(oth_f[:, :], prev_i[:, :]))
                ch.link(v.tensor_tensor(c.goes_on[:, :], dst_f[:, :], oth_f[:, :], ALU.is_equal))
                ch.link(v.tensor_scalar(c.pen_fwd[:, :], c.goes_on[:, :], 1.0, BIG, ALU.subtract, ALU.mult))
                ch.link(v.tensor_copy(oth_f[:, :], next_i[:, :]))
                ch.link(v.tensor_tensor(junk[:, :], dst_f[:, :], oth_f[:, :], ALU.is_equal))
                ch.link(v.tensor_scalar(c.pen_bwd[:, :], junk[:, :], 1.0, BIG, ALU.subtract, ALU.mult))
                ch.link(v.tensor_reduce(c.edge_pen[:, 0:1], c.goes_on[:, :], AX.X, ALU.min))
                ch.link(v.tensor_reduce(c.edge_pen[:, 1:2], c.pen_fwd[:, :], AX.X, ALU.min))
                ch.link(v.tensor_reduce(c.edge_pen[:, 2:3], c.pen_bwd[:, :], AX.X, ALU.min))
                for n in range(NT + 1):
                    ch.link(v.tensor_scalar(junk[:, :], dst_f[:, :], float(P * n), None, ALU.is_lt, ALU.add,
                                            accum_out=below[:, n:n + 1]))
                v.nop().then_inc(counted, 1)
                dve.wait_ge(summed, 1)
                ch.link(v.tensor_copy(bound_i[:, :], pcol[:, :]))
                ch.link(v.tensor_scalar(blk_i[:, 0:NT + 1], bound_i[:, :], 7, None, ALU.arith_shift_right))
                ch.link(v.tensor_copy(blk_f[:, 0:NT + 1], blk_i[:, 0:NT + 1]))
                ch.link(v.tensor_scalar(bound_i[:, :], bound_i[:, :], -1.0, None, ALU.add))
                ch.link(v.tensor_scalar(blk_i[:, NT + 1:], bound_i[:, :], 7, None, ALU.arith_shift_right))
                ch.link(v.tensor_copy(blk_f[:, NT + 1:], blk_i[:, NT + 1:]))
                ch.link(v.tensor_copy(below[:, :], pcol[:, :]))
                ch.link(v.tensor_tensor(has[:, :], below[:, 1:NT + 1], below[:, 0:NT], ALU.is_gt))
                ch.link(v.tensor_tensor(cnt[:, :], blk_f[:, NT + 2:], blk_f[:, 0:NT], ALU.subtract))
                ch.link(v.tensor_scalar(cnt[:, :], cnt[:, :], 1.0, None, ALU.add))
                ch.link(v.tensor_tensor(cnt[:, :], cnt[:, :], has[:, :], ALU.mult))
                ch.link(v.tensor_scalar(cnt[:, :], cnt[:, :], 1.0, float(QUAD - 1), ALU.max, ALU.add))
                ch.link(v.tensor_copy(cnt_i[:, :], cnt[:, :]))
                ch.link(v.tensor_scalar(cnt_i[:, :], cnt_i[:, :], 2, 2, ALU.arith_shift_right,
                                        ALU.logical_shift_left))
                ch.link(v.tensor_copy(cnt[:, :], cnt_i[:, :]))
                ch.link(v.memset(gs[:, :], 0.0))
                ch.link(v.tensor_tensor_scan(gs[:, 1:NT + 1], cnt[:, :], off[:, :], 0.0, ALU.add, ALU.add))
                ch.link(v.tensor_copy(c.first_step[:, :], gs[0:1, :]))
                ch.link(v.tensor_tensor(off[:, :], blk_f[:, 0:NT], gs[:, 0:NT], ALU.subtract))
                ch.link(v.tensor_copy(d_off[:, 0:1], off[:, 0:1]))
                ch.link(v.tensor_tensor(d_off[:, 1:NT], off[:, 1:NT], off[:, 0:NT - 1], ALU.subtract))
                dve.wait_ge(numbered, 3)
                ch.link(v.tensor_copy(gnum[:, :], gnum_i[:, :]))
                for k in range(GC):
                    g = gnum[:, k:k + 1]
                    ch.link(v.tensor_scalar(le[:, :], gs[:, 0:NT], g, None, ALU.is_le, ALU.add,
                                            accum_out=tn[:, k:k + 1]))
                    ch.link(v.tensor_tensor_reduce(le[:, :], le[:, :], d_off[:, :], 1.0, 0.0, ALU.mult,
                                                   ALU.add, te[:, k:k + 1]))
                ch.link(v.tensor_tensor(te[:, :], te[:, :], gnum[:, :], ALU.add))
                ch.link(v.tensor_scalar(te[:, :], te[:, :], float(EC), None, ALU.min))
                ch.link(v.tensor_scalar(tn[:, :], tn[:, :], 1.0, None, ALU.subtract))
                v.tensor_copy(c.te_i[:, :], te[:, :]).then_inc(chosen, 1)
                for k in range(GC):
                    v.tensor_scalar(sel[:, k, :], c.iota[:, 0:NT], tn[:, k:k + 1], None, ALU.is_equal)
                ch.link(v.tensor_scalar(tmp[:, :], tn[:, :], float(P), None, ALU.mult))
                dve.wait_ge(fetched, 3 * GC * 16)
                ch.link(v.tensor_copy(rows_s[:, :, :], rows_i[:, :, :]))
                ch.link(v.tensor_copy(rows_r[:, :, :], rows_d[:, :, :]))
                for k in range(GC):
                    ins = v.tensor_scalar(rows_r[:, k, :], rows_r[:, k, :], tmp[:, k:k + 1], None, ALU.subtract)
                ch.link(ins)
                v.nop().then_inc(laid, 1)
                for b in range(GC // 4):
                    s = slice(b * 4 * P, (b + 1) * 4 * P)
                    dve.wait_ge(turned, b + 1)
                    v.tensor_copy(c.idx[:, s], psum[:, 0, :, :].rearrange("p a b -> p (a b)"))
                    v.tensor_copy(c.drel[:, s], psum[:, 1, :, :].rearrange("p a b -> p (a b)"))
                    v.tensor_copy(c.ew[:, s], psum[:, 2, :, :].rearrange("p a b -> p (a b)")).then_inc(kept, 1)

            @block.tensor
            def _(pe):
                pe.wait_ge(counted, 1)
                nc.tensor.matmul(pcol[:, :], c.ones[:, :], below[:, :], start=True, stop=True).then_inc(summed, 1)
                pe.wait_ge(laid, 1)
                for b in range(GC // 4):
                    if b:
                        pe.wait_ge(kept, b)
                    for m, rows in enumerate((rows_s, rows_r, rows_w)):
                        for k in range(4):
                            ins = nc.tensor.transpose(psum[:, m, k, :], rows[:, 4 * b + k, :], c.ident[:, :])
                    ins.then_inc(turned, 1)

        step_cols = st.sb("step_cols", [P, 2, GMAX])
        lt = st.sb("lt", [P, 8, P + 1], BF16)
        ones_h = st.sb("ones_h", [P, 1], BF16)
        iota_h = st.sb("iota_h", [P, P + 1], BF16)
        rel = st.sb("rel", [P, GMAX])
        tcol = st.sb("tcol", [P, P])
        at_f = st.sb("at_f", [P, 2, NT])
        pcnt = st.ps("pcnt", [P, 2, 16])
        pfirst = st.ps("pfirst", [P, 2, NT])
        pt = st.ps("pt", [P, P])
        setup = st.sem("setup")
        compared = st.sem("compared")
        colsum = st.sem("colsum")
        moved = st.sem("moved")
        own2 = st.sem("own2")
        tposed = st.sem("tposed")
        tkept = st.sem("tkept")
        found = st.sem("found")
        NGB = GMAX // 8
        with nc.Block() as block:
            @block.vector
            def _(dve):
                v = nc.vector
                ch = Chain(dve, own2)
                ch.link(v.memset(ones_h[:, :], 1.0))
                ch.link(v.tensor_copy(iota_h[:, :], c.iota[:, :]))
                with dve.Fori(0, NGB) as i:
                    dve.wait_ge(colsum, i)
                    for k in range(8):
                        ins = v.tensor_scalar(lt[:, k, :], iota_h[:, :], c.drel[:, ds(i * 8 + k)], None, ALU.is_gt)
                    ins.then_inc(compared, 1)
                    dve.wait_ge(colsum, i + 1)
                    v.tensor_copy(step_cols[:, :, ds(i * 8, 8)], pcnt[:, :, 0:8]).then_inc(moved, 1)
                n = 0
                for m in range(2):
                    for k in range(GC):
                        n += 1
                        dve.wait_ge(tposed, n)
                        v.tensor_copy(tcol[:, :], pt[:, :]).then_inc(tkept, 1)
                dve.wait_ge(found, 1)
                ch.link(v.tensor_copy(at_f[:, :, :], pfirst[:, :, :]))
                ch.link(v.tensor_tensor(at_f[:, 1, :], at_f[:, 1, :], at_f[:, 0, :], ALU.is_equal))
                ch.link(v.tensor_scalar(at_f[:, 1, :], at_f[:, 1, :], float(FAR), None, ALU.mult))
                ch.link(v.tensor_scalar(blk_f[:, 0:NT], blk_f[:, 0:NT], float(P), None, ALU.mult))
                ch.link(v.tensor_tensor(at_f[:, 0, :], at_f[:, 0, :], blk_f[:, 0:NT], ALU.add))
                ch.link(v.tensor_tensor(at_f[:, 0, :], at_f[:, 0, :], at_f[:, 1, :], ALU.add))
                ch.link(v.tensor_copy(c.first_edge[:, :], at_f[:, 0, :]))

            @block.tensor
            def _(pe):
                with pe.Fori(0, NGB) as i:
                    pe.wait_ge(compared, i + 1)
                    pe.wait_ge(moved, i)
                    for k in range(8):
                        nc.tensor.matmul(pcnt[:, 0, k:k + 1], lt[:, k, 0:P], ones_h[:, :], start=True, stop=True)
                        ins = nc.tensor.matmul(pcnt[:, 1, k:k + 1], lt[:, k, 1:P + 1], ones_h[:, :],
                                               start=True, stop=True)
                    ins.then_inc(colsum, 1)
                pe.wait_ge(moved, NGB)
                n = 0
                for m in range(2):
                    for k in range(GC):
                        if n:
                            pe.wait_ge(tkept, n)
                        nc.tensor.transpose(pt[:, :], step_cols[:, m, k * P:(k + 1) * P], c.ident[:, :]
                                            ).then_inc(tposed, 1)
                        n += 1
                        pe.wait_ge(tkept, n)
                        ins = nc.tensor.matmul(pfirst[:, m, :], tcol[:, :], sel[:, k, :],
                                               start=(k == 0), stop=(k == GC - 1))
                ins.then_inc(found, 1)



def norm_stage(nc, kit, c, a, X, add, outs, want):
    with kit.stage() as st:
        sb, ps, sem = st.sb, st.ps, st.sem
        xin = sb("xin", [P, UT, D])
        xs = sb("xs", [P, UT, D])
        stats = sb("stats", [P, UT, 6])
        mv = sb("mv", [P, UT, 2])
        std = sb("std", [P, UT])
        rstd = sb("rstd", [P, UT])
        pT = [ps(f"pT{k}", [P, 2, P]) for k in range(2)]
        loaded, own, varied, rooted = sem("loaded"), sem("own"), sem("varied"), sem("rooted")
        normed, used, turned, kept, stored = sem("normed"), sem("used"), sem("turned"), sem("kept"), sem("stored")
        read, passed = sem("read"), sem("passed")
        eps = sb("eps", [P, 1])
        if want == "project":
            xt = sb("xt", [P, 2, 2, P])
            hs = sb("hs", [P, UT, D + 2 * H])
            pH = [ps(f"pH{k}", [P, D + 2 * H]) for k in range(2)]
            prod, hkept, hstored = sem("prod"), sem("hkept"), sem("hstored")
        with nc.Block() as block:
            if add == "input":
                @block.sync
                def _(sp):
                    with sp.Fori(0, NB) as i:
                        sp.wait_ge(read, i)
                        sp.dma_start(xin[:, :, :], a["x"][ds(i * UT * P, UT * P), :].rearrange(
                            "(k p) d -> p k d", p=P)).then_inc(loaded, 16)
                        if want == "project":
                            sp.wait_ge(hkept, i * UT + UT)
                            r = ds(i * UT * P, UT * P)
                            sp.dma_start(outs["rows"][r, :].rearrange("(k p) d -> p k d", p=P),
                                         hs[:, :, 0:D]).then_inc(hstored, 16)
                            sp.dma_start(outs["logits"][r, :].rearrange("(k p) d -> p k d", p=P),
                                         hs[:, :, D:D + H]).then_inc(hstored, 16)
                    if want == "project":
                        sp.wait_ge(hstored, 32 * NB)
            elif want == "rows":
                @block.sync
                def _(sp):
                    with sp.Fori(0, NB) as i:
                        sp.wait_ge(normed, (i + 1) * UT)
                        sp.dma_start(outs["rows"][ds(i * UT * P, UT * P), :].rearrange("(k p) d -> p k d", p=P),
                                     outs["sbuf"][:, ds(i * UT, UT), :]).then_inc(stored, 16)
                    sp.wait_ge(stored, 16 * NB)

            @block.vector
            def _(dve):
                v = nc.vector
                v.memset(eps[:, :], LN_EPS).then_inc(own, 1)
                dve.wait_ge(own, 1)
                L = 2 if add == "none" or want == "project" else 3
                with dve.Fori(0, NB) as i:
                    o = i * L + 1
                    tiles = ds(i * UT, UT)
                    if want == "project":
                        src = xin
                        dve.wait_ge(loaded, (i + 1) * 16)
                    else:
                        if add == "input":
                            dve.wait_ge(loaded, (i + 1) * 16)
                            v.tensor_tensor(X[:, tiles, :], X[:, tiles, :], xin[:, :, :], ALU.add).then_inc(own, 1)
                            dve.wait_ge(own, o + 1)
                            o = o + 1
                        elif add == "scaled":
                            for k in range(UT):
                                t = ds(i * UT + k)
                                ins = v.scalar_tensor_tensor(out=X[:, t, :], in0=outs["adds"][:, t, :],
                                                             scalar=outs["scale"][:, t], in1=X[:, t, :],
                                                             op0=ALU.mult, op1=ALU.add)
                            ins.then_inc(own, 1)
                            dve.wait_ge(own, o + 1)
                            o = o + 1
                    def tile(k):
                        return xin[:, k, :] if want == "project" else X[:, ds(i * UT + k), :]
                    dve.sem_inc(passed, 1)
                    for k in range(UT):
                        ins = v.bn_stats(stats[:, k, :], tile(k))
                    ins.then_inc(own, 1)
                    dve.wait_ge(own, o + 1)
                    dve.sem_inc(passed, 1)
                    for k in range(UT):
                        ins = v.bn_aggr(mv[:, k, :], stats[:, k, :])
                    ins.then_inc(varied, 1)
                    dve.wait_ge(rooted, i + 1)
                    v.reciprocal(rstd[:, :], std[:, :]).then_inc(own, 1)
                    dve.wait_ge(own, o + 2)
                    if want != "rows":
                        dve.wait_ge(used, i * UT)
                    for k in range(UT):
                        out = outs["sbuf"][:, ds(i * UT + k), :] if want == "rows" else xs[:, k, :]
                        ins = v.tensor_scalar(out, tile(k), mv[:, k, 0:1], rstd[:, k:k + 1],
                                              ALU.subtract, ALU.mult)
                        ins.then_inc(normed, 1)
                    dve.wait_ge(normed, (i + 1) * UT)
                    if add == "input":
                        dve.sem_inc(read, 1)
                    if want == "project":
                        for k in range(UT):
                            dve.wait_ge(prod, i * UT + k + 1)
                            if k == 0:
                                dve.wait_ge(hstored, i * 32)
                            v.tensor_copy(c.logit[:, ds(i * UT + k), :], pH[k % 2][:, D:D + 2 * H])
                            v.tensor_copy(hs[:, k, :], pH[k % 2][:, :]).then_inc(hkept, 1)

            @block.scalar
            def _(act):
                with act.Fori(0, NB) as i:
                    act.wait_ge(varied, i + 1)
                    nc.scalar.activation(std[:, :], mv[:, :, 1], ACT.Sqrt, bias=eps[:, :]).then_inc(rooted, 1)
                    if want != "rows":
                        for k in range(UT):
                            act.wait_ge(turned, i * UT + k + 1)
                            if want == "project":
                                if k >= 2:
                                    act.wait_ge(prod, i * UT + k - 1)
                                else:
                                    act.wait_ge(prod, i * UT)
                                to = xt[:, k % 2, :, :]
                            else:
                                to = outs["sbuf"][:, :, ds((i * UT + k) * P, P)]
                            nc.scalar.activation(to, pT[k % 2][:, :, :], ACT.Copy).then_inc(kept, 1)

            if want != "rows":
                @block.tensor
                def _(pe):
                    with pe.Fori(0, NB) as i:
                        for k in range(UT):
                            pe.wait_ge(normed, i * UT + k + 1)
                            if k >= 2:
                                pe.wait_ge(kept, i * UT + k - 1)
                            else:
                                pe.wait_ge(kept, i * UT)
                            for h in range(2):
                                ins = nc.tensor.transpose(pT[k % 2][:, h, :], xs[:, k, h * P:(h + 1) * P],
                                                          c.ident[:, :])
                            ins.then_inc(turned, 1)
                            if want == "project":
                                pe.wait_ge(kept, i * UT + k + 1)
                                if k >= 2:
                                    pe.wait_ge(hkept, i * UT + k - 1)
                                else:
                                    pe.wait_ge(hkept, i * UT)
                                for h in range(2):
                                    ins = nc.tensor.matmul(pH[k % 2][:, :], xt[:, k % 2, h, :], c.wp[:, h, :],
                                                           start=(h == 0), stop=(h == 1))
                                ins.then_inc(prod, 1)
                        pe.wait_ge(turned, i * UT + UT)
                        pe.sem_inc(used, UT)


def attention_weights(nc, kit, c, a, layer):
    with kit.stage() as st:
        sb, ps, sem = st.sb, st.ps, st.sem
        avec = sb("avec", [P, 2, 2 * H])
        wt = sb("wt", [P, 2, D])
        pw = ps("pw", [P, 2, 2, P])
        pa = ps("pa", [P, 2, 2 * H])
        clear, loaded, turned, kept, prod = sem("clear"), sem("loaded"), sem("turned"), sem("kept"), sem("prod")
        done = sem("done")
        with nc.Block() as block:
            @block.sync
            def _(sp):
                sp.dma_start(c.wp[:, :, 0:D], a[f"L0_gnn_W{layer}"].rearrange("(k p) n -> p k n", p=P)
                             ).then_inc(loaded, 16)
                sp.dma_start(c.gbias[:, :], a[f"L0_gnn_b{layer}"].rearrange("(a n) -> a n", a=1)
                             .to_broadcast([P, D])).then_inc(loaded, 16)
                sp.wait_ge(clear, 1)
                for j, s in enumerate((a[f"L0_gnn_as{layer}"], a[f"L0_gnn_ad{layer}"])):
                    for h in range(H):
                        r = h * HD % P
                        sp.dma_start(avec[r:r + HD, h * HD // P, j * H + h:j * H + h + 1],
                                     s[h, :].rearrange("(n a) -> n a", a=1)).then_inc(loaded, 16)

            @block.vector
            def _(dve):
                nc.vector.memset(avec[:, :, :], 0.0).then_inc(clear, 1)
                dve.wait_ge(turned, 1)
                nc.vector.tensor_copy(wt[:, :, :].rearrange("p a (b n) -> p a b n", b=2), pw[:, :, :, :]).then_inc(kept, 1)
                dve.wait_ge(prod, 1)
                nc.vector.tensor_copy(c.wp[:, :, D:D + 2 * H], pa[:, :, :]).then_inc(done, 1)

            @block.tensor
            def _(pe):
                pe.wait_ge(loaded, (2 + 2 * H) * 16)
                for j in range(2):
                    for k in range(2):
                        ins = nc.tensor.transpose(pw[:, j, k, :], c.wp[:, k, j * P:(j + 1) * P], c.ident[:, :])
                ins.then_inc(turned, 1)
                pe.wait_ge(kept, 1)
                for k in range(2):
                    for j in range(2):
                        ins = nc.tensor.matmul(pa[:, k, :], wt[:, j, k * P:(k + 1) * P], avec[:, j, :],
                                               start=(j == 0), stop=(j == 1))
                ins.then_inc(prod, 1)



def edge_softmax(nc, kit, c, a, layer):
    with kit.stage() as st:
        sb, ps, sem = st.sb, st.ps, st.sem
        src_i = sb("src_i", [P, EC], I32)
        e = sb("e", [P, EC, H])
        own8 = sb("own8", [P, EC, 2 * H])
        node = sb("node", [P, EC, 2 * H])
        mx = sb("mx", [P, EC, H])
        ns = sb("ns", [P, NT, 2 * H])
        nmax = sb("nmax", [P, NT, H])
        t4 = sb("t4", [P, NT, H])
        ends = sb("ends", [P, 2 * H + 1])
        rows = sb("rows", [2 * H, 2, P + 2])
        carry = sb("carry", [P, 2 * H])
        prow = ps("prow", [2 * H, P])
        pflag = ps("pflag", [2 * H, P])
        pcar = ps("pcar", [P, 2 * H])
        pturn = [ps(f"pturn{k}", [P, 4, P]) for k in range(2)]
        prows = sb("prows", [P, GC, H * P])
        idx8 = sb("idx8", [P, 2, 8], I32)
        gat, own, ld, self_done, spread_done = st.pool_sem("gat"), sem("own"), sem("ld"), sem("selfd"), st.pool_sem("spread")
        re_read, ended, rowed, rkept, carried = sem("reread"), sem("ended"), sem("rowed"), sem("rkept"), sem("carried")
        exped, wrote, maxed, mgot, wexp = sem("exped"), sem("wrote"), sem("maxed"), st.pool_sem("mgot"), sem("wexp")
        fetched, turned, kept = st.pool_sem("fetched"), sem("turned"), sem("kept")
        idx_put, issued, prefill = sem("idxput"), sem("issued"), sem("prefill")
        raw1, raw2, wrote_max = sem("raw1"), sem("raw2"), sem("wrote_max")
        NGB = -(-EC // 8)
        GB2 = NGB // 2
        with nc.Block() as block:
            @block.sync
            def _(sp):
                sp.dma_start(src_i[:, :], a["src"][0:EP].rearrange("(p j) -> p j", p=P)).then_inc(ld, 16)
                sp.wait_ge(spread_done, 16 * NT)
                sp.dma_start(own8[:, :, :], c.spread.rearrange("(p j) c -> p j c", p=P)).then_inc(re_read, 16)
                sp.wait_ge(maxed, 1)
                sp.dma_start(c.emax.rearrange("(p j) c -> p j c", p=P), mx[:, :, :]).then_inc(wrote_max, 16)
                sp.wait_ge(exped, 1)
                sp.dma_start(c.pay[0:EC, :].rearrange("t (q h) -> (t q) h", h=H).rearrange(
                    "(p j) h -> p j h", p=P), e[:, :, :]).then_inc(wrote, 16)

            @block.gpsimd
            def _(pool):
                pool.wait_ge(self_done, 1)
                for t in range(NT):
                    pool.indirect_dma_start(c.spread, bass.IndirectOffsetOnAxis(ap=c.first_edge[:, t:t + 1], axis=0),
                                            ns[:, t, :], None, bounds_check=EP - 1, oob_is_err=False
                                            ).then_inc(spread_done, 16)
                pool.wait_ge(ld, 16)
                for j in range(EC):
                    pool.indirect_dma_start(e[:, j, :], None, c.src_logit,
                                            bass.IndirectOffsetOnAxis(ap=src_i[:, j:j + 1], axis=0)
                                            ).then_inc(gat, 16)
                pool.wait_ge(wrote_max, 16)
                pool.wait_ge(prefill, 1)
                for t in range(NT):
                    pool.indirect_dma_start(nmax[:, t, :], None, c.emax,
                                            bass.IndirectOffsetOnAxis(ap=c.first_edge[:, t:t + 1], axis=0),
                                            bounds_check=EP - 1, oob_is_err=False).then_inc(mgot, 16)
                pool.wait_ge(wrote, 16)
                for k in range(GC):
                    pool.indirect_dma_start(prows[:, k, :], None, c.pay,
                                            bass.IndirectOffsetOnAxis(ap=c.te_i[:, k:k + 1], axis=0)
                                            ).then_inc(fetched, 16)

            @block.vector
            def _(dve):
                v = nc.vector
                ch = Chain(dve, own)
                ch.link(v.tensor_copy(ns[:, :, 0:H], c.logit[:, :, H:2 * H]))
                ch.link(v.tensor_tensor(t4[:, :, :], c.logit[:, :, 0:H], c.logit[:, :, H:2 * H], ALU.add))
                v.scalar_tensor_tensor(out=ns[:, :, H:2 * H], in0=t4[:, :, :], scalar=SLOPE, in1=t4[:, :, :],
                                       op0=ALU.mult, op1=ALU.max).then_inc(self_done, 1)
                dve.wait_ge(self_done, 1)
                v.tensor_copy(nmax[:, :, :], ns[:, :, H:2 * H]).then_inc(prefill, 1)

                def scan(out, flags, vals, ncol, op0, op1, init, back, flag_end, n):
                    s = slice(None, None, -1) if back else slice(None)
                    last = 0 if back else EC - 1
                    for h in range(ncol):
                        ins = v.tensor_tensor_scan(out[:, s, h], flags[:, s], vals[:, s, h], init, op0, op1)
                    ch.link(ins)
                    ch.link(v.tensor_copy(ends[:, 0:ncol], out[:, last, 0:ncol]))
                    ch.link(v.tensor_copy(carry[:, 0:ncol], flag_end.to_broadcast([P, ncol])))
                    v.nop().then_inc(ended, 1)
                    dve.wait_ge(rowed, n)
                    ch.link(v.memset(rows[:, 1, :], init))
                    ch.link(v.tensor_copy(rows[0:ncol, 0, 0:P], pflag[0:ncol, :]))
                    row_out = rows[0:ncol, 1, P - 1::-1] if back else rows[0:ncol, 1, 1:P + 1]
                    row_s = slice(None, None, -1) if back else slice(None)
                    if back:
                        ch.link(v.tensor_tensor_scan(rows[0:ncol, 1, P - 2::-1], rows[0:ncol, 0, P - 1:0:-1],
                                                     prow[0:ncol, P - 1:0:-1], init, op0, op1))
                    else:
                        ch.link(v.tensor_tensor_scan(rows[0:ncol, 1, 1:P], rows[0:ncol, 0, 0:P - 1],
                                                     prow[0:ncol, 0:P - 1], init, op0, op1))
                    v.nop().then_inc(rkept, 1)
                    dve.wait_ge(carried, n)
                    ch.link(v.tensor_copy(carry[:, 0:ncol], pcar[:, 0:ncol]))
                    for h in range(ncol):
                        ins = v.tensor_tensor_scan(out[:, s, h], flags[:, s], vals[:, s, h],
                                                   carry[:, h:h + 1], op0, op1)
                    ch.link(ins)

                dve.wait_ge(re_read, 16)
                ch.link(v.tensor_scalar(mx[:, :, 0], c.goes_on[:, :], -1.0, 1.0, ALU.mult, ALU.add))
                ch.link(v.tensor_tensor(own8[:, :, :], own8[:, :, :],
                                        mx[:, :, 0:1].to_broadcast([P, EC, 2 * H]), ALU.mult))
                scan(node, c.goes_on, own8, 2 * H, ALU.mult, ALU.add, 0.0, False, c.edge_pen[:, 0:1], 1)
                dve.wait_ge(gat, 16 * EC)
                ch.link(v.tensor_tensor(e[:, :, :], e[:, :, :], node[:, :, 0:H], ALU.add))
                ch.link(v.scalar_tensor_tensor(out=e[:, :, :], in0=e[:, :, :], scalar=SLOPE, in1=e[:, :, :],
                                               op0=ALU.mult, op1=ALU.max))
                scan(own8, c.pen_fwd, e, H, ALU.add, ALU.max, -BIG, False, c.edge_pen[:, 1:2], 2)
                scan(mx, c.pen_bwd, own8, H, ALU.add, ALU.max, -BIG, True, c.edge_pen[:, 2:3], 3)
                ch.link(v.tensor_tensor(mx[:, :, :], mx[:, :, :], node[:, :, H:2 * H], ALU.max))
                v.nop().then_inc(maxed, 1)
                v.tensor_tensor(e[:, :, :], e[:, :, :], mx[:, :, :], ALU.subtract).then_inc(raw1, 1)
                dve.wait_ge(mgot, 16 * NT)
                v.tensor_tensor(nmax[:, :, :], ns[:, :, H:2 * H], nmax[:, :, :], ALU.subtract).then_inc(raw2, 1)
                for k in range(GC):
                    dve.wait_ge(turned, k + 1)
                    v.tensor_copy(c.paid[:, k * P:(k + 1) * P, :].rearrange("p g h -> p h g"), pturn[k % 2][:, :, :]
                                  ).then_inc(kept, 1)

            @block.scalar
            def _(act):
                act.wait_ge(raw1, 1)
                nc.scalar.activation(e[:, :, :], e[:, :, :], ACT.Exp).then_inc(exped, 1)
                act.wait_ge(raw2, 1)
                nc.scalar.activation(c.self_w[:, :, :], nmax[:, :, :], ACT.Exp).then_inc(wexp, 1)

            @block.tensor
            def _(pe):
                for n, ncol in ((1, 2 * H), (2, H), (3, H)):
                    pe.wait_ge(ended, n)
                    nc.tensor.transpose(prow[0:ncol, :], ends[:, 0:ncol], c.ident[:, :])
                    nc.tensor.transpose(pflag[0:ncol, :], carry[:, 0:ncol], c.ident[:, :]).then_inc(rowed, 1)
                    pe.wait_ge(rkept, n)
                    nc.tensor.transpose(pcar[:, 0:ncol], rows[0:ncol, 1, 0:P], c.ident[0:ncol, 0:ncol]
                                        ).then_inc(carried, 1)
                pe.wait_ge(fetched, 16 * GC)
                for k in range(GC):
                    if k >= 2:
                        pe.wait_ge(kept, k - 1)
                    for h in range(H):
                        ins = nc.tensor.transpose(pturn[k % 2][:, h, :], prows[:, k, h::H], c.ident[:, :])
                    ins.then_inc(turned, 1)


def edge_pass(nc, kit, c, table, att, accs):
    W = RW if att else D
    with kit.stage() as st:
        sb, ps, sem = st.sb, st.ps, st.sem
        rows = sb("rows", [P, RING, RW])
        hot = sb("hot", [P, QUAD, P])
        ix = sb("ix", [P, RING], I32)
        zero = sb("zero", [1, RW])
        acc = ps("acc", [P, 2, 512])
        landed = [st.pool_sem(f"landed{q}") for q in range(RING // QUAD)]
        index_put = sem("index_put")
        freed = sem("freed")
        hot_made = sem("hot_made")
        weighed = sem("weighed")
        cleared = sem("cleared")
        summed = sem("summed")
        kept = sem("kept")
        passed = [sem(f"passed{k}") for k in range(3)]
        PAIRS = RING // 2
        with nc.Block() as block:
            def bodies(eng):
                total = eng.value_load(c.first_step[0:1, NT:NT + 1], min_val=QUAD * NT, max_val=GMAX - RING)
                return eng.snap((total + (RING - 1)) >> (RING.bit_length() - 1))

            @block.gpsimd
            def _(pool):
                nb = bodies(pool)
                with pool.Fori(0, nb) as i:
                    for h in range(2):
                        pool.wait_ge(freed, i * PAIRS + (h + 1) * PAIRS // 2)
                        pool.sem_inc(passed[0], 1)
                        half = slice(h * RING // 2, (h + 1) * RING // 2)
                        nc.gpsimd.tensor_copy(ix[:, half], c.idx[:, ds(i * RING + h * RING // 2, RING // 2)]
                                              ).then_inc(index_put, 1)
                        pool.wait_ge(index_put, i * 2 + (h + 1))
                        pool.sem_inc(passed[0], 1)
                        for k in range(half.start, half.stop):
                            pool.indirect_dma_start(rows[:, k, 0:D], None, table,
                                                    bass.IndirectOffsetOnAxis(ap=ix[:, k:k + 1], axis=0)
                                                    ).then_inc(landed[k // QUAD], 16)

            @block.vector
            def _(dve):
                v = nc.vector
                v.memset(zero[:, :], 0.0).then_inc(cleared, 1)
                dve.sem_inc(hot_made, 2)
                nb = bodies(dve)
                with dve.Fori(0, nb) as i:
                    for q in range(RING // QUAD):
                        steps = slice(q * QUAD, (q + 1) * QUAD)
                        dve.wait_ge(landed[q], (i + 1) * 16 * QUAD)
                        dve.sem_inc(passed[1], 1)
                        cols = ds(i * RING + q * QUAD, QUAD)
                        if att:
                            r = rows[:, steps, 0:D].rearrange("p s (h f) -> p s h f", h=H)
                            w = c.paid[:, cols, :].rearrange("p s (h o) -> p s h o", o=1)
                            v.tensor_tensor(r, r, w.to_broadcast([P, QUAD, H, HD]), ALU.mult)
                            v.tensor_copy(rows[:, steps, D:RW], c.paid[:, cols, :]).then_inc(weighed, 1)
                        else:
                            r = rows[:, steps, 0:D]
                            w = c.ew[:, cols].rearrange("p (s o) -> p s o", o=1)
                            v.tensor_tensor(r, r, w.to_broadcast([P, QUAD, D]), ALU.mult).then_inc(weighed, 1)
                        for b in range(2):
                            dve.wait_ge(freed, i * PAIRS + (2 * q + b + PAIRS - 1))
                            dve.wait_ge(hot_made, i * PAIRS + (2 * q + b + 1))
                            dve.sem_inc(passed[1], 1)
                            d = c.drel[:, ds(i * RING + q * QUAD + 2 * b, 2)].rearrange("p (s o) -> p s o", o=1)
                            v.tensor_tensor(hot[:, 2 * b:2 * b + 2, :],
                                            c.iota[:, 0:P].rearrange("p (o n) -> p o n", o=1).to_broadcast([P, 2, P]),
                                            d.to_broadcast([P, 2, P]), ALU.is_equal).then_inc(hot_made, 1)

            @block.tensor
            def _(pe):
                pe.sem_inc(freed, PAIRS)
                pe.wait_ge(cleared, 1)
                with pe.Fori(0, NT) as n:
                    g0 = pe.value_load(c.first_step[0:1, ds(n)], min_val=0, max_val=GMAX - RING)
                    g1 = pe.value_load(c.first_step[0:1, ds(n + 1)], min_val=0, max_val=GMAX - RING)
                    pe.wait_ge(kept, n + 1)
                    pe.sem_inc(passed[2], 1)
                    A = acc[:, ds(n & 1), 0:W].rearrange("p o d -> p (o d)")
                    nc.tensor.matmul(A, zero[0:1, 0:P], zero[0:1, 0:W], start=True, stop=False,
                                     skip_group_check=True)
                    with pe.Fori(g0, g1, QUAD) as g:
                        for b in range(QUAD):
                            if b % 2 == 0:
                                pe.wait_ge(hot_made, (g >> 1) + (b // 2 + 3))
                            row = rows[:, ds((g & (RING - QUAD)) + b), 0:W].rearrange("p o d -> p (o d)")
                            ins = nc.tensor.matmul(A, hot[:, b, :], row, start=False, stop=False,
                                                   skip_group_check=True)
                            if b % 2:
                                ins.then_inc(freed, 1)
                    nc.tensor.matmul(A, zero[0:1, 0:P], zero[0:1, 0:W], start=False, stop=True,
                                     skip_group_check=True).then_inc(summed, 1)
                pe.wait_ge(summed, NT)
                pe.sem_inc(freed, PAIRS)

            @block.scalar
            def _(act):
                act.sem_inc(kept, 2)
                with act.Fori(0, NT) as n:
                    act.wait_ge(summed, n + 1)
                    nc.scalar.activation(accs[:, ds(n), 0:W], acc[:, ds(n & 1), 0:W], ACT.Copy).then_inc(kept, 1)


def attention_end(nc, kit, c, table, accs, outs):
    project = "sbuf" not in outs
    with kit.stage() as st:
        sb, ps, sem = st.sb, st.ps, st.sem
        own_row = sb("own_row", [P, UT, D])
        rden = sb("rden", [P, NT, H])
        fin = sb("fin", [P, UT, D])
        xt = sb("xt", [P, UT, 2, P])
        hs = sb("hs", [P, UT, D + 2 * H])
        pT = [ps(f"pT{k}", [P, 2, P]) for k in range(2)]
        pH = [ps(f"pH{k}", [P, D + 2 * H]) for k in range(2)]
        loaded = [st.pool_sem(f"loaded{k}") for k in range(UT)]
        stored = [sem(f"stored{k}") for k in range(UT)]
        own, read, fin_made, turned = sem("own"), sem("read"), sem("fin_made"), sem("turned")
        kept, prod, hkept = sem("kept"), sem("prod"), sem("hkept")
        passed = [sem(f"passed{k}") for k in range(4)]

        def ring2(k):
            return UT + max(k - 1, 0)

        with nc.Block() as block:
            @block.gpsimd
            def _(pool):
                with pool.Fori(0, NB) as i:
                    for k in range(UT):
                        pool.wait_ge(read, i * UT + (k + 1))
                        pool.sem_inc(passed[3], 1)
                        pool.dma_start(own_row[:, k, :], table[ds((i * UT + k) * P, P), :]).then_inc(loaded[k], 16)

            @block.vector
            def _(dve):
                v = nc.vector
                dve.sem_inc(read, UT)
                v.tensor_tensor(rden[:, :, :], accs[:, :, D:RW], c.self_w[:, :, :], ALU.add).then_inc(own, 1)
                dve.wait_ge(own, 1)
                v.tensor_scalar(rden[:, :, :], rden[:, :, :], 1e-16, None, ALU.add).then_inc(own, 1)
                dve.wait_ge(own, 2)
                v.reciprocal(rden[:, :, :], rden[:, :, :]).then_inc(own, 1)
                dve.wait_ge(own, 3)
                with dve.Fori(0, NB) as i:
                    for k in range(UT):
                        t = ds(i * UT + k)
                        o = i * (3 * UT) + (3 * k + 3)
                        by_head = lambda ap: ap.rearrange("p o (h f) -> p (o h) f", h=H)
                        wide = lambda ap: ap.rearrange("p o (h e) -> p (o h) e", e=1).to_broadcast([P, H, HD])
                        row = own_row[:, k:k + 1, :]
                        dve.wait_ge(loaded[k], (i + 1) * 16)
                        dve.sem_inc(passed[0], 1)
                        v.tensor_tensor(by_head(row), by_head(row), wide(c.self_w[:, t, :]), ALU.mult).then_inc(own, 1)
                        dve.wait_ge(own, o + 1)
                        dve.sem_inc(passed[0], 1)
                        v.tensor_tensor(row, row, accs[:, t, 0:D], ALU.add).then_inc(own, 1)
                        dve.wait_ge(own, o + 2)
                        dve.sem_inc(passed[0], 1)
                        v.tensor_tensor(by_head(row), by_head(row), wide(rden[:, t, :]), ALU.mult).then_inc(own, 1)
                        dve.wait_ge(own, o + 3)
                        if project:
                            dve.wait_ge(turned, i * UT + (k + 1))
                            dve.sem_inc(passed[0], 1)
                            v.tensor_tensor(fin[:, k, :], own_row[:, k, :], c.gbias[:, :], ALU.add
                                            ).then_inc(fin_made, 1)
                        else:
                            dve.sem_inc(passed[0], 1)
                            v.tensor_tensor(outs["sbuf"][:, t, :], row, c.gbias[:, :].rearrange(
                                "p (o d) -> p o d", o=1), ALU.add).then_inc(fin_made, 1)
                        dve.wait_ge(fin_made, i * UT + (k + 1))
                        dve.sem_inc(read, 1)

            if project:
                @block.tensor
                def _(pe):
                    pe.sem_inc(turned, UT)
                    pe.sem_inc(prod, UT)
                    with pe.Fori(0, NB) as i:
                        for k in range(UT + 1):
                            if k < UT:
                                pe.wait_ge(fin_made, i * UT + (k + 1))
                                pe.wait_ge(kept, i * UT + ring2(k))
                                pe.sem_inc(passed[1], 1)
                                for f in range(2):
                                    ins = nc.tensor.transpose(pT[k % 2][:, f, :], fin[:, k, f * P:(f + 1) * P],
                                                              c.ident[:, :])
                                ins.then_inc(turned, 1)
                            if k:
                                m = k - 1
                                pe.wait_ge(kept, i * UT + (m + 1 + UT))
                                pe.wait_ge(hkept, i * UT + ring2(m))
                                pe.sem_inc(passed[1], 1)
                                for f in range(2):
                                    ins = nc.tensor.matmul(pH[m % 2][:, :], xt[:, m, f, :], c.wp[:, f, :],
                                                           start=(f == 0), stop=(f == 1))
                                ins.then_inc(prod, 1)

                @block.scalar
                def _(act):
                    act.sem_inc(kept, UT)
                    act.sem_inc(hkept, UT)
                    with act.Fori(0, NB) as i:
                        for k in range(UT + 1):
                            if k < UT:
                                act.wait_ge(turned, i * UT + (k + 1 + UT))
                                act.wait_ge(prod, i * UT + (k + 1))
                                act.sem_inc(passed[2], 1)
                                nc.scalar.activation(xt[:, k, :, :], pT[k % 2][:, :, :], ACT.Copy).then_inc(kept, 1)
                            if k:
                                m = k - 1
                                act.wait_ge(prod, i * UT + (m + 1 + UT))
                                act.wait_ge(stored[m], i * 32 + 32)
                                act.sem_inc(passed[2], 1)
                                nc.scalar.activation(hs[:, m, :], pH[m % 2][:, :], ACT.Copy)
                                nc.scalar.activation(c.logit[:, ds(i * UT + m), :].rearrange("p o d -> p (o d)"),
                                                     pH[m % 2][:, D:D + 2 * H], ACT.Copy).then_inc(hkept, 1)

                @block.sync
                def _(sp):
                    for k in range(UT):
                        sp.sem_inc(stored[k], 32)
                    with sp.Fori(0, NB) as i:
                        for k in range(UT):
                            sp.wait_ge(hkept, i * UT + (k + 1 + UT))
                            r = ds((i * UT + k) * P, P)
                            sp.dma_start(outs["rows"][r, :], hs[:, k, 0:D]).then_inc(stored[k], 16)
                            sp.dma_start(outs["logits"][r, :], hs[:, k, D:D + H]).then_inc(stored[k], 16)
                    for k in range(UT):
                        sp.wait_ge(stored[k], 32 * NB + 32)


def mix_end(nc, kit, c, acc, outs):
    with kit.stage() as st:
        sb, ps, sem = st.sb, st.ps, st.sem
        fin = sb("fin", [P, UT, 2 * D])
        xt = sb("xt", [P, UT, 4, P])
        ys = sb("ys", [P, 2, D])
        pT = [ps(f"pT{k}", [P, 4, P]) for k in range(2)]
        pH = [ps(f"pH{k}", [P, D]) for k in range(2)]
        junk = sb("junk", [P, D])
        own, fin_made, turned, kept = sem("own"), sem("fin_made"), sem("turned"), sem("kept")
        prod, hkept, made, put = sem("prod"), sem("hkept"), sem("made"), sem("put")
        passed = [sem(f"passed{k}") for k in range(3)]

        def ring2(k):
            return UT + max(k - 1, 0)

        with nc.Block() as block:
            @block.vector
            def _(dve):
                v = nc.vector
                dve.sem_inc(hkept, UT)
                dve.sem_inc(made, UT)
                with dve.Fori(0, NB) as i:
                    for k in range(UT + 1):
                        if k < UT:
                            t = ds(i * UT + k)
                            emb = outs["sbuf"][:, t, :]
                            dve.wait_ge(turned, i * UT + (k + 1))
                            dve.sem_inc(passed[0], 1)
                            v.tensor_copy(fin[:, k:k + 1, 0:D], emb)
                            v.tensor_tensor(fin[:, k:k + 1, D:2 * D], acc(t), emb, ALU.mult).then_inc(own, 1)
                            dve.wait_ge(own, i * (2 * UT) + (2 * k + 1))
                            dve.sem_inc(passed[0], 1)
                            v.tensor_tensor(fin[:, k:k + 1, D:2 * D], fin[:, k:k + 1, D:2 * D], acc(t), ALU.add
                                            ).then_inc(own, 1)
                            dve.wait_ge(own, i * (2 * UT) + (2 * k + 2))
                            dve.sem_inc(fin_made, 1)
                        if k:
                            m = k - 1
                            dve.wait_ge(prod, i * UT + k)
                            dve.wait_ge(put, i * UT + ring2(m))
                            dve.sem_inc(passed[0], 1)
                            y = ys[:, m % 2, :]
                            v.tensor_tensor(junk[:, :], pH[m % 2][:, :], c.gbias[:, :], ALU.add).then_inc(hkept, 1)
                            dve.wait_ge(hkept, i * UT + (k + UT))
                            dve.sem_inc(passed[0], 1)
                            v.scalar_tensor_tensor(out=y, in0=junk[:, :], scalar=SLOPE, in1=junk[:, :],
                                                   op0=ALU.mult, op1=ALU.max).then_inc(made, 1)
                            dve.wait_ge(made, i * UT + (k + UT))
                            dve.sem_inc(passed[0], 1)

            @block.tensor
            def _(pe):
                pe.sem_inc(turned, UT)
                with pe.Fori(0, NB) as i:
                    for k in range(UT + 1):
                        if k < UT:
                            pe.wait_ge(fin_made, i * UT + (k + 1))
                            pe.wait_ge(kept, i * UT + ring2(k))
                            pe.sem_inc(passed[1], 1)
                            for f in range(4):
                                ins = nc.tensor.transpose(pT[k % 2][:, f, :], fin[:, k, f * P:(f + 1) * P],
                                                          c.ident[:, :])
                            ins.then_inc(turned, 1)
                        if k:
                            m = k - 1
                            pe.wait_ge(kept, i * UT + (m + 1 + UT))
                            pe.wait_ge(hkept, i * UT + ring2(m))
                            pe.sem_inc(passed[1], 1)
                            for f in range(4):
                                ins = nc.tensor.matmul(pH[m % 2][:, :], xt[:, m, f, :], outs["w"][:, f, :],
                                                       start=(f == 0), stop=(f == 3))
                            ins.then_inc(prod, 1)

            @block.scalar
            def _(act):
                act.sem_inc(kept, UT)
                act.sem_inc(put, UT)
                with act.Fori(0, NB) as i:
                    for k in range(UT + 1):
                        if k < UT:
                            act.wait_ge(turned, i * UT + (k + 1 + UT))
                            act.sem_inc(passed[2], 1)
                            nc.scalar.activation(xt[:, k, :, :], pT[k % 2][:, :, :], ACT.Copy).then_inc(kept, 1)
                        if k:
                            m = k - 1
                            t = ds(i * UT + m)
                            act.wait_ge(made, i * UT + (k + UT))
                            act.sem_inc(passed[2], 1)
                            nc.scalar.activation(outs["sbuf"][:, t, :].rearrange("p o d -> p (o d)"),
                                                 ys[:, m % 2, :], ACT.Copy).then_inc(put, 1)

        summed = st.sem("summed")
        squares = st.sb("squares", [P, UT, D])
        squared = st.sem("squared")
        with nc.Block() as block:
            @block.scalar
            def _(act):
                act.sem_inc(summed, 1)
                with act.Fori(0, NB) as i:
                    act.wait_ge(summed, i + 1)
                    act.sem_inc(passed[2], 1)
                    nc.scalar.activation(squares[:, :, :], outs["sbuf"][:, ds(i * UT, UT), :], ACT.Square
                                         ).then_inc(squared, 1)

            @block.vector
            def _(dve):
                with dve.Fori(0, NB) as i:
                    dve.wait_ge(squared, i + 1)
                    dve.sem_inc(passed[0], 1)
                    nc.vector.tensor_reduce(outs["sumsq"][:, ds(i * UT, UT)], squares[:, :, :], AX.X, ALU.add
                                            ).then_inc(summed, 1)



def router(nc, kit, c, xT, wr, E, gbias, gate):
    with kit.stage() as st:
        sb, ps, sem = st.sb, st.ps, st.sem
        lt = sb("lt", [E, UT * P])
        logits = sb("logits", [P, NT, 8])
        best = sb("best", [P, NT, 8])
        at = sb("at", [P, NT, 8], U32)
        at_f = sb("at_f", [P, NT, 2])
        ex = sb("ex", [P, NT, 8])
        z = sb("z", [P, NT, 1])
        w1 = sb("w1", [P, NT, 1])
        w2 = sb("w2", [P, NT, 1])
        dd = sb("dd", [P, NT, 1])
        hit = sb("hit", [P, NT, 8])
        pL = [ps(f"pL{k}", [E, CH]) for k in range(2)]
        pG = ps("pG", [P, UT, E])
        prod, kept, turned, put, own = sem("prod"), sem("kept"), sem("turned"), sem("put"), sem("own")
        asked, given, passed = sem("asked"), sem("given"), sem("passed")
        with nc.Block() as block:
            @block.tensor
            def _(pe):
                with pe.Fori(0, NB) as i:
                    pe.wait_ge(kept, i)
                    for m in range(2):
                        for k in range(2):
                            ins = nc.tensor.matmul(pL[m][:, :], wr[:, k, :], xT[:, k, ds(i * UT * P + m * CH, CH)],
                                                   start=(k == 0), stop=(k == 1))
                    ins.then_inc(prod, 1)
                    pe.wait_ge(kept, i + 1)
                    pe.wait_ge(put, i)
                    pe.sem_inc(passed, 1)
                    for k in range(UT):
                        ins = nc.tensor.transpose(pG[:, k, :], lt[:, k * P:(k + 1) * P], c.ident[0:E, 0:E])
                    ins.then_inc(turned, 1)

            @block.vector
            def _(dve):
                v = nc.vector
                v.memset(logits[:, :, :], -BIG).then_inc(own, 1)
                dve.wait_ge(own, 1)
                with dve.Fori(0, NB) as i:
                    dve.wait_ge(prod, i + 1)
                    dve.wait_ge(turned, i)
                    for m in range(2):
                        to = lt[:, m * CH:(m + 1) * CH]
                        if gbias is None:
                            ins = v.tensor_copy(to, pL[m][:, :])
                        else:
                            ins = v.tensor_scalar(to, pL[m][:, :], gbias[:, :], None, ALU.add)
                    ins.then_inc(kept, 1)
                    dve.wait_ge(turned, i + 1)
                    v.tensor_copy(logits[:, ds(i * UT, UT), 0:E], pG[:, :, :]).then_inc(put, 1)
                ch = Chain(dve, own)
                ch.n = 1
                dve.wait_ge(put, NB)
                for t in range(NT):
                    ins = v.max(best[:, t, :], logits[:, t, :])
                ch.link(ins)
                for t in range(NT):
                    ins = v.max_index(at[:, t, :], best[:, t, :], logits[:, t, :])
                ch.link(ins)
                ch.link(v.tensor_copy(at_f[:, :, :], at[:, :, 0:2]))
                v.tensor_tensor(ex[:, :, :], logits[:, :, :], best[:, :, 0:1].to_broadcast([P, NT, 8]),
                                ALU.subtract).then_inc(asked, 1)
                dve.wait_ge(given, 1)
                ch.link(v.tensor_reduce(z[:, :, 0], ex[:, :, :], AX.X, ALU.add))
                ch.link(v.reciprocal(z[:, :, :], z[:, :, :]))
                ch.link(v.tensor_tensor(dd[:, :, :], best[:, :, 1:2], best[:, :, 0:1], ALU.subtract))
                v.nop().then_inc(asked, 1)
                dve.wait_ge(given, 2)
                ch.link(v.tensor_tensor(w2[:, :, :], dd[:, :, :], z[:, :, :], ALU.mult))
                ch.link(v.tensor_copy(w1[:, :, :], z[:, :, :]))
                if gbias is not None:
                    v.tensor_tensor(w2[:, :, :], w2[:, :, :], w1[:, :, :], ALU.subtract).then_inc(asked, 1)
                    dve.wait_ge(given, 3)
                    ch.link(v.memset(w1[:, :, :], 1.0))
                ch.link(v.tensor_tensor(z[:, :, :], w1[:, :, :], w2[:, :, :], ALU.add))
                ch.link(v.reciprocal(z[:, :, :], z[:, :, :]))
                ch.link(v.tensor_tensor(w1[:, :, :], w1[:, :, :], z[:, :, :], ALU.mult))
                ch.link(v.tensor_tensor(w2[:, :, :], w2[:, :, :], z[:, :, :], ALU.mult))
                iota = c.iota[:, 0:E].rearrange("p (o e) -> p o e", o=1).to_broadcast([P, NT, E])
                h = hit[:, :, 0:E]
                ch.link(v.tensor_tensor(h, iota, at_f[:, :, 0:1].to_broadcast([P, NT, E]), ALU.is_equal))
                ch.link(v.tensor_tensor(gate[:, :, :], h, w1[:, :, :].to_broadcast([P, NT, E]), ALU.mult))
                ch.link(v.tensor_tensor(h, iota, at_f[:, :, 1:2].to_broadcast([P, NT, E]), ALU.is_equal))
                ch.link(v.tensor_tensor(h, h, w2[:, :, :].to_broadcast([P, NT, E]), ALU.mult))
                ch.link(v.tensor_tensor(gate[:, :, :], gate[:, :, :], h, ALU.add))

            @block.scalar
            def _(act):
                act.wait_ge(asked, 1)
                nc.scalar.activation(ex[:, :, :], ex[:, :, :], ACT.Exp).then_inc(given, 1)
                act.wait_ge(asked, 2)
                nc.scalar.activation(dd[:, :, :], dd[:, :, :], ACT.Exp).then_inc(given, 1)
                if gbias is not None:
                    act.wait_ge(asked, 3)
                    nc.scalar.activation(w2[:, :, :], w2[:, :, :], ACT.Exp).then_inc(given, 1)


def experts_gelu(nc, kit, c, a, xT, gate9, X):
    NE9 = E0 + 1
    with kit.stage() as st:
        sb, ps, sem = st.sb, st.ps, st.sem
        w1n = sb("w1n", [P, 2, F0])
        w1 = sb("w1", [P, 2, F0])
        w2 = sb("w2", [P, FT0, D])
        b1 = sb("b1", [P, FT0])
        b2 = sb("b2", [P, D])
        hT = sb("hT", [P, FT0, UT * P])
        tmp = sb("tmp", [P, 2, D])
        p1 = [ps(f"p1{k}", [P, 512]) for k in range(4)]
        p2 = [ps(f"p2{k}", [P, 512]) for k in range(3)]
        w1_loaded, w1_put, w2_loaded = sem("w1_loaded"), sem("w1_put"), sem("w2_loaded")
        up, bent, down, tmp_made, added = sem("up"), sem("bent"), sem("down"), sem("tmpm"), sem("added")
        passed = [sem(f"passed{k}") for k in range(3)]
        UPS = 2 * FT0
        with nc.Block() as block:
            @block.sync
            def _(sp):
                with sp.Fori(0, NE9) as e:
                    sp.wait_ge(w1_put, e)
                    sp.dma_start(w1n[:, :, :], a["W1all"][ds(e), :, :].rearrange("o (k p) f -> p (o k) f", p=P)
                                 ).then_inc(w1_loaded, 16)
                    sp.wait_ge(added, e * NT)
                    sp.wait_ge(bent, e * NB * UPS)
                    sp.dma_start(w2[:, :, :], a["W2all"][ds(e), :, :].rearrange("o (f p) d -> p (o f) d", p=P)
                                 ).then_inc(w2_loaded, 16)
                    sp.dma_start(b1[:, :], a["b1all"][ds(e), :, :].rearrange("o p f -> p (o f)")
                                 ).then_inc(w2_loaded, 16)
                    sp.dma_start(b2[:, :], a["b2all"][ds(e), :].to_broadcast([P, D])).then_inc(w2_loaded, 16)

            @block.gpsimd
            def _(pool):
                with pool.Fori(0, NE9) as e:
                    pool.wait_ge(w1_loaded, (e + 1) * 16)
                    pool.wait_ge(up, e * NB * UPS)
                    pool.sem_inc(passed[0], 1)
                    nc.gpsimd.tensor_copy(w1[:, :, :], w1n[:, :, :]).then_inc(w1_put, 1)

            @block.tensor
            def _(pe):
                with pe.Fori(0, NE9) as e:
                    pe.wait_ge(w1_put, e + 1)
                    pe.sem_inc(passed[1], 1)
                    with pe.Fori(0, NB) as i:
                        o = e * (NB * UPS) + i * UPS
                        t0 = e * NT + i * UT
                        for m in range(2):
                            for f in range(FT0):
                                u = m * FT0 + f
                                if u >= 4:
                                    pe.wait_ge(bent, o + (u - 3))
                                else:
                                    pe.wait_ge(bent, o)
                                for k in range(2):
                                    ins = nc.tensor.matmul(p1[u % 4][:, 0:CH], w1[:, k, f * P:(f + 1) * P],
                                                           xT[:, k, ds(i * UT * P + m * CH, CH)],
                                                           start=(k == 0), stop=(k == 1))
                                ins.then_inc(up, 1)
                        pe.wait_ge(w2_loaded, (e + 1) * 48)
                        for t in range(UT):
                            pe.wait_ge(bent, o + (FT0 if (t + 1) * P <= CH else UPS))
                            pe.wait_ge(tmp_made, t0 + (t - 2) if t >= 3 else t0)
                            for f in range(FT0):
                                ins = nc.tensor.matmul(p2[t % 3][:, 0:D], hT[:, f, t * P:(t + 1) * P], w2[:, f, :],
                                                       start=(f == 0), stop=(f == FT0 - 1))
                            ins.then_inc(down, 1)

            @block.scalar
            def _(act):
                with act.Fori(0, NE9) as e:
                    act.wait_ge(w2_loaded, (e + 1) * 48)
                    with act.Fori(0, NB) as i:
                        o = e * (NB * UPS) + i * UPS
                        t0 = e * NT + i * UT
                        act.wait_ge(down, t0)
                        for m in range(2):
                            for f in range(FT0):
                                u = m * FT0 + f
                                act.wait_ge(up, o + (u + 1))
                                nc.scalar.activation(hT[:, f, m * CH:(m + 1) * CH], p1[u % 4][:, 0:CH], ACT.Gelu,
                                                     bias=b1[:, f:f + 1]).then_inc(bent, 1)

            @block.vector
            def _(dve):
                v = nc.vector
                with dve.Fori(0, NE9) as e:
                    dve.wait_ge(w2_loaded, (e + 1) * 48)
                    dve.sem_inc(passed[2], 1)
                    with dve.Fori(0, NB) as i:
                        for t in range(UT):
                            T = e * NT + i * UT + t
                            n = ds(i * UT + t)
                            dve.wait_ge(added, T - 1 if t else T)
                            dve.sem_inc(passed[2], 1)
                            dve.wait_ge(down, T + 1)
                            v.tensor_tensor(tmp[:, t % 2, :], p2[t % 3][:, 0:D], b2[:, :], ALU.add
                                            ).then_inc(tmp_made, 1)
                            dve.wait_ge(tmp_made, T + 1)
                            x = X[:, n, :].rearrange("p o d -> p (o d)")
                            v.scalar_tensor_tensor(out=x, in0=tmp[:, t % 2, :],
                                                   scalar=gate9[:, n, ds(e)].rearrange("p o e -> p (o e)"),
                                                   in1=x, op0=ALU.mult, op1=ALU.add).then_inc(added, 1)


def experts_relu(nc, kit, c, a, xT, gate, X, out):
    with kit.stage() as st:
        sb, ps, sem = st.sb, st.ps, st.sem
        sw1, sw2, sw3 = sb("sw1", [P, 2, D]), sb("sw2", [P, 2, P]), sb("sw3", [P, D])
        ew1, ew2, ew3 = sb("ew1", [P, E1, 2, P]), sb("ew2", [P, E1, 64]), sb("ew3", [64, E1, D])
        sb1, sb2, sb3 = sb("sb1", [P, 2]), sb("sb2", [P, 1]), sb("sb3", [P, D])
        eb1, eb2, eb3 = sb("eb1", [P, E1]), sb("eb2", [64, E1]), sb("eb3", [P, E1, D])
        h1 = sb("h1", [P, 6, UT * P])
        h2 = sb("h2", [P, UT * P])
        g2 = sb("g2", [64, E1, UT * P])
        tmp = sb("tmp", [P, 5, D])
        p1 = [ps(f"p1{k}", [P, 512]) for k in range(4)]
        p3 = [ps(f"p3{k}", [P, 512]) for k in range(4)]
        loaded, up, bent, down, tmp_made, added, stored = (sem(x) for x in (
            "loaded", "up", "bent", "down", "tmpm", "added", "stored"))
        UPS = 2 * (6 + 5)
        NL = 12
        with nc.Block() as block:
            @block.sync
            def _(sp):
                for to, fr in (
                        (sw1[:, :, :], a["L1_ffn_sW1"].rearrange("(k p) f -> p k f", p=P)),
                        (sw2[:, :, :], a["L1_ffn_sW2"].rearrange("(k p) f -> p k f", p=P)),
                        (sw3[:, :], a["L1_ffn_sW3"]),
                        (ew1[:, :, :, :].rearrange("p e k f -> p (e k) f"),
                         a["L1_ffn_eW1"].rearrange("e (k p) f -> p (e k) f", p=P)),
                        (ew2[:, :, :], a["L1_ffn_eW2"].rearrange("e p f -> p e f")),
                        (ew3[:, :, :], a["L1_ffn_eW3"].rearrange("e p f -> p e f")),
                        (sb1[:, :], a["L1_ffn_sb1"]),
                        (sb2[:, :], a["L1_ffn_sb2"]),
                        (sb3[:, :], a["L1_ffn_sb3"].rearrange("(o d) -> o d", o=1).to_broadcast([P, D])),
                        (eb1[:, :], a["L1_ffn_eb1"]),
                        (eb2[:, :], a["L1_ffn_eb2"]),
                        (eb3[:, :, :].rearrange("p e d -> p (e d)"),
                         a["L1_ffn_eb3"].rearrange("(o e) d -> o (e d)", o=1).to_broadcast([P, E1 * D]))):
                    sp.dma_start(to, fr).then_inc(loaded, 16)
                with sp.Fori(0, NB) as i:
                    sp.wait_ge(added, (i + 1) * UT * 5)
                    sp.dma_start(out[ds(i * UT * P, UT * P), :].rearrange("(k p) d -> p k d", p=P),
                                 X[:, ds(i * UT, UT), :]).then_inc(stored, 16)
                sp.wait_ge(stored, 16 * NB)

            @block.tensor
            def _(pe):
                pe.wait_ge(loaded, NL * 16)
                with pe.Fori(0, NB) as i:
                    o = i * UPS
                    def bank(u):
                        pe.wait_ge(bent, o + (u - 3) if u >= 4 else o)
                        return p1[u % 4]
                    for m in range(2):
                        cols = slice(m * CH, (m + 1) * CH)
                        for f in range(6):
                            pb = bank(m * 11 + f)
                            for k in range(2):
                                w = sw1[:, k, f * P:(f + 1) * P] if f < 2 else ew1[:, f - 2, k, :]
                                ins = nc.tensor.matmul(pb[:, 0:CH], w, xT[:, k, ds(i * UT * P + m * CH, CH)],
                                                       start=(k == 0), stop=(k == 1))
                            ins.then_inc(up, 1)
                        pb = bank(m * 11 + 6)
                        pe.wait_ge(bent, o + (m * 11 + 6))
                        for k in range(2):
                            ins = nc.tensor.matmul(pb[:, 0:CH], sw2[:, k, :], h1[:, k, cols],
                                                   start=(k == 0), stop=(k == 1))
                        ins.then_inc(up, 1)
                        for e in range(E1):
                            pb = bank(m * 11 + 7 + e)
                            nc.tensor.matmul(pb[0:64, 0:CH], ew2[:, e, :], h1[:, 2 + e, cols],
                                             start=True, stop=True).then_inc(up, 1)
                    for t in range(UT):
                        pe.wait_ge(bent, o + (11 if (t + 1) * P <= CH else 22))
                        for e in range(5):
                            j = t * 5 + e
                            pe.wait_ge(tmp_made, i * (5 * UT) + (j - 3 if j >= 4 else 0))
                            lhs = h2[:, t * P:(t + 1) * P] if e == 0 else g2[:, e - 1, t * P:(t + 1) * P]
                            rhs = sw3[:, :] if e == 0 else ew3[:, e - 1, :]
                            nc.tensor.matmul(p3[j % 4][:, 0:D], lhs, rhs, start=True, stop=True).then_inc(down, 1)

            @block.scalar
            def _(act):
                act.wait_ge(loaded, NL * 16)
                with act.Fori(0, NB) as i:
                    act.wait_ge(down, i * (5 * UT))
                    for m in range(2):
                        cols = slice(m * CH, (m + 1) * CH)
                        for j in range(11):
                            u = m * 11 + j
                            act.wait_ge(up, i * UPS + (u + 1))
                            pb = p1[u % 4]
                            if j < 6:
                                to, fr = h1[:, j, cols], pb[:, 0:CH]
                                bias = sb1[:, j:j + 1] if j < 2 else eb1[:, j - 2:j - 1]
                            elif j == 6:
                                to, fr, bias = h2[:, cols], pb[:, 0:CH], sb2[:, :]
                            else:
                                to, fr, bias = g2[:, j - 7, cols], pb[0:64, 0:CH], eb2[:, j - 7:j - 6]
                            nc.scalar.activation(to, fr, ACT.Relu, bias=bias).then_inc(bent, 1)

            @block.vector
            def _(dve):
                v = nc.vector
                dve.wait_ge(loaded, NL * 16)
                with dve.Fori(0, NB) as i:
                    for t in range(UT):
                        n = ds(i * UT + t)
                        x = X[:, n, :].rearrange("p o d -> p (o d)")
                        for e in range(5):
                            j = t * 5 + e
                            dve.wait_ge(down, i * (5 * UT) + (j + 1))
                            b = sb3[:, :] if e == 0 else eb3[:, e - 1, :]
                            v.tensor_tensor(tmp[:, e, :], p3[j % 4][:, 0:D], b, ALU.add).then_inc(tmp_made, 1)
                            dve.wait_ge(tmp_made, i * (5 * UT) + (j + 1))
                            if j:
                                dve.wait_ge(added, i * (5 * UT) + j)
                            if e == 0:
                                ins = v.tensor_tensor(x, x, tmp[:, e, :], ALU.add)
                            else:
                                ins = v.scalar_tensor_tensor(out=x, in0=tmp[:, e, :],
                                                             scalar=gate[:, n, e - 1:e].rearrange("p o e -> p (o e)"),
                                                             in1=x, op0=ALU.mult, op1=ALU.add)
                            ins.then_inc(added, 1)


class Consts:
    pass


def loads(nc, kit, pairs):
    with kit.stage() as st:
        loaded = st.sem("loaded")
        with nc.Block() as block:
            @block.sync
            def _(sp):
                for to, fr in pairs:
                    sp.dma_start(to, fr).then_inc(loaded, 16)
                sp.wait_ge(loaded, 16 * len(pairs))


def program(nc, a, out):
    kit = Kit(nc)
    c = Consts()

    def dram(name, shape, dt=F32):
        return nc.dram_tensor(name, shape, dt).ap()

    c.t_src, c.t_dst = dram("t_src", [TROWS, P], I32), dram("t_dst", [TROWS, P], I32)
    c.t_w = dram("t_w", [TROWS, P])
    c.pay = dram("pay", [TROWS, P * H])
    c.spread = dram("spread", [EP, 2 * H])
    c.emax = dram("emax", [EP, H])
    table = [dram(f"table{k}", [NP, D]) for k in range(2)]
    c.src_logit = dram("src_logit", [NP, H])

    with kit.stage() as whole:
        c.ident, c.ones = whole.sb("ident", [P, P]), whole.sb("ones", [P, P])
        c.iota = whole.sb("iota", [P, P + 1])
        c.far_i = whole.sb("far_i", [P, P], I32)
        c.idx = whole.sb("idx", [P, GMAX], I32)
        c.drel, c.ew = whole.sb("drel", [P, GMAX]), whole.sb("ew", [P, GMAX])
        c.first_step = whole.sb("first_step", [1, NT + 1], I32)
        c.gbias = whole.sb("gbias", [P, D])
        X = whole.sb("X", [P, NT, D])
        with kit.stage() as gat:
            c.te_i = gat.sb("te_i", [P, GC], I32)
            c.first_edge = gat.sb("first_edge", [P, NT], I32)
            c.goes_on = gat.sb("goes_on", [P, EC])
            c.pen_fwd = gat.sb("pen_fwd", [P, EC])
            c.pen_bwd = gat.sb("pen_bwd", [P, EC])
            c.edge_pen = gat.sb("edge_pen", [P, 3])
            c.paid = gat.sb("paid", [P, GMAX, H])
            c.self_w = gat.sb("self_w", [P, NT, H])
            c.wp = gat.sb("wp", [P, 2, D + 2 * H])
            c.logit = gat.sb("logit", [P, NT, 2 * H])
            constants(nc, kit, c)
            step_tables(nc, kit, c, a)
            attention_weights(nc, kit, c, a, 0)
            norm_stage(nc, kit, c, a, None, "input", {"rows": table[0], "logits": c.src_logit}, "project")
            for layer in range(3):
                edge_softmax(nc, kit, c, a, layer)
                with kit.stage() as st:
                    accs = st.sb("accs", [P, NT, RW])
                    edge_pass(nc, kit, c, table[layer % 2], True, accs)
                    next_weights(nc, kit, c, a, layer)
                    outs = ({"rows": table[(layer + 1) % 2], "logits": c.src_logit} if layer < 2
                            else {"sbuf": X})
                    attention_end(nc, kit, c, table[layer % 2], accs, outs)
        with kit.stage() as moe:
            xT = moe.sb("xT", [P, 2, NP])
            gate9 = moe.sb("gate9", [P, NT, E0 + 1])
            wr = moe.sb("wr", [P, 2, E0])
            norm_stage(nc, kit, c, a, X, "input", {"sbuf": xT}, "turned")
            loads(nc, kit, [(wr[:, :, :], a["L0_ffn_Wr"].rearrange("(k p) e -> p k e", p=P))])
            router(nc, kit, c, xT, wr, E0, None, gate9[:, :, 1:E0 + 1])
            fill(nc, kit, gate9[:, :, 0:1], 1.0)
            experts_gelu(nc, kit, c, a, xT, gate9, X)
        with kit.stage() as mix:
            xT = mix.sb("xT2", [P, 2, NP])
            gate = mix.sb("gate4", [P, NT, E1])
            gw, gb = mix.sb("gw", [P, 2, E1]), mix.sb("gb", [E1, 1])
            with kit.stage() as st:
                emb = st.sb("emb", [P, NT, D])
                sumsq = st.sb("sumsq", [P, NT])
                w = st.sb("w", [P, 4, D])
                b = st.sb("b", [P, D])
                norm_stage(nc, kit, c, a, X, "none", {"sbuf": emb, "rows": table[0]}, "rows")
                loads(nc, kit, [
                    (w[:, 0:2, :], a["W1T"].rearrange("(k p) n -> p k n", p=P)),
                    (w[:, 2:4, :], a["W2T"].rearrange("(k p) n -> p k n", p=P)),
                    (c.gbias[:, :], a["L1_gnn_b1"].rearrange("(o n) -> o n", o=1).to_broadcast([P, D])),
                    (b[:, :], a["L1_gnn_b2"].rearrange("(o n) -> o n", o=1).to_broadcast([P, D]))])
                add_into(nc, kit, c.gbias[:, :], b[:, :])
                sums = xT[:, :, :].rearrange("p k n -> p (k n)")
                edge_pass(nc, kit, c, table[0], False, sums.rearrange("p (t d) -> p t d", d=D))
                mix_end(nc, kit, c, lambda t: sums.rearrange("p (t d) -> p t d", d=D)[:, t, :],
                        {"sbuf": emb, "w": w, "sumsq": sumsq})
                inverse_norms(nc, kit, sumsq)
                norm_stage(nc, kit, c, a, X, "scaled", {"sbuf": xT, "adds": emb, "scale": sumsq}, "turned")
            loads(nc, kit, [(gw[:, :, :], a["L1_ffn_gW"].rearrange("(k p) e -> p k e", p=P)),
                            (gb[:, :], a["L1_ffn_gb"])])
            router(nc, kit, c, xT, gw, E1, gb, gate[:, :, :])
            experts_relu(nc, kit, c, a, xT, gate, X, out)


def next_weights(nc, kit, c, a, layer):
    if layer < 2:
        attention_weights(nc, kit, c, a, layer + 1)
    with kit.stage() as st:
        loaded = st.sem("loaded")
        with nc.Block() as block:
            @block.sync
            def _(sp):
                sp.dma_start(c.gbias[:, :], a[f"L0_gnn_b{layer}"].rearrange("(a n) -> a n", a=1)
                             .to_broadcast([P, D])).then_inc(loaded, 16)
                sp.wait_ge(loaded, 16)



def fill(nc, kit, ap, value):
    with kit.stage() as st:
        done = st.sem("done")
        with nc.Block() as block:
            @block.vector
            def _(dve):
                nc.vector.memset(ap, value).then_inc(done, 1)


def add_into(nc, kit, to, ap):
    with kit.stage() as st:
        done = st.sem("done")
        with nc.Block() as block:
            @block.vector
            def _(dve):
                nc.vector.tensor_tensor(to, to, ap, ALU.add).then_inc(done, 1)


def inverse_norms(nc, kit, s):
    with kit.stage() as st:
        rooted, own = st.sem("rooted"), st.sem("own")
        with nc.Block() as block:
            @block.scalar
            def _(act):
                nc.scalar.activation(s[:, :], s[:, :], ACT.Sqrt).then_inc(rooted, 1)

            @block.vector
            def _(dve):
                dve.wait_ge(rooted, 1)
                nc.vector.tensor_scalar(s[:, :], s[:, :], 1e-12, None, ALU.max).then_inc(own, 1)
                dve.wait_ge(own, 1)
                nc.vector.reciprocal(s[:, :], s[:, :]).then_inc(own, 1)



def kernel(**inputs):
    import concourse.bacc as bacc
    from concourse.bass_utils import run_bass_kernel_spmd

    nc = bacc.Bacc("TRN2", target_bir_lowering=False, num_devices=1)
    v = {k: np.asarray(x) for k, x in inputs.items()}
    v["x"] = np.concatenate([v["x"], np.zeros((NP - NN, D), v["x"].dtype)])
    v["src"] = np.concatenate([v["src"], np.zeros(EP - NE, v["src"].dtype)])
    v["dst"] = np.concatenate([np.full(1, -1, v["dst"].dtype), v["dst"],
                               np.full(EP - NE + 1, FAR, v["dst"].dtype)])
    v["edge_weight"] = np.concatenate([v["edge_weight"], np.zeros(EP - NE, v["edge_weight"].dtype)])
    v["W1all"] = np.concatenate([v.pop("L0_ffn_W1s")[None], v.pop("L0_ffn_W1p")])
    v["b1all"] = np.concatenate([v.pop("L0_ffn_b1s")[None], v.pop("L0_ffn_b1p")])
    v["b1all"] = v["b1all"].reshape(E0 + 1, FT0, P).transpose(0, 2, 1)
    v["L1_ffn_sb1"] = v["L1_ffn_sb1"].reshape(2, P).T
    v["L1_ffn_sb2"] = v["L1_ffn_sb2"].reshape(P, 1)
    v["L1_ffn_eb1"], v["L1_ffn_eb2"] = v["L1_ffn_eb1"].T, v["L1_ffn_eb2"].T
    v["L1_ffn_gb"] = v["L1_ffn_gb"].reshape(E1, 1)
    v["W2all"] = np.concatenate([v.pop("L0_ffn_W2s")[None], v.pop("L0_ffn_W2p")])
    v["b2all"] = np.concatenate([v.pop("L0_ffn_b2s")[None], v.pop("L0_ffn_b2p")])
    v["W1T"] = v.pop("L1_gnn_W1").T
    v["W2T"] = v.pop("L1_gnn_W2").T
    arrays, aps = {}, {}
    for name, x in v.items():
        arrays[f"in_{name}"] = np.ascontiguousarray(x)
        aps[name] = nc.dram_tensor(f"in_{name}", x.shape, mybir.dt.from_np(x.dtype), kind="ExternalInput").ap()
    out = nc.dram_tensor("out_x", (NP, D), F32, kind="ExternalOutput").ap()
    program(nc, aps, out)
    r = run_bass_kernel_spmd(nc, [arrays], core_ids=[0])
    return r.results[0]["out_x"][0:NN]
```

```python
from contextlib import ExitStack

import numpy as np

import concourse.bass as bass
from concourse import mybir

F32 = mybir.dt.float32
I32 = mybir.dt.int32
U32 = mybir.dt.uint32
BF16 = mybir.dt.bfloat16
ALU = mybir.AluOpType
ACT = mybir.ActivationFunctionType
AX = mybir.AxisListType

P = 128
D = 256
NN = 6250
NE = 100000
NT = -(-NN // P)
NP = NT * P
EC = -(-NE // P)
EP = EC * P
H = 4
HD = D // H
SLOPE = 0.2
LN_EPS = 1e-5
BIG = 1e30
FAR = 1 << 22

RING = 16
QUAD = 4
TROWS = EC + 2
GMAX = 1024
assert EC + 4 * NT <= GMAX - RING
GC = GMAX // P

RW = D + H
UT = 7
NB = NT // UT
CH = UT * P // 2
assert UT * NB == NT and CH <= 512

E0, F0 = 8, 1024
E1 = 4
FILL = 13
GS = 2 * P
SHG = -(-NP // GS)
MAXG = SHG + 2 * NP // GS + E0
FT0 = F0 // P


LOOK = 528
LOOK_C = 8
assert LOOK % 16 == 0 and LOOK < LOOK_C * P


class Kit:

    def __init__(self, nc):
        self.nc, self.n = nc, 0

    def stage(self):
        return Stage(self)


class Stage(ExitStack):
    def __init__(self, kit):
        super().__init__()
        self.kit, self.sems = kit, []

    def sb(self, name, shape, dt=F32):
        self.kit.n += 1
        return self.enter_context(self.kit.nc.sbuf_tensor(f"{name}_{self.kit.n}", shape, dt))

    def ps(self, name, shape, dt=F32):
        self.kit.n += 1
        n = int(np.prod(shape[1:]))
        whole = self.enter_context(self.kit.nc.psum_tensor(f"{name}_{self.kit.n}", [P, -(-n // 512) * 512], dt))
        view = whole[0:shape[0], 0:n]
        if len(shape) == 2:
            return view
        names = "abcd"[:len(shape) - 1]
        return view.rearrange(f"p ({' '.join(names)}) -> p {' '.join(names)}", **dict(zip(names, shape[1:])))

    def sem(self, name):
        self.kit.n += 1
        if not self.sems:
            self.callback(self.zero_sems)
        s = self.kit.nc.alloc_semaphore(f"{name}_{self.kit.n}")
        self.sems.append(s)
        return s

    def pool_sem(self, name):
        self.kit.n += 1
        return self.kit.nc.alloc_semaphore(f"{name}_{self.kit.n}")

    def zero_sems(self):
        nc = self.kit.nc
        with nc.Block() as block:
            @block.gpsimd
            def _(pool):
                for s in self.sems:
                    pool.sem_clear(s)
        for s in self.sems:
            nc.release_semaphore(s)


class Chain:

    def __init__(self, eng, sem):
        self.eng, self.sem, self.n = eng, sem, 0

    def link(self, ins):
        self.n += 1
        ins.then_inc(self.sem, 1)
        self.eng.wait_ge(self.sem, self.n)


def ds(start, size=1):
    return bass.ds(start, size)



def constants(nc, kit, c):
    with kit.stage() as st:
        zeroed = st.sem("zeroed")
        made = st.sem("made")
        counted = st.sem("counted")
        iota_i = st.sb("iota_i", [P, P + 1], I32)
        with nc.Block() as block:
            @block.gpsimd
            def _(pool):
                nc.gpsimd.memset(c.ident[:, :], 0.0).then_inc(zeroed, 1)
                nc.gpsimd.memset(c.ones[:, :], 1.0).then_inc(made, 1)
                pool.wait_ge(zeroed, 1)
                nc.gpsimd.affine_select(out=c.ident[:, :], in_=c.ident[:, :], compare_op=ALU.not_equal,
                                        fill=1.0, base=0, pattern=[[-1, P]], channel_multiplier=1
                                        ).then_inc(made, 1)
                nc.gpsimd.iota(iota_i[:, :], pattern=[[1, P + 1]], base=0, channel_multiplier=0
                               ).then_inc(counted, 1)

            @block.vector
            def _(dve):
                dve.wait_ge(counted, 1)
                nc.vector.tensor_copy(c.iota[:, :], iota_i[:, :]).then_inc(made, 1)


def step_tables(nc, kit, c, a):
    with kit.stage() as st:
        sb, ps, sem = st.sb, st.ps, st.sem
        dst_i = sb("dst_i", [P, EC], I32)
        prev_i = sb("prev_i", [P, EC], I32)
        next_i = sb("next_i", [P, EC], I32)
        dst_f = sb("dst_f", [P, EC])
        oth_f = sb("oth_f", [P, EC])
        junk = sb("junk", [P, EC])
        below = sb("below", [P, NT + 1])
        bound_i = sb("bound_i", [P, NT + 1], I32)
        blk_i = sb("blk_i", [P, 2 * (NT + 1)], I32)
        blk_f = sb("blk_f", [P, 2 * (NT + 1)])
        cnt = sb("cnt", [P, NT])
        has = sb("has", [P, NT])
        cnt_i = sb("cnt_i", [P, NT], I32)
        gs = sb("gs", [P, NT + 1])
        off = sb("off", [P, NT])
        d_off = sb("d_off", [P, NT])
        gnum_i = sb("gnum_i", [P, GC], I32)
        gnum = sb("gnum", [P, GC])
        le = sb("le", [P, NT])
        tn = sb("tn", [P, GC])
        te = sb("te", [P, GC])
        tmp = sb("tmp", [P, GC])
        zrow = sb("zrow", [P, P])
        zsp = sb("zsp", [P, EC * 8])
        rows_i = sb("rows_i", [P, GC, P], I32)
        rows_d = sb("rows_d", [P, GC, P], I32)
        rows_w = sb("rows_w", [P, GC, P])
        rows_s = sb("rows_s", [P, GC, P])
        rows_r = sb("rows_r", [P, GC, P])
        psum = ps("psum", [P, 3, 4, P])
        pcol = ps("pcol", [P, NT + 1])
        loaded = sem("loaded")
        dve_own = sem("dve_own")
        numbered = sem("numbered")
        table = sem("table")
        filled = sem("filled")
        counted = sem("counted")
        summed = sem("summed")
        chosen = sem("chosen")
        fetched = st.pool_sem("fetched")
        laid = sem("laid")
        turned = sem("turned")
        kept = sem("kept")
        sel = sb("sel", [P, GC, NT])
        with nc.Block() as block:
            @block.sync
            def _(sp):
                sp.dma_start(dst_i[:, :], a["dst"][1:1 + EP].rearrange("(p j) -> p j", p=P)).then_inc(loaded, 16)
                sp.dma_start(prev_i[:, :], a["dst"][0:EP].rearrange("(p j) -> p j", p=P)).then_inc(loaded, 16)
                sp.dma_start(next_i[:, :], a["dst"][2:2 + EP].rearrange("(p j) -> p j", p=P)).then_inc(loaded, 16)
                e = a["dst"][1:1 + EP].rearrange("(t q) -> t q", q=P)
                sp.dma_start(c.t_dst[0:EC, :], e).then_inc(table, 16)
                sp.dma_start(c.t_src[0:EC, :], a["src"][0:EP].rearrange("(t q) -> t q", q=P)).then_inc(table, 16)
                sp.dma_start(c.t_w[0:EC, :], a["edge_weight"][0:EP].rearrange("(t q) -> t q", q=P)).then_inc(table, 16)
                sp.wait_ge(numbered, 3)
                sp.dma_start(c.t_dst[EC:TROWS, :], c.far_i[0:TROWS - EC, :]).then_inc(table, 16)
                sp.dma_start(c.t_src[EC:TROWS, :], zrow[:, :].bitcast(I32)[0:TROWS - EC, :]).then_inc(table, 16)
                sp.dma_start(c.t_w[EC:TROWS, :], zrow[0:TROWS - EC, :]).then_inc(table, 16)
                sp.dma_start(c.spread.rearrange("(p j) c -> p (j c)", p=P), zsp[:, :]).then_inc(table, 16)
                sp.dma_start(c.pay[EC:TROWS, :], zsp[0:TROWS - EC, 0:H * P]).then_inc(table, 16)
                width = FILL * D
                empty = c.slots_in[NP:(MAXG + 1) * GS, :].rearrange("(f p r) d -> f p (r d)", p=P, r=FILL)
                for f in range(empty.shape[0]):
                    sp.dma_start(empty[f, :, :], zsp[:, 0:width]).then_inc(filled, 16)
                few = (SHG + 2 * NP // GS) * GS
                sp.dma_start(c.slots_out[few:, :].rearrange("(p r) d -> p (r d)", p=P),
                             zsp[:, 0:((MAXG + 1) * GS - few) // P * D]).then_inc(filled, 16)
                sp.wait_ge(filled, (empty.shape[0] + 1) * 16)
                sp.wait_ge(table, 8 * 16)

            @block.gpsimd
            def _(pool):
                nc.gpsimd.iota(gnum_i[:, :], pattern=[[P, GC]], base=0, channel_multiplier=1).then_inc(numbered, 1)
                nc.gpsimd.iota(c.far_i[:, :], pattern=[[0, P]], base=FAR, channel_multiplier=0).then_inc(numbered, 1)
                pool.wait_ge(chosen, 1)
                pool.wait_ge(table, 8 * 16)
                for k in range(GC):
                    at = bass.IndirectOffsetOnAxis(ap=c.te_i[:, k:k + 1], axis=0)
                    pool.indirect_dma_start(rows_i[:, k, :], None, c.t_src, at).then_inc(fetched, 16)
                    pool.indirect_dma_start(rows_d[:, k, :], None, c.t_dst, at).then_inc(fetched, 16)
                    pool.indirect_dma_start(rows_w[:, k, :], None, c.t_w, at).then_inc(fetched, 16)

            @block.vector
            def _(dve):
                ch = Chain(dve, dve_own)
                v = nc.vector
                v.memset(zsp[:, :], 0.0)
                v.memset(zrow[:, :], 0.0).then_inc(numbered, 1)
                v.memset(off[:, :], 0.0)
                dve.wait_ge(loaded, 48)
                ch.link(v.tensor_copy(dst_f[:, :], dst_i[:, :]))
                ch.link(v.tensor_copy(oth_f[:, :], prev_i[:, :]))
                ch.link(v.tensor_tensor(c.goes_on[:, :], dst_f[:, :], oth_f[:, :], ALU.is_equal))
                ch.link(v.tensor_scalar(c.pen_fwd[:, :], c.goes_on[:, :], 1.0, BIG, ALU.subtract, ALU.mult))
                ch.link(v.tensor_copy(oth_f[:, :], next_i[:, :]))
                ch.link(v.tensor_tensor(junk[:, :], dst_f[:, :], oth_f[:, :], ALU.is_equal))
                ch.link(v.tensor_scalar(c.pen_bwd[:, :], junk[:, :], 1.0, BIG, ALU.subtract, ALU.mult))
                ch.link(v.tensor_reduce(c.edge_pen[:, 0:1], c.goes_on[:, :], AX.X, ALU.min))
                ch.link(v.tensor_reduce(c.edge_pen[:, 1:2], c.pen_fwd[:, :], AX.X, ALU.min))
                ch.link(v.tensor_reduce(c.edge_pen[:, 2:3], c.pen_bwd[:, :], AX.X, ALU.min))
                for n in range(NT + 1):
                    ch.link(v.tensor_scalar(junk[:, :], dst_f[:, :], float(P * n), None, ALU.is_lt, ALU.add,
                                            accum_out=below[:, n:n + 1]))
                v.nop().then_inc(counted, 1)
                dve.wait_ge(summed, 1)
                ch.link(v.tensor_copy(bound_i[:, :], pcol[:, :]))
                ch.link(v.tensor_scalar(blk_i[:, 0:NT + 1], bound_i[:, :], 7, None, ALU.arith_shift_right))
                ch.link(v.tensor_copy(blk_f[:, 0:NT + 1], blk_i[:, 0:NT + 1]))
                ch.link(v.tensor_scalar(bound_i[:, :], bound_i[:, :], -1.0, None, ALU.add))
                ch.link(v.tensor_scalar(blk_i[:, NT + 1:], bound_i[:, :], 7, None, ALU.arith_shift_right))
                ch.link(v.tensor_copy(blk_f[:, NT + 1:], blk_i[:, NT + 1:]))
                ch.link(v.tensor_copy(below[:, :], pcol[:, :]))
                ch.link(v.tensor_tensor(has[:, :], below[:, 1:NT + 1], below[:, 0:NT], ALU.is_gt))
                ch.link(v.tensor_tensor(cnt[:, :], blk_f[:, NT + 2:], blk_f[:, 0:NT], ALU.subtract))
                ch.link(v.tensor_scalar(cnt[:, :], cnt[:, :], 1.0, None, ALU.add))
                ch.link(v.tensor_tensor(cnt[:, :], cnt[:, :], has[:, :], ALU.mult))
                ch.link(v.tensor_scalar(cnt[:, :], cnt[:, :], 1.0, float(QUAD - 1), ALU.max, ALU.add))
                ch.link(v.tensor_copy(cnt_i[:, :], cnt[:, :]))
                ch.link(v.tensor_scalar(cnt_i[:, :], cnt_i[:, :], 2, 2, ALU.arith_shift_right,
                                        ALU.logical_shift_left))
                ch.link(v.tensor_copy(cnt[:, :], cnt_i[:, :]))
                ch.link(v.memset(gs[:, :], 0.0))
                ch.link(v.tensor_tensor_scan(gs[:, 1:NT + 1], cnt[:, :], off[:, :], 0.0, ALU.add, ALU.add))
                ch.link(v.tensor_copy(c.first_step[:, :], gs[0:1, :]))
                ch.link(v.tensor_tensor(off[:, :], blk_f[:, 0:NT], gs[:, 0:NT], ALU.subtract))
                ch.link(v.tensor_copy(d_off[:, 0:1], off[:, 0:1]))
                ch.link(v.tensor_tensor(d_off[:, 1:NT], off[:, 1:NT], off[:, 0:NT - 1], ALU.subtract))
                dve.wait_ge(numbered, 3)
                ch.link(v.tensor_copy(gnum[:, :], gnum_i[:, :]))
                for k in range(GC):
                    g = gnum[:, k:k + 1]
                    ch.link(v.tensor_scalar(le[:, :], gs[:, 0:NT], g, None, ALU.is_le, ALU.add,
                                            accum_out=tn[:, k:k + 1]))
                    ch.link(v.tensor_tensor_reduce(le[:, :], le[:, :], d_off[:, :], 1.0, 0.0, ALU.mult,
                                                   ALU.add, te[:, k:k + 1]))
                ch.link(v.tensor_tensor(te[:, :], te[:, :], gnum[:, :], ALU.add))
                ch.link(v.tensor_scalar(te[:, :], te[:, :], float(EC), None, ALU.min))
                ch.link(v.tensor_scalar(tn[:, :], tn[:, :], 1.0, None, ALU.subtract))
                v.tensor_copy(c.te_i[:, :], te[:, :]).then_inc(chosen, 1)
                for k in range(GC):
                    v.tensor_scalar(sel[:, k, :], c.iota[:, 0:NT], tn[:, k:k + 1], None, ALU.is_equal)
                ch.link(v.tensor_scalar(tmp[:, :], tn[:, :], float(P), None, ALU.mult))
                dve.wait_ge(fetched, 3 * GC * 16)
                ch.link(v.tensor_copy(rows_s[:, :, :], rows_i[:, :, :]))
                ch.link(v.tensor_copy(rows_r[:, :, :], rows_d[:, :, :]))
                for k in range(GC):
                    ins = v.tensor_scalar(rows_r[:, k, :], rows_r[:, k, :], tmp[:, k:k + 1], None, ALU.subtract)
                ch.link(ins)
                v.nop().then_inc(laid, 1)
                for b in range(GC // 4):
                    s = slice(b * 4 * P, (b + 1) * 4 * P)
                    dve.wait_ge(turned, b + 1)
                    v.tensor_copy(c.idx[:, s], psum[:, 0, :, :].rearrange("p a b -> p (a b)"))
                    v.tensor_copy(c.drel[:, s], psum[:, 1, :, :].rearrange("p a b -> p (a b)"))
                    v.tensor_copy(c.ew[:, s], psum[:, 2, :, :].rearrange("p a b -> p (a b)")).then_inc(kept, 1)

            @block.tensor
            def _(pe):
                pe.wait_ge(counted, 1)
                nc.tensor.matmul(pcol[:, :], c.ones[:, :], below[:, :], start=True, stop=True).then_inc(summed, 1)
                pe.wait_ge(laid, 1)
                for b in range(GC // 4):
                    if b:
                        pe.wait_ge(kept, b)
                    for m, rows in enumerate((rows_s, rows_r, rows_w)):
                        for k in range(4):
                            ins = nc.tensor.transpose(psum[:, m, k, :], rows[:, 4 * b + k, :], c.ident[:, :])
                    ins.then_inc(turned, 1)

        step_cols = st.sb("step_cols", [P, GMAX])
        lt = [st.sb(f"lt{b}", [P, 8, P], BF16) for b in range(2)]
        ones_h = st.sb("ones_h", [P, 1], BF16)
        iota_h = st.sb("iota_h", [P, 1, P], BF16)
        drel_h = st.sb("drel_h", [P, GMAX, 1], BF16)
        inside = st.sb("inside", [P, GMAX], BF16)
        tcol = st.sb("tcol", [P, P + 1])
        at_f = st.sb("at_f", [P, 2, NT])
        pcnt = [st.ps(f"pcnt{b}", [P, 8]) for b in range(2)]
        pfirst = psum[:, 0:2, 0, 0:NT]
        pt = st.ps("pt", [P, P + 1])
        setup, compared, colsum = st.sem("setup"), st.sem("compared"), st.sem("colsum")
        moved, own2, tposed = st.sem("moved"), st.sem("own2"), st.sem("tposed")
        tkept, found = st.sem("tkept"), st.sem("found")
        passed = [st.sem(f"passed{j}") for j in range(3)]
        NGB = GMAX // 8
        with nc.Block() as block:
            @block.vector
            def _(dve):
                v = nc.vector
                ch = Chain(dve, own2)
                v.memset(ones_h[:, :], 1.0)
                v.tensor_copy(drel_h[:, :, 0], c.drel[:, :])
                v.tensor_scalar(inside[:, :], c.drel[:, :], float(P), None, ALU.is_lt).then_inc(setup, 1)
                ch.link(v.tensor_copy(iota_h[:, 0, :], c.iota[:, 0:P]))
                dve.wait_ge(setup, 1)
                with dve.Fori(0, NGB // 2) as i:
                    for b in range(2):
                        dve.wait_ge(colsum, i * 2 + (b + 1))
                        dve.sem_inc(passed[0], 1)
                        v.tensor_tensor(lt[b][:, :, :], iota_h[:, :, :].to_broadcast([P, 8, P]),
                                        drel_h[:, ds(i * 16 + b * 8, 8), :].to_broadcast([P, 8, P]), ALU.is_gt
                                        ).then_inc(compared, 1)
                for k in range(GC):
                    dve.wait_ge(tposed, k + 1)
                    if k:
                        dve.wait_ge(found, k)
                    v.tensor_copy(tcol[:, :], pt[:, :]).then_inc(tkept, 1)
                dve.wait_ge(found, GC)
                ch.link(v.tensor_copy(at_f[:, :, :], pfirst[:, :, :]))
                ch.link(v.tensor_tensor(at_f[:, 1, :], at_f[:, 1, :], at_f[:, 0, :], ALU.is_equal))
                ch.link(v.tensor_scalar(at_f[:, 1, :], at_f[:, 1, :], float(FAR), None, ALU.mult))
                ch.link(v.tensor_scalar(blk_f[:, 0:NT], blk_f[:, 0:NT], float(P), None, ALU.mult))
                ch.link(v.tensor_tensor(at_f[:, 0, :], at_f[:, 0, :], blk_f[:, 0:NT], ALU.add))
                ch.link(v.tensor_tensor(at_f[:, 0, :], at_f[:, 0, :], at_f[:, 1, :], ALU.add))
                ch.link(v.tensor_copy(c.first_edge[:, :], at_f[:, 0, :]))

            @block.scalar
            def _(act):
                act.sem_inc(moved, 2)
                with act.Fori(0, NGB // 2) as i:
                    for b in range(2):
                        act.wait_ge(colsum, i * 2 + (b + 3))
                        act.sem_inc(passed[1], 1)
                        nc.scalar.activation(step_cols[:, ds(i * 16 + b * 8, 8)], pcnt[b][:, :], ACT.Copy
                                             ).then_inc(moved, 1)

            @block.tensor
            def _(pe):
                pe.wait_ge(setup, 1)
                pe.sem_inc(colsum, 2)
                with pe.Fori(0, NGB // 2) as i:
                    for b in range(2):
                        pe.wait_ge(compared, i * 2 + (b + 1))
                        pe.wait_ge(moved, i * 2 + (b + 1))
                        pe.sem_inc(passed[2], 1)
                        for k in range(8):
                            ins = nc.tensor.matmul(pcnt[b][:, k:k + 1], lt[b][:, k, :], ones_h[:, :],
                                                   start=True, stop=True)
                        ins.then_inc(colsum, 1)
                pe.wait_ge(moved, NGB + 2)
                for k in range(GC):
                    if k:
                        pe.wait_ge(tkept, k)
                    nc.tensor.transpose(pt[:, 0:P], step_cols[:, k * P:(k + 1) * P], c.ident[:, :])
                    nc.tensor.matmul(pt[:, P:P + 1], inside[:, k * P:(k + 1) * P], ones_h[:, :],
                                     start=True, stop=True).then_inc(tposed, 1)
                    pe.wait_ge(tkept, k + 1)
                    for m in range(2):
                        ins = nc.tensor.matmul(pfirst[:, m, :], tcol[:, m:m + P], sel[:, k, :],
                                               start=(k == 0), stop=(k == GC - 1), skip_group_check=True)
                    ins.then_inc(found, 1)



def norm_stage(nc, kit, c, a, X, add, outs, want):
    project, turn = want == "project", want != "rows"
    with kit.stage() as st:
        sb, ps, sem = st.sb, st.ps, st.sem
        xin = sb("xin", [P, 2 * UT, D]) if add == "input" else None
        xs = sb("xs", [P, UT, D]) if turn else None
        stats = sb("stats", [P, UT, 6])
        mv = sb("mv", [P, UT, 2])
        rstd, std = sb("rstd", [P, UT, 1]), sb("std", [P, UT, 1])
        eps = sb("eps", [P, 1])
        varied = sem("varied")
        rooted = sem("rooted")
        pT = [ps(f"pT{k}", [P, 2, P]) for k in range(2)] if turn else None
        loaded = st.pool_sem("loaded")
        read = sem("read")
        own = sem("own")
        summed = sem("summed")
        normed = sem("normed")
        turned = sem("turned")
        kept = sem("kept")
        rowed = sem("rowed")
        stored = sem("stored")
        passed = [sem(f"passed{k}") for k in range(4)]
        if project:
            xt = sb("xt", [P, UT, 2, P])
            hs = sb("hs", [P, UT, D + 2 * H])
            pH = [ps(f"pH{k}", [P, D + 2 * H]) for k in range(2)]
            prod = sem("prod")
            hkept = sem("hkept")
            hstored = [sem(f"hstored{k}") for k in range(UT)]

        def ring2(k):
            return UT + max(k - 1, 0)

        with nc.Block() as block:
            if add == "input":
                @block.gpsimd
                def _(pool):
                    with pool.Fori(0, NB) as i:
                        pool.wait_ge(read, i + 1)
                        pool.sem_inc(passed[3], 1)
                        pool.dma_start(xin[:, ds((i & 1) * UT, UT), :], a["x"][ds(i * (UT * P), UT * P), :].rearrange(
                            "(k p) d -> p k d", p=P)).then_inc(loaded, 16)
                        pool.wait_ge(loaded, (i + 1) * 16)
                        pool.sem_inc(passed[3], 1)

            if want in ("rows", "both"):
                @block.sync
                def _(sp):
                    with sp.Fori(0, NB) as i:
                        if want == "rows":
                            sp.wait_ge(normed, (i + 1) * UT)
                        else:
                            sp.wait_ge(rowed, i + 2)
                        sp.dma_start(outs["rows"][ds(i * (UT * P), UT * P), :].rearrange("(k p) d -> p k d", p=P),
                                     outs["rows_sb"][:, ds(i * UT, UT), :]).then_inc(stored, 16)
                    sp.wait_ge(stored, 16 * NB)
            elif project:
                @block.sync
                def _(sp):
                    for k in range(UT):
                        sp.sem_inc(hstored[k], 32)
                    with sp.Fori(0, NB) as i:
                        for k in range(UT):
                            sp.wait_ge(hkept, i * UT + (k + 1 + UT))
                            r = ds((i * UT + k) * P, P)
                            sp.dma_start(outs["rows"][r, :], hs[:, k, 0:D]).then_inc(hstored[k], 16)
                            sp.dma_start(outs["logits"][r, :], hs[:, k, D:D + H]).then_inc(hstored[k], 16)
                    for k in range(UT):
                        sp.wait_ge(hstored[k], 32 * NB + 32)

            @block.vector
            def _(dve):
                v = nc.vector
                dve.sem_inc(read, 2)
                v.memset(eps[:, :], LN_EPS).then_inc(varied, 1)
                with dve.Fori(0, NB) as i:
                    o = i * 3
                    tiles = ds(i * UT, UT)
                    half = ds((i & 1) * UT, UT)
                    if add == "input":
                        dve.wait_ge(loaded, (i + 1) * 16)
                        dve.sem_inc(passed[0], 1)
                        if not project:
                            v.tensor_tensor(X[:, tiles, :], X[:, tiles, :], xin[:, half, :], ALU.add
                                            ).then_inc(summed, 1)
                    elif add == "scaled":
                        for k in range(UT):
                            t = ds(i * UT + k)
                            ins = v.scalar_tensor_tensor(out=X[:, t, :], in0=outs["adds"][:, t, :],
                                                         scalar=outs["scale"][:, t], in1=X[:, t, :],
                                                         op0=ALU.mult, op1=ALU.add)
                        ins.then_inc(summed, 1)
                    if not project and add != "none":
                        dve.wait_ge(summed, i + 1)
                        if add == "input":
                            dve.sem_inc(read, 1)
                        dve.sem_inc(passed[0], 1)

                    def tile(k):
                        return xin[:, ds((i & 1) * UT + k), :] if project else X[:, ds(i * UT + k), :]
                    for k in range(UT):
                        ins = v.bn_stats(stats[:, k, :], tile(k))
                    ins.then_inc(own, 1)
                    dve.wait_ge(own, o + 1)
                    dve.sem_inc(passed[0], 1)
                    for k in range(UT):
                        ins = v.bn_aggr(mv[:, k, :], stats[:, k, :])
                    ins.then_inc(own, 1)
                    dve.wait_ge(own, o + 2)
                    dve.sem_inc(passed[0], 1)
                    dve.sem_inc(varied, 1)
                    dve.wait_ge(rooted, i + 1)
                    v.reciprocal(rstd[:, :, :], std[:, :, :]).then_inc(own, 1)
                    dve.wait_ge(own, o + 3)
                    if want == "both":
                        dve.wait_ge(rowed, i + 1)
                    dve.sem_inc(passed[0], 1)
                    for k in range(UT):
                        if turn:
                            dve.wait_ge(turned, i * UT + (k + 1))
                            dve.sem_inc(passed[0], 1)
                        out = xs[:, k:k + 1, :] if turn else outs["rows_sb"][:, ds(i * UT + k), :]
                        v.tensor_scalar(out, tile(k), mv[:, k, 0:1], rstd[:, k, :],
                                        ALU.subtract, ALU.mult).then_inc(normed, 1)
                    dve.wait_ge(normed, (i + 1) * UT)
                    dve.sem_inc(read if project else passed[0], 1)

            @block.scalar
            def _(act):
                def root(i):
                    act.wait_ge(varied, i + 2)
                    nc.scalar.activation(std[:, :, :], mv[:, :, 1:2], ACT.Sqrt, bias=eps[:, :]).then_inc(rooted, 1)

                def part(i, steps):
                    for k in steps:
                        if want == "both" and k == 4:
                            act.wait_ge(normed, i * UT + UT)
                            act.sem_inc(passed[1], 1)
                            nc.scalar.activation(outs["rows_sb"][:, ds(i * UT, UT), :], xs[:, :, :], ACT.Copy
                                                 ).then_inc(rowed, 1)
                        if k < UT:
                            act.wait_ge(turned, i * UT + (k + 1 + UT))
                            if project:
                                act.wait_ge(prod, i * UT + (k + 1))
                            act.sem_inc(passed[1], 1)
                            to = xt[:, k, :, :] if project else outs["sbuf"][:, :, ds((i * UT + k) * P, P)]
                            nc.scalar.activation(to, pT[k % 2][:, :, :], ACT.Copy).then_inc(kept, 1)
                        if project and k:
                            m = k - 1
                            act.wait_ge(prod, i * UT + (m + 1 + UT))
                            act.wait_ge(hstored[m], i * 32 + 32)
                            act.sem_inc(passed[1], 1)
                            nc.scalar.activation(hs[:, m, :], pH[m % 2][:, :], ACT.Copy)
                            nc.scalar.activation(c.logit[:, ds(i * UT + m), :].rearrange("p o d -> p (o d)"),
                                                 pH[m % 2][:, D:D + 2 * H], ACT.Copy).then_inc(hkept, 1)

                early, late = (range(4), range(4, UT + project)) if turn else ((), ())
                if turn:
                    act.sem_inc(rowed, 1)
                    act.sem_inc(kept, UT)
                if project:
                    act.sem_inc(hkept, UT)
                root(0)
                part(0, early)
                with act.Fori(0, NB - 1) as i:
                    root(i + 1)
                    part(i, late)
                    part(i + 1, early)
                part(NB - 1, late)

            if turn:
                @block.tensor
                def _(pe):
                    pe.sem_inc(turned, UT)
                    if project:
                        pe.sem_inc(prod, UT)
                    with pe.Fori(0, NB) as i:
                        for k in range(UT + project):
                            if k < UT:
                                pe.wait_ge(normed, i * UT + (k + 1))
                                pe.wait_ge(kept, i * UT + ring2(k))
                                pe.sem_inc(passed[2], 1)
                                for h in range(2):
                                    ins = nc.tensor.transpose(pT[k % 2][:, h, :], xs[:, k, h * P:(h + 1) * P],
                                                              c.ident[:, :])
                                ins.then_inc(turned, 1)
                            if project and k:
                                m = k - 1
                                pe.wait_ge(kept, i * UT + (m + 1 + UT))
                                pe.wait_ge(hkept, i * UT + ring2(m))
                                pe.sem_inc(passed[2], 1)
                                for h in range(2):
                                    ins = nc.tensor.matmul(pH[m % 2][:, :], xt[:, m, h, :], c.wp[:, h, :],
                                                           start=(h == 0), stop=(h == 1))
                                ins.then_inc(prod, 1)


def attention_weights(nc, kit, c, a):
    L = len(c.wps)
    with kit.stage() as st:
        sb, ps, sem = st.sb, st.ps, st.sem
        avec = sb("avec", [P, L, 2, 2 * H])
        wt = [sb(f"wt{l}", [P, 2, D]) for l in range(L)]
        pw = [ps(f"pw{l}", [P, 2, 2, P]) for l in range(L)]
        pa = [ps(f"pa{l}", [P, 2, 2 * H]) for l in range(L)]
        loaded = [sem(f"loaded{l}") for l in range(L)]
        clear, turned, kept, prod, done = sem("clear"), sem("turned"), sem("kept"), sem("prod"), sem("done")
        with nc.Block() as block:
            def load(eng, l):
                eng.dma_start(c.wps[l][:, :, 0:D], a[f"L0_gnn_W{l}"].rearrange("(k p) n -> p k n", p=P)
                              ).then_inc(loaded[l], 16)
                eng.dma_start(c.gbiases[l][:, :], a[f"L0_gnn_b{l}"].rearrange("(a n) -> a n", a=1)
                              .to_broadcast([P, D])).then_inc(loaded[l], 16)
                eng.wait_ge(clear, 1)
                for j, s in enumerate((a[f"L0_gnn_as{l}"], a[f"L0_gnn_ad{l}"])):
                    for h in range(H):
                        r = h * HD % P
                        eng.dma_start(avec[r:r + HD, l, h * HD // P, j * H + h:j * H + h + 1],
                                      s[h, :].rearrange("(n a) -> n a", a=1)).then_inc(loaded[l], 16)

            @block.sync
            def _(sp):
                for l in range(0, L, 2):
                    load(sp, l)

            @block.scalar
            def _(act):
                for l in range(1, L, 2):
                    load(act, l)

            @block.vector
            def _(dve):
                nc.vector.memset(avec[:, :, :, :], 0.0).then_inc(clear, 1)
                for l in range(L):
                    dve.wait_ge(turned, l + 1)
                    nc.vector.tensor_copy(wt[l][:, :, :].rearrange("p a (b n) -> p a b n", b=2), pw[l][:, :, :, :]
                                          ).then_inc(kept, 1)
                for l in range(L):
                    dve.wait_ge(prod, l + 1)
                    nc.vector.tensor_copy(c.wps[l][:, :, D:D + 2 * H], pa[l][:, :, :]).then_inc(done, 1)

            @block.tensor
            def _(pe):
                for l in range(L):
                    pe.wait_ge(loaded[l], (2 + 2 * H) * 16)
                    for j in range(2):
                        for k in range(2):
                            ins = nc.tensor.transpose(pw[l][:, j, k, :], c.wps[l][:, k, j * P:(j + 1) * P],
                                                      c.ident[:, :])
                    ins.then_inc(turned, 1)
                for l in range(L):
                    pe.wait_ge(kept, l + 1)
                    for k in range(2):
                        for j in range(2):
                            ins = nc.tensor.matmul(pa[l][:, k, :], wt[l][:, j, k * P:(k + 1) * P], avec[:, l, j, :],
                                                   start=(j == 0), stop=(j == 1))
                    ins.then_inc(prod, 1)



def source_parts(nc, kit, c, a):
    with kit.stage() as st:
        src_i = st.sb("src_i", [P, EC], I32)
        part_i = st.sb("part_i", [P, 2, LOOK], I32)
        within = st.sb("within", [P, LOOK_C * P])
        pt = st.ps("pt", [P, LOOK_C, P])
        loaded, own, ready, turned = st.sem("loaded"), st.sem("own"), st.sem("ready"), st.sem("turned")
        with nc.Block() as block:
            @block.sync
            def _(sp):
                sp.dma_start(src_i[:, :], a["src"][0:EP].rearrange("(p j) -> p j", p=P)).then_inc(loaded, 16)

            @block.vector
            def _(dve):
                v = nc.vector
                ch = Chain(dve, own)
                ch.link(v.memset(within[:, :], 0.0))
                dve.wait_ge(loaded, 16)
                cols = src_i[:, EC - LOOK:EC]
                v.tensor_scalar(part_i[:, 0, :], cols, 7, None, ALU.arith_shift_right)
                ch.link(v.tensor_scalar(part_i[:, 1, :], cols, P - 1, None, ALU.bitwise_and))
                v.tensor_copy(c.src_tile[:, :], part_i[:, 0, :])
                v.tensor_copy(c.ident_h[:, :], c.ident[:, :])
                v.tensor_copy(within[:, 0:LOOK], part_i[:, 1, :]).then_inc(ready, 1)
                dve.wait_ge(turned, 1)
                ch.link(v.tensor_copy(c.src_within[:, :, :], pt[:, :, :]))

            @block.tensor
            def _(pe):
                pe.wait_ge(ready, 1)
                for k in range(LOOK_C):
                    ins = nc.tensor.transpose(pt[:, k, :], within[:, k * P:(k + 1) * P], c.ident[:, :])
                ins.then_inc(turned, 1)


def source_logits(nc, kit, c, a, e, ns, own8):
    FIRST = EC - LOOK
    HALF = 8
    with kit.stage() as st:
        sb, ps, sem = st.sb, st.ps, st.sem
        src_i = sb("src_i", [P, EC], I32)
        t4 = sb("t4", [P, NT, H])
        node_i, node_f = sb("node_i", [P, 1], I32), sb("node_f", [P, 1])
        full = sb("full", [P, H, NT])
        rest = sb("rest", [P, H, NT])
        parts = sb("parts", [P, 3, H, NT], BF16)
        hot = [sb(f"hot{h}", [P, HALF, P], BF16) for h in range(2)]
        tile_hot = sb("tile_hot", [P, HALF, NT])
        apart = sb("apart", [P, 2, 4, P])
        prod = [sb(f"prod{h}", [P, HALF, H, NT]) for h in range(2)]
        pb = [ps(f"pb{b}", [P, 4, P]) for b in range(2)]
        pl = [ps(f"pl{q}", [P, 2, H * NT]) for q in range(4)]
        gat, spread_done = st.pool_sem("gat"), st.pool_sem("spread_done")
        ld, own, self_done, re_read = sem("ld"), sem("own"), sem("self_done"), sem("re_read")
        numbered, split, negated = sem("numbered"), sem("split"), sem("negated")
        parted = sem("parted")
        spread = sem("spread")
        hot_made = sem("hot_made")
        looked = sem("looked")
        masked = sem("masked")
        picked = sem("picked")
        reduced = sem("reduced")
        passed = [sem(f"passed{k}") for k in range(3)]
        with nc.Block() as block:
            @block.sync
            def _(sp):
                sp.dma_start(src_i[:, :], a["src"][0:EP].rearrange("(p j) -> p j", p=P)).then_inc(ld, 16)
                sp.wait_ge(spread_done, 16 * NT)
                sp.dma_start(own8[:, :, :], c.spread.rearrange("(p j) c -> p j c", p=P)).then_inc(re_read, 16)
                sp.wait_ge(re_read, 16)

            @block.gpsimd
            def _(pool):
                nc.gpsimd.iota(node_i[:, :], pattern=[[0, 1]], base=0, channel_multiplier=1).then_inc(numbered, 1)
                pool.wait_ge(self_done, 1)
                for t in range(NT):
                    pool.indirect_dma_start(c.spread, bass.IndirectOffsetOnAxis(ap=c.first_edge[:, t:t + 1], axis=0),
                                            ns[:, t, :], None, bounds_check=EP - 1, oob_is_err=False
                                            ).then_inc(spread_done, 16)
                pool.wait_ge(ld, 16)
                for j in range(FIRST):
                    pool.indirect_dma_start(e[:, j, :], None, c.src_logit,
                                            bass.IndirectOffsetOnAxis(ap=src_i[:, j:j + 1], axis=0)
                                            ).then_inc(gat, 16)
                pool.wait_ge(gat, 16 * FIRST)

            @block.vector
            def _(dve):
                v = nc.vector
                ch = Chain(dve, own)
                ch.link(v.tensor_copy(ns[:, :, 0:H], c.logit[:, :, H:2 * H]))
                ch.link(v.tensor_tensor(t4[:, :, :], c.logit[:, :, 0:H], c.logit[:, :, H:2 * H], ALU.add))
                v.scalar_tensor_tensor(out=ns[:, :, H:2 * H], in0=t4[:, :, :], scalar=SLOPE, in1=t4[:, :, :],
                                       op0=ALU.mult, op1=ALU.max).then_inc(self_done, 1)
                dve.wait_ge(numbered, 1)
                v.tensor_scalar(node_f[:, :], node_i[:, :], -1.0, None, ALU.mult).then_inc(negated, 1)
                ch.link(v.tensor_copy(full[:, :, :], c.logit[:, :, 0:H].rearrange("p t h -> p h t")))
                for m in range(3):
                    left = full if m == 0 else rest
                    ch.link(v.tensor_copy(parts[:, m, :, :], left[:, :, :]))
                    if m < 2:
                        ch.link(v.tensor_tensor(rest[:, :, :], left[:, :, :], parts[:, m, :, :], ALU.subtract))
                v.nop().then_inc(split, 1)
                dve.sem_inc(picked, 4)
                dve.sem_inc(reduced, 2)

                with dve.Fori(0, LOOK // (2 * HALF)) as i:
                    for h in range(2):
                        turn = i * 2 + h
                        cols = ds(i * (2 * HALF) + h * HALF, HALF)
                        dve.wait_ge(picked, turn * 4 + 4)
                        dve.sem_inc(passed[0], 1)
                        v.tensor_tensor(tile_hot[:, :, :],
                                        c.iota[:, 0:NT].rearrange("p (o n) -> p o n", o=1).to_broadcast([P, HALF, NT]),
                                        c.src_tile[:, cols].rearrange("p (s o) -> p s o", o=1)
                                        .to_broadcast([P, HALF, NT]), ALU.is_equal).then_inc(masked, 1)
                        dve.wait_ge(masked, turn + 1)
                        dve.wait_ge(reduced, turn + 1)
                        for q in range(4):
                            dve.wait_ge(looked, turn * 4 + (q + 9))
                            dve.sem_inc(passed[0], 1)
                            m = tile_hot[:, 2 * q:2 * q + 2, :].rearrange("p s (o n) -> p s o n", o=1)
                            v.tensor_tensor(prod[h][:, 2 * q:2 * q + 2, :, :],
                                            pl[q][:, :, :].rearrange("p s (h n) -> p s h n", h=H),
                                            m.to_broadcast([P, 2, H, NT]), ALU.mult).then_inc(picked, 1)
                        dve.wait_ge(picked, turn * 4 + 8)
                        dve.sem_inc(passed[0], 1)
                        v.tensor_reduce(e[:, ds(i * (2 * HALF) + (h * HALF + FIRST), HALF), :], prod[h][:, :, :, :],
                                        AX.X, ALU.add).then_inc(reduced, 1)

            @block.scalar
            def _(act):
                act.sem_inc(hot_made, 2)
                act.wait_ge(negated, 1)

                def compare(turn, h):
                    for b in range(2):
                        act.wait_ge(spread, turn * 2 + (b + 1))
                        act.wait_ge(looked, turn * 4 + (2 * b + 2))
                        act.wait_ge(hot_made, turn * 2 + (b + 1))
                        act.sem_inc(passed[2], 1)
                        nc.scalar.activation(apart[:, b, :, :], pb[b][:, :, :], ACT.Abs, bias=node_f[:, :]
                                             ).then_inc(parted, 1)
                        act.wait_ge(parted, turn * 2 + (b + 1))
                        act.sem_inc(passed[2], 1)
                        nc.scalar.activation(hot[h][:, 4 * b:4 * b + 4, :], apart[:, b, :, :], ACT.Relu, bias=1.0,
                                             scale=-1.0).then_inc(hot_made, 1)

                with act.Fori(0, LOOK // (2 * HALF)) as i:
                    for h in range(2):
                        compare(i * 2 + h, h)

            @block.tensor
            def _(pe):
                pe.wait_ge(split, 1)
                pe.sem_inc(looked, 8)

                def spread_out(turn, chunk, col):
                    for b in range(2):
                        pe.wait_ge(hot_made, turn * 2 + (b + 1))
                        pe.sem_inc(passed[1], 1)
                        for k in range(4):
                            one = c.ident_h[:, col(4 * b + k)].to_broadcast([P, P])
                            ins = nc.tensor.matmul(pb[b][:, k, :], one, chunk, start=True, stop=True)
                        ins.then_inc(spread, 1)

                spread_out(0, c.src_within[:, 0, :], lambda k: slice(k, k + 1))
                with pe.Fori(0, LOOK // (2 * HALF)) as i:
                    for h in range(2):
                        turn = i * 2 + h
                        nxt = i * (2 * HALF) + (h + 1) * HALF
                        chunk = c.src_within[:, ds((nxt >> 7) & (LOOK_C - 1)), :].rearrange("p o n -> p (o n)")
                        spread_out(turn + 1, chunk, lambda k: ds((nxt & (P - HALF)) + k))
                        for q in range(4):
                            if q % 2 == 0:
                                pe.wait_ge(hot_made, turn * 2 + (q // 2 + 3))
                            pe.wait_ge(picked, turn * 4 + (q + 1))
                            pe.sem_inc(passed[1], 1)
                            for s in range(2):
                                for m in range(3):
                                    ins = nc.tensor.matmul(pl[q][:, s, :], hot[h][:, 2 * q + s, :],
                                                           parts[:, m, :, :].rearrange("p h n -> p (h n)"),
                                                           start=(m == 0), stop=(m == 2))
                            ins.then_inc(looked, 1)


def edge_softmax(nc, kit, c, a, layer):
    with kit.stage() as st:
        sb, ps, sem = st.sb, st.ps, st.sem
        e = sb("e", [P, EC, H])
        own8 = sb("own8", [P, EC, 2 * H])
        ns = sb("ns", [P, NT, 2 * H])
        source_logits(nc, kit, c, a, e, ns, own8)
        node = sb("node", [P, EC, 2 * H])
        mx = sb("mx", [P, EC, H])
        nmax = sb("nmax", [P, NT, H])
        ends = sb("ends", [P, 2 * H + 1])
        rows = sb("rows", [2 * H, 2, P + 2])
        carry = sb("carry", [P, 2 * H])
        prow = ps("prow", [2 * H, P])
        pflag = ps("pflag", [2 * H, P])
        pcar = ps("pcar", [P, 2 * H])
        pturn = [ps(f"pturn{k}", [P, 4, P]) for k in range(2)]
        prows = sb("prows", [P, GC, H * P])
        own = sem("own")
        ended, rowed, rkept, carried = sem("ended"), sem("rowed"), sem("rkept"), sem("carried")
        exped, wrote, maxed, mgot, wexp = sem("exped"), sem("wrote"), sem("maxed"), st.pool_sem("mgot"), sem("wexp")
        fetched, turned, kept = st.pool_sem("fetched"), sem("turned"), sem("kept")
        prefill = sem("prefill")
        raw1, raw2, wrote_max = sem("raw1"), sem("raw2"), sem("wrote_max")
        with nc.Block() as block:
            @block.sync
            def _(sp):
                sp.wait_ge(maxed, 1)
                sp.dma_start(c.emax.rearrange("(p j) c -> p j c", p=P), mx[:, :, :]).then_inc(wrote_max, 16)
                sp.wait_ge(exped, 1)
                sp.dma_start(c.pay[0:EC, :].rearrange("t (q h) -> (t q) h", h=H).rearrange(
                    "(p j) h -> p j h", p=P), e[:, :, :]).then_inc(wrote, 16)

            @block.gpsimd
            def _(pool):
                pool.wait_ge(wrote_max, 16)
                pool.wait_ge(prefill, 1)
                for t in range(NT):
                    pool.indirect_dma_start(nmax[:, t, :], None, c.emax,
                                            bass.IndirectOffsetOnAxis(ap=c.first_edge[:, t:t + 1], axis=0),
                                            bounds_check=EP - 1, oob_is_err=False).then_inc(mgot, 16)
                pool.wait_ge(wrote, 16)
                for k in range(GC):
                    pool.indirect_dma_start(prows[:, k, :], None, c.pay,
                                            bass.IndirectOffsetOnAxis(ap=c.te_i[:, k:k + 1], axis=0)
                                            ).then_inc(fetched, 16)

            @block.vector
            def _(dve):
                v = nc.vector
                ch = Chain(dve, own)
                v.tensor_copy(nmax[:, :, :], ns[:, :, H:2 * H]).then_inc(prefill, 1)

                def scan(out, flags, vals, ncol, op0, op1, init, back, flag_end, n):
                    s = slice(None, None, -1) if back else slice(None)
                    last = 0 if back else EC - 1
                    for h in range(ncol):
                        ins = v.tensor_tensor_scan(out[:, s, h], flags[:, s], vals[:, s, h], init, op0, op1)
                    ch.link(ins)
                    ch.link(v.tensor_copy(ends[:, 0:ncol], out[:, last, 0:ncol]))
                    ch.link(v.tensor_copy(carry[:, 0:ncol], flag_end.to_broadcast([P, ncol])))
                    v.nop().then_inc(ended, 1)
                    dve.wait_ge(rowed, n)
                    ch.link(v.memset(rows[:, 1, :], init))
                    ch.link(v.tensor_copy(rows[0:ncol, 0, 0:P], pflag[0:ncol, :]))
                    row_out = rows[0:ncol, 1, P - 1::-1] if back else rows[0:ncol, 1, 1:P + 1]
                    row_s = slice(None, None, -1) if back else slice(None)
                    if back:
                        ch.link(v.tensor_tensor_scan(rows[0:ncol, 1, P - 2::-1], rows[0:ncol, 0, P - 1:0:-1],
                                                     prow[0:ncol, P - 1:0:-1], init, op0, op1))
                    else:
                        ch.link(v.tensor_tensor_scan(rows[0:ncol, 1, 1:P], rows[0:ncol, 0, 0:P - 1],
                                                     prow[0:ncol, 0:P - 1], init, op0, op1))
                    v.nop().then_inc(rkept, 1)
                    dve.wait_ge(carried, n)
                    ch.link(v.tensor_copy(carry[:, 0:ncol], pcar[:, 0:ncol]))
                    for h in range(ncol):
                        ins = v.tensor_tensor_scan(out[:, s, h], flags[:, s], vals[:, s, h],
                                                   carry[:, h:h + 1], op0, op1)
                    ch.link(ins)

                ch.link(v.tensor_scalar(mx[:, :, 0], c.goes_on[:, :], -1.0, 1.0, ALU.mult, ALU.add))
                ch.link(v.tensor_tensor(own8[:, :, :], own8[:, :, :],
                                        mx[:, :, 0:1].to_broadcast([P, EC, 2 * H]), ALU.mult))
                scan(node, c.goes_on, own8, 2 * H, ALU.mult, ALU.add, 0.0, False, c.edge_pen[:, 0:1], 1)
                ch.link(v.tensor_tensor(e[:, :, :], e[:, :, :], node[:, :, 0:H], ALU.add))
                ch.link(v.scalar_tensor_tensor(out=e[:, :, :], in0=e[:, :, :], scalar=SLOPE, in1=e[:, :, :],
                                               op0=ALU.mult, op1=ALU.max))
                scan(own8, c.pen_fwd, e, H, ALU.add, ALU.max, -BIG, False, c.edge_pen[:, 1:2], 2)
                scan(mx, c.pen_bwd, own8, H, ALU.add, ALU.max, -BIG, True, c.edge_pen[:, 2:3], 3)
                ch.link(v.tensor_tensor(mx[:, :, :], mx[:, :, :], node[:, :, H:2 * H], ALU.max))
                v.nop().then_inc(maxed, 1)
                v.tensor_tensor(e[:, :, :], e[:, :, :], mx[:, :, :], ALU.subtract).then_inc(raw1, 1)
                dve.wait_ge(mgot, 16 * NT)
                v.tensor_tensor(nmax[:, :, :], ns[:, :, H:2 * H], nmax[:, :, :], ALU.subtract).then_inc(raw2, 1)
                for k in range(GC):
                    dve.wait_ge(turned, k + 1)
                    v.tensor_copy(c.paid[:, k * P:(k + 1) * P, :].rearrange("p g h -> p h g"), pturn[k % 2][:, :, :]
                                  ).then_inc(kept, 1)

            @block.scalar
            def _(act):
                act.wait_ge(raw1, 1)
                nc.scalar.activation(e[:, :, :], e[:, :, :], ACT.Exp).then_inc(exped, 1)
                act.wait_ge(raw2, 1)
                nc.scalar.activation(c.self_w[:, :, :], nmax[:, :, :], ACT.Exp).then_inc(wexp, 1)

            @block.tensor
            def _(pe):
                for n, ncol in ((1, 2 * H), (2, H), (3, H)):
                    pe.wait_ge(ended, n)
                    nc.tensor.transpose(prow[0:ncol, :], ends[:, 0:ncol], c.ident[:, :])
                    nc.tensor.transpose(pflag[0:ncol, :], carry[:, 0:ncol], c.ident[:, :]).then_inc(rowed, 1)
                    pe.wait_ge(rkept, n)
                    nc.tensor.transpose(pcar[:, 0:ncol], rows[0:ncol, 1, 0:P], c.ident[0:ncol, 0:ncol]
                                        ).then_inc(carried, 1)
                pe.wait_ge(fetched, 16 * GC)
                for k in range(GC):
                    if k >= 2:
                        pe.wait_ge(kept, k - 1)
                    for h in range(H):
                        ins = nc.tensor.transpose(pturn[k % 2][:, h, :], prows[:, k, h::H], c.ident[:, :])
                    ins.then_inc(turned, 1)


def edge_pass(nc, kit, c, table, att, accs):
    W = RW if att else D
    with kit.stage() as st:
        sb, ps, sem = st.sb, st.ps, st.sem
        rows = sb("rows", [P, RING, RW])
        hot = sb("hot", [P, QUAD, P])
        ix = sb("ix", [P, RING], I32)
        zero = sb("zero", [1, RW])
        acc = ps("acc", [P, 2, 512])
        landed = [st.pool_sem(f"landed{q}") for q in range(RING // QUAD)]
        index_put = sem("index_put")
        freed = sem("freed")
        hot_made = sem("hot_made")
        weighed = sem("weighed")
        cleared = sem("cleared")
        summed = sem("summed")
        kept = sem("kept")
        passed = [sem(f"passed{k}") for k in range(3)]
        PAIRS = RING // 2
        with nc.Block() as block:
            def bodies(eng):
                total = eng.value_load(c.first_step[0:1, NT:NT + 1], min_val=QUAD * NT, max_val=GMAX - RING)
                return eng.snap((total + (RING - 1)) >> (RING.bit_length() - 1))

            @block.gpsimd
            def _(pool):
                nb = bodies(pool)
                with pool.Fori(0, nb) as i:
                    for h in range(2):
                        pool.wait_ge(freed, i * PAIRS + (h + 1) * PAIRS // 2)
                        pool.sem_inc(passed[0], 1)
                        half = slice(h * RING // 2, (h + 1) * RING // 2)
                        nc.gpsimd.tensor_copy(ix[:, half], c.idx[:, ds(i * RING + h * RING // 2, RING // 2)]
                                              ).then_inc(index_put, 1)
                        pool.wait_ge(index_put, i * 2 + (h + 1))
                        pool.sem_inc(passed[0], 1)
                        for k in range(half.start, half.stop):
                            pool.indirect_dma_start(rows[:, k, 0:D], None, table,
                                                    bass.IndirectOffsetOnAxis(ap=ix[:, k:k + 1], axis=0)
                                                    ).then_inc(landed[k // QUAD], 16)

            @block.vector
            def _(dve):
                v = nc.vector
                v.memset(zero[:, :], 0.0).then_inc(cleared, 1)
                dve.sem_inc(hot_made, 2)
                nb = bodies(dve)
                with dve.Fori(0, nb) as i:
                    for q in range(RING // QUAD):
                        steps = slice(q * QUAD, (q + 1) * QUAD)
                        dve.wait_ge(landed[q], (i + 1) * 16 * QUAD)
                        dve.sem_inc(passed[1], 1)
                        cols = ds(i * RING + q * QUAD, QUAD)
                        if att:
                            r = rows[:, steps, 0:D].rearrange("p s (h f) -> p s h f", h=H)
                            w = c.paid[:, cols, :].rearrange("p s (h o) -> p s h o", o=1)
                            v.tensor_tensor(r, r, w.to_broadcast([P, QUAD, H, HD]), ALU.mult)
                            v.tensor_copy(rows[:, steps, D:RW], c.paid[:, cols, :]).then_inc(weighed, 1)
                        else:
                            r = rows[:, steps, 0:D]
                            w = c.ew[:, cols].rearrange("p (s o) -> p s o", o=1)
                            v.tensor_tensor(r, r, w.to_broadcast([P, QUAD, D]), ALU.mult).then_inc(weighed, 1)
                        for b in range(2):
                            dve.wait_ge(freed, i * PAIRS + (2 * q + b + PAIRS - 1))
                            dve.wait_ge(hot_made, i * PAIRS + (2 * q + b + 1))
                            dve.sem_inc(passed[1], 1)
                            d = c.drel[:, ds(i * RING + q * QUAD + 2 * b, 2)].rearrange("p (s o) -> p s o", o=1)
                            v.tensor_tensor(hot[:, 2 * b:2 * b + 2, :],
                                            c.iota[:, 0:P].rearrange("p (o n) -> p o n", o=1).to_broadcast([P, 2, P]),
                                            d.to_broadcast([P, 2, P]), ALU.is_equal).then_inc(hot_made, 1)

            @block.tensor
            def _(pe):
                pe.sem_inc(freed, PAIRS)
                pe.wait_ge(cleared, 1)
                with pe.Fori(0, NT) as n:
                    g0 = pe.value_load(c.first_step[0:1, ds(n)], min_val=0, max_val=GMAX - RING)
                    g1 = pe.value_load(c.first_step[0:1, ds(n + 1)], min_val=0, max_val=GMAX - RING)
                    pe.wait_ge(kept, n + 1)
                    pe.sem_inc(passed[2], 1)
                    A = acc[:, ds(n & 1), 0:W].rearrange("p o d -> p (o d)")
                    nc.tensor.matmul(A, zero[0:1, 0:P], zero[0:1, 0:W], start=True, stop=False,
                                     skip_group_check=True)
                    with pe.Fori(g0, g1, QUAD) as g:
                        for b in range(QUAD):
                            if b % 2 == 0:
                                pe.wait_ge(hot_made, (g >> 1) + (b // 2 + 3))
                            row = rows[:, ds((g & (RING - QUAD)) + b), 0:W].rearrange("p o d -> p (o d)")
                            ins = nc.tensor.matmul(A, hot[:, b, :], row, start=False, stop=False,
                                                   skip_group_check=True)
                            if b % 2:
                                ins.then_inc(freed, 1)
                    nc.tensor.matmul(A, zero[0:1, 0:P], zero[0:1, 0:W], start=False, stop=True,
                                     skip_group_check=True).then_inc(summed, 1)
                pe.wait_ge(summed, NT)
                pe.sem_inc(freed, PAIRS)

            @block.scalar
            def _(act):
                act.sem_inc(kept, 2)
                with act.Fori(0, NT) as n:
                    act.wait_ge(summed, n + 1)
                    nc.scalar.activation(accs[:, ds(n), 0:W], acc[:, ds(n & 1), 0:W], ACT.Copy).then_inc(kept, 1)


def attention_end(nc, kit, c, table, accs, outs):
    project = "sbuf" not in outs
    with kit.stage() as st:
        sb, ps, sem = st.sb, st.ps, st.sem
        own_row = sb("own_row", [P, UT, D])
        rden = sb("rden", [P, NT, H])
        fin = sb("fin", [P, UT, D])
        xt = sb("xt", [P, UT, 2, P])
        hs = sb("hs", [P, UT, D + 2 * H])
        pT = [ps(f"pT{k}", [P, 2, P]) for k in range(2)]
        pH = [ps(f"pH{k}", [P, D + 2 * H]) for k in range(2)]
        loaded = st.pool_sem("loaded")
        stored = [sem(f"stored{k}") for k in range(UT)]
        own, read, fin_made, turned = sem("own"), sem("read"), sem("fin_made"), sem("turned")
        kept, prod, hkept = sem("kept"), sem("prod"), sem("hkept")
        passed = [sem(f"passed{k}") for k in range(4)]

        def ring2(k):
            return UT + max(k - 1, 0)

        with nc.Block() as block:
            @block.gpsimd
            def _(pool):
                with pool.Fori(0, NB) as i:
                    pool.wait_ge(read, i + 1)
                    pool.sem_inc(passed[3], 1)
                    pool.dma_start(own_row[:, :, :], table[ds(i * (UT * P), UT * P), :].rearrange(
                        "(k p) d -> p k d", p=P)).then_inc(loaded, 16)

            @block.vector
            def _(dve):
                v = nc.vector
                dve.sem_inc(read, 1)
                v.tensor_tensor(rden[:, :, :], accs[:, :, D:RW], c.self_w[:, :, :], ALU.add).then_inc(own, 1)
                dve.wait_ge(own, 1)
                v.tensor_scalar(rden[:, :, :], rden[:, :, :], 1e-16, None, ALU.add).then_inc(own, 1)
                dve.wait_ge(own, 2)
                v.reciprocal(rden[:, :, :], rden[:, :, :]).then_inc(own, 1)
                dve.wait_ge(own, 3)
                with dve.Fori(0, NB) as i:
                    o = i * 3 + 3
                    tiles = ds(i * UT, UT)
                    by_head = lambda ap: ap.rearrange("p t (h f) -> p t h f", h=H)
                    wide = lambda ap: ap.rearrange("p t (h e) -> p t h e", e=1).to_broadcast([P, UT, H, HD])
                    sums = accs[:, tiles, 0:D]
                    dve.wait_ge(loaded, (i + 1) * 16)
                    dve.sem_inc(passed[0], 1)
                    v.tensor_tensor(by_head(own_row[:, :, :]), by_head(own_row[:, :, :]), wide(c.self_w[:, tiles, :]),
                                    ALU.mult).then_inc(own, 1)
                    dve.wait_ge(own, o + 1)
                    dve.sem_inc(passed[0], 1)
                    v.tensor_tensor(sums, sums, own_row[:, :, :], ALU.add).then_inc(own, 1)
                    dve.wait_ge(own, o + 2)
                    dve.sem_inc(read, 1)
                    v.tensor_tensor(by_head(sums), by_head(sums), wide(rden[:, tiles, :]), ALU.mult).then_inc(own, 1)
                    dve.wait_ge(own, o + 3)
                    dve.sem_inc(passed[0], 1)
                    for k in range(UT):
                        t = ds(i * UT + k)
                        bias = c.gbias[:, :].rearrange("p (o d) -> p o d", o=1)
                        if project:
                            dve.wait_ge(turned, i * UT + (k + 1))
                            dve.sem_inc(passed[0], 1)
                            v.tensor_tensor(fin[:, k:k + 1, :], accs[:, t, 0:D], bias, ALU.add).then_inc(fin_made, 1)
                        else:
                            v.tensor_tensor(outs["sbuf"][:, t, :], accs[:, t, 0:D], bias, ALU.add).then_inc(fin_made, 1)

            if project:
                @block.tensor
                def _(pe):
                    pe.sem_inc(turned, UT)
                    pe.sem_inc(prod, UT)
                    with pe.Fori(0, NB) as i:
                        for k in range(UT + 1):
                            if k < UT:
                                pe.wait_ge(fin_made, i * UT + (k + 1))
                                pe.wait_ge(kept, i * UT + ring2(k))
                                pe.sem_inc(passed[1], 1)
                                for f in range(2):
                                    ins = nc.tensor.transpose(pT[k % 2][:, f, :], fin[:, k, f * P:(f + 1) * P],
                                                              c.ident[:, :])
                                ins.then_inc(turned, 1)
                            if k:
                                m = k - 1
                                pe.wait_ge(kept, i * UT + (m + 1 + UT))
                                pe.wait_ge(hkept, i * UT + ring2(m))
                                pe.sem_inc(passed[1], 1)
                                for f in range(2):
                                    ins = nc.tensor.matmul(pH[m % 2][:, :], xt[:, m, f, :], c.wp[:, f, :],
                                                           start=(f == 0), stop=(f == 1))
                                ins.then_inc(prod, 1)

                @block.scalar
                def _(act):
                    act.sem_inc(kept, UT)
                    act.sem_inc(hkept, UT)
                    with act.Fori(0, NB) as i:
                        for k in range(UT + 1):
                            if k < UT:
                                act.wait_ge(turned, i * UT + (k + 1 + UT))
                                act.wait_ge(prod, i * UT + (k + 1))
                                act.sem_inc(passed[2], 1)
                                nc.scalar.activation(xt[:, k, :, :], pT[k % 2][:, :, :], ACT.Copy).then_inc(kept, 1)
                            if k:
                                m = k - 1
                                act.wait_ge(prod, i * UT + (m + 1 + UT))
                                act.wait_ge(stored[m], i * 32 + 32)
                                act.sem_inc(passed[2], 1)
                                nc.scalar.activation(hs[:, m, :], pH[m % 2][:, :], ACT.Copy)
                                nc.scalar.activation(c.logit[:, ds(i * UT + m), :].rearrange("p o d -> p (o d)"),
                                                     pH[m % 2][:, D:D + 2 * H], ACT.Copy).then_inc(hkept, 1)

                @block.sync
                def _(sp):
                    for k in range(UT):
                        sp.sem_inc(stored[k], 32)
                    with sp.Fori(0, NB) as i:
                        for k in range(UT):
                            sp.wait_ge(hkept, i * UT + (k + 1 + UT))
                            r = ds((i * UT + k) * P, P)
                            sp.dma_start(outs["rows"][r, :], hs[:, k, 0:D]).then_inc(stored[k], 16)
                            sp.dma_start(outs["logits"][r, :], hs[:, k, D:D + H]).then_inc(stored[k], 16)
                    for k in range(UT):
                        sp.wait_ge(stored[k], 32 * NB + 32)


def mix_end(nc, kit, c, acc, outs):
    with kit.stage() as st:
        sb, ps, sem = st.sb, st.ps, st.sem
        fin = sb("fin", [P, UT, 2 * D])
        xt = sb("xt", [P, UT, 4, P])
        ys = sb("ys", [P, 2, D])
        pT = [ps(f"pT{k}", [P, 4, P]) for k in range(2)]
        pH = [ps(f"pH{k}", [P, D]) for k in range(2)]
        junk = sb("junk", [P, D])
        own, fin_made, turned, kept = sem("own"), sem("fin_made"), sem("turned"), sem("kept")
        prod, hkept, made, put = sem("prod"), sem("hkept"), sem("made"), sem("put")
        passed = [sem(f"passed{k}") for k in range(3)]

        def ring2(k):
            return UT + max(k - 1, 0)

        with nc.Block() as block:
            @block.vector
            def _(dve):
                v = nc.vector
                dve.sem_inc(hkept, UT)
                dve.sem_inc(made, UT)
                with dve.Fori(0, NB) as i:
                    for k in range(UT + 2):
                        if k < UT:
                            t = ds(i * UT + k)
                            emb = outs["sbuf"][:, t, :]
                            dve.wait_ge(turned, i * UT + (k + 1))
                            dve.sem_inc(passed[0], 1)
                            v.tensor_copy(fin[:, k:k + 1, 0:D], emb)
                            v.tensor_tensor(fin[:, k:k + 1, D:2 * D], acc(t), emb, ALU.mult).then_inc(own, 1)
                            dve.wait_ge(own, i * (2 * UT) + (2 * k + 1))
                            dve.sem_inc(passed[0], 1)
                            v.tensor_tensor(fin[:, k:k + 1, D:2 * D], fin[:, k:k + 1, D:2 * D], acc(t), ALU.add
                                            ).then_inc(own, 1)
                            dve.wait_ge(own, i * (2 * UT) + (2 * k + 2))
                            dve.sem_inc(fin_made, 1)
                        if k > 1:
                            m = k - 2
                            dve.wait_ge(prod, i * UT + (m + 1))
                            dve.wait_ge(put, i * UT + ring2(m))
                            dve.sem_inc(passed[0], 1)
                            y = ys[:, m % 2, :]
                            v.tensor_tensor(junk[:, :], pH[m % 2][:, :], c.gbias[:, :], ALU.add).then_inc(hkept, 1)
                            dve.wait_ge(hkept, i * UT + (m + 1 + UT))
                            dve.sem_inc(passed[0], 1)
                            v.scalar_tensor_tensor(out=y, in0=junk[:, :], scalar=SLOPE, in1=junk[:, :],
                                                   op0=ALU.mult, op1=ALU.max).then_inc(made, 1)
                            dve.wait_ge(made, i * UT + (m + 1 + UT))
                            dve.sem_inc(passed[0], 1)

            @block.tensor
            def _(pe):
                pe.sem_inc(turned, UT)
                with pe.Fori(0, NB) as i:
                    for k in range(UT + 1):
                        if k < UT:
                            pe.wait_ge(fin_made, i * UT + (k + 1))
                            pe.wait_ge(kept, i * UT + ring2(k))
                            pe.sem_inc(passed[1], 1)
                            for f in range(4):
                                ins = nc.tensor.transpose(pT[k % 2][:, f, :], fin[:, k, f * P:(f + 1) * P],
                                                          c.ident[:, :])
                            ins.then_inc(turned, 1)
                        if k:
                            m = k - 1
                            pe.wait_ge(kept, i * UT + (m + 1 + UT))
                            pe.wait_ge(hkept, i * UT + ring2(m))
                            pe.sem_inc(passed[1], 1)
                            for f in range(4):
                                ins = nc.tensor.matmul(pH[m % 2][:, :], xt[:, m, f, :], outs["w"][:, f, :],
                                                       start=(f == 0), stop=(f == 3))
                            ins.then_inc(prod, 1)

            @block.scalar
            def _(act):
                act.sem_inc(kept, UT)
                act.sem_inc(put, UT)
                with act.Fori(0, NB) as i:
                    for k in range(UT + 2):
                        if k < UT:
                            act.wait_ge(turned, i * UT + (k + 1 + UT))
                            act.sem_inc(passed[2], 1)
                            nc.scalar.activation(xt[:, k, :, :], pT[k % 2][:, :, :], ACT.Copy).then_inc(kept, 1)
                        if k > 1:
                            m = k - 2
                            t = ds(i * UT + m)
                            act.wait_ge(made, i * UT + (m + 1 + UT))
                            act.sem_inc(passed[2], 1)
                            nc.scalar.activation(outs["sbuf"][:, t, :].rearrange("p o d -> p (o d)"),
                                                 ys[:, m % 2, :], ACT.Copy).then_inc(put, 1)

        summed = st.sem("summed")
        squares = st.sb("squares", [P, UT, D])
        squared = st.sem("squared")
        with nc.Block() as block:
            @block.scalar
            def _(act):
                act.sem_inc(summed, 1)
                with act.Fori(0, NB) as i:
                    act.wait_ge(summed, i + 1)
                    act.sem_inc(passed[2], 1)
                    nc.scalar.activation(squares[:, :, :], outs["sbuf"][:, ds(i * UT, UT), :], ACT.Square
                                         ).then_inc(squared, 1)

            @block.vector
            def _(dve):
                with dve.Fori(0, NB) as i:
                    dve.wait_ge(squared, i + 1)
                    dve.sem_inc(passed[0], 1)
                    nc.vector.tensor_reduce(outs["sumsq"][:, ds(i * UT, UT)], squares[:, :, :], AX.X, ALU.add
                                            ).then_inc(summed, 1)



def router(nc, kit, c, xT, wr, E, gbias, at_f, w1, w2, gate):
    with kit.stage() as st:
        sb, ps, sem = st.sb, st.ps, st.sem
        lt = sb("lt", [E, UT * P])
        logits = sb("logits", [P, NT, 8])
        best = sb("best", [P, NT, 8])
        at = sb("at", [P, NT, 8], U32)
        ex = sb("ex", [P, NT, 8])
        z = sb("z", [P, NT, 1])
        dd = sb("dd", [P, NT, 1])
        hit = sb("hit", [P, NT, 8])
        pL = [ps(f"pL{k}", [E, CH]) for k in range(2)]
        pG = ps("pG", [P, UT, E])
        prod, kept, turned, put, own = sem("prod"), sem("kept"), sem("turned"), sem("put"), sem("own")
        asked, given, passed = sem("asked"), sem("given"), sem("passed")
        with nc.Block() as block:
            @block.tensor
            def _(pe):
                with pe.Fori(0, NB) as i:
                    pe.wait_ge(kept, i + 1)
                    for m in range(2):
                        for k in range(2):
                            ins = nc.tensor.matmul(pL[m][:, :], wr[:, k, :], xT[:, k, ds(i * UT * P + m * CH, CH)],
                                                   start=(k == 0), stop=(k == 1))
                    ins.then_inc(prod, 1)
                    pe.wait_ge(kept, i + 2)
                    pe.wait_ge(put, i + 1)
                    pe.sem_inc(passed, 1)
                    for k in range(UT):
                        ins = nc.tensor.transpose(pG[:, k, :], lt[:, k * P:(k + 1) * P], c.ident[0:E, 0:E])
                    ins.then_inc(turned, 1)

            @block.vector
            def _(dve):
                v = nc.vector
                v.memset(logits[:, :, :], -BIG).then_inc(own, 1)
                dve.wait_ge(own, 1)
                for s in (kept, put, turned):
                    dve.sem_inc(s, 1)
                with dve.Fori(0, NB) as i:
                    dve.wait_ge(prod, i + 1)
                    dve.wait_ge(turned, i + 1)
                    for m in range(2):
                        to = lt[:, m * CH:(m + 1) * CH]
                        if gbias is None:
                            ins = v.tensor_copy(to, pL[m][:, :])
                        else:
                            ins = v.tensor_scalar(to, pL[m][:, :], gbias[:, :], None, ALU.add)
                    ins.then_inc(kept, 1)
                    dve.wait_ge(turned, i + 2)
                    v.tensor_copy(logits[:, ds(i * UT, UT), 0:E], pG[:, :, :]).then_inc(put, 1)
                ch = Chain(dve, own)
                ch.n = 1
                dve.wait_ge(put, NB + 1)
                for t in range(NT):
                    ins = v.max(best[:, t, :], logits[:, t, :])
                ch.link(ins)
                for t in range(NT):
                    ins = v.max_index(at[:, t, :], best[:, t, :], logits[:, t, :])
                ch.link(ins)
                ch.link(v.tensor_copy(at_f[:, :, :], at[:, :, 0:2]))
                v.tensor_tensor(ex[:, :, :], logits[:, :, :], best[:, :, 0:1].to_broadcast([P, NT, 8]),
                                ALU.subtract).then_inc(asked, 1)
                dve.wait_ge(given, 1)
                ch.link(v.tensor_reduce(z[:, :, 0], ex[:, :, :], AX.X, ALU.add))
                ch.link(v.reciprocal(z[:, :, :], z[:, :, :]))
                ch.link(v.tensor_tensor(dd[:, :, :], best[:, :, 1:2], best[:, :, 0:1], ALU.subtract))
                v.nop().then_inc(asked, 1)
                dve.wait_ge(given, 2)
                ch.link(v.tensor_tensor(w2[:, :, :], dd[:, :, :], z[:, :, :], ALU.mult))
                ch.link(v.tensor_copy(w1[:, :, :], z[:, :, :]))
                if gbias is not None:
                    v.tensor_tensor(w2[:, :, :], w2[:, :, :], w1[:, :, :], ALU.subtract).then_inc(asked, 1)
                    dve.wait_ge(given, 3)
                    ch.link(v.memset(w1[:, :, :], 1.0))
                ch.link(v.tensor_tensor(z[:, :, :], w1[:, :, :], w2[:, :, :], ALU.add))
                ch.link(v.reciprocal(z[:, :, :], z[:, :, :]))
                ch.link(v.tensor_tensor(w1[:, :, :], w1[:, :, :], z[:, :, :], ALU.mult))
                ch.link(v.tensor_tensor(w2[:, :, :], w2[:, :, :], z[:, :, :], ALU.mult))
                if gate is None:
                    return
                iota = c.iota[:, 0:E].rearrange("p (o e) -> p o e", o=1).to_broadcast([P, NT, E])
                h = hit[:, :, 0:E]
                ch.link(v.tensor_tensor(h, iota, at_f[:, :, 0:1].to_broadcast([P, NT, E]), ALU.is_equal))
                ch.link(v.tensor_tensor(gate[:, :, :], h, w1[:, :, :].to_broadcast([P, NT, E]), ALU.mult))
                ch.link(v.tensor_tensor(h, iota, at_f[:, :, 1:2].to_broadcast([P, NT, E]), ALU.is_equal))
                ch.link(v.tensor_tensor(h, h, w2[:, :, :].to_broadcast([P, NT, E]), ALU.mult))
                ch.link(v.tensor_tensor(gate[:, :, :], gate[:, :, :], h, ALU.add))

            @block.scalar
            def _(act):
                act.wait_ge(asked, 1)
                nc.scalar.activation(ex[:, :, :], ex[:, :, :], ACT.Exp).then_inc(given, 1)
                act.wait_ge(asked, 2)
                nc.scalar.activation(dd[:, :, :], dd[:, :, :], ACT.Exp).then_inc(given, 1)
                if gbias is not None:
                    act.wait_ge(asked, 3)
                    nc.scalar.activation(w2[:, :, :], w2[:, :, :], ACT.Exp).then_inc(given, 1)


def assign_slots(nc, kit, c, pick, slot_i, group_i):
    with kit.stage() as st:
        sb, ps, sem = st.sb, st.ps, st.sem
        row_i, row = sb("row_i", [P, 1], I32), sb("row", [P, 1])
        before = sb("before", [P, P])
        one = sb("one", [P, NT])
        hit = [sb(f"hit{j}", [P, NT, E0]) for j in range(2)]
        both = sb("both", [P, NT, E0])
        rank = sb("rank", [P, NT, E0])
        tot = sb("tot", [P, E0])
        ng_i, ng = sb("ng_i", [P, E0], I32), sb("ng", [P, E0])
        zero = sb("zero", [P, E0])
        first = sb("first", [P, E0 + 2])
        base = sb("base", [P, 1, E0])
        slot = sb("slot", [P, NT, 2])
        pre = ps("pre", [P, E0])
        cnt = ps("cnt", [P, E0])
        numbered, own, ready, summed = sem("numbered"), sem("own"), sem("ready"), sem("summed")
        with nc.Block() as block:
            @block.gpsimd
            def _(pool):
                nc.gpsimd.iota(row_i[:, :], pattern=[[0, 1]], base=0, channel_multiplier=1).then_inc(numbered, 1)

            @block.tensor
            def _(pe):
                pe.wait_ge(ready, 1)
                nc.tensor.matmul(pre[:, :], before[:, :], tot[:, :], start=True, stop=True)
                nc.tensor.matmul(cnt[:, :], c.ones[:, :], tot[:, :], start=True, stop=True).then_inc(summed, 1)

            @block.vector
            def _(dve):
                v = nc.vector
                ch = Chain(dve, own)
                iota = c.iota[:, 0:E0].rearrange("p (o e) -> p o e", o=1).to_broadcast([P, NT, E0])
                v.memset(one[:, :], 1.0)
                v.memset(zero[:, :], 0.0)
                v.memset(first[:, 0:1], 0.0)
                v.memset(first[:, 1:2], float(SHG))
                for j in range(2):
                    ch.link(v.tensor_tensor(hit[j][:, :, :], iota, pick[:, :, j:j + 1].to_broadcast([P, NT, E0]),
                                            ALU.is_equal))
                ch.link(v.tensor_tensor(both[:, :, :], hit[0][:, :, :], hit[1][:, :, :], ALU.add))
                for e in range(E0):
                    ins = v.tensor_tensor_scan(rank[:, :, e], one[:, :], both[:, :, e], 0.0, ALU.mult, ALU.add)
                ch.link(ins)
                ch.link(v.tensor_copy(tot[:, :], rank[:, NT - 1, :]))
                dve.wait_ge(numbered, 1)
                ch.link(v.tensor_copy(row[:, :], row_i[:, :]))
                v.tensor_scalar(before[:, :], c.iota[:, 0:P], row[:, :], None, ALU.is_gt).then_inc(ready, 1)
                dve.wait_ge(summed, 1)
                ch.link(v.tensor_scalar(ng[:, :], cnt[:, :], float(GS - 1), None, ALU.add))
                ch.link(v.tensor_copy(ng_i[:, :], ng[:, :]))
                ch.link(v.tensor_scalar(ng_i[:, :], ng_i[:, :], 8, None, ALU.arith_shift_right))
                ch.link(v.tensor_copy(ng[:, :], ng_i[:, :]))
                ch.link(v.tensor_scalar(ng[:, :], ng[:, :], 1.0, None, ALU.max))
                ch.link(v.tensor_tensor_scan(first[:, 2:], ng[:, :], zero[:, :], float(SHG), ALU.add, ALU.add))
                ch.link(v.tensor_copy(group_i[:, :], first[0:1, :]))
                ch.link(v.tensor_scalar(base[:, 0, :], first[:, 1:E0 + 1], float(GS), -1.0, ALU.mult, ALU.add))
                ch.link(v.tensor_tensor(base[:, 0, :], base[:, 0, :], pre[:, :], ALU.add))
                ch.link(v.tensor_tensor(rank[:, :, :], rank[:, :, :], base[:, :, :].to_broadcast([P, NT, E0]), ALU.add))
                for j in range(2):
                    ch.link(v.tensor_tensor(hit[j][:, :, :], hit[j][:, :, :], rank[:, :, :], ALU.mult))
                    ch.link(v.tensor_reduce(slot[:, :, j], hit[j][:, :, :], AX.X, ALU.add))
                ch.link(v.tensor_copy(slot_i[:, :, :], slot[:, :, :]))


def experts_gelu(nc, kit, c, a, rows, slot_i, group_i, slots_in, slots_out, hT):
    with kit.stage() as st:
        sb, ps, sem = st.sb, st.ps, st.sem
        w1 = [sb(f"w1{b}", [P, 2, F0]) for b in range(2)]
        w2 = [sb(f"w2{b}", [P, FT0, D]) for b in range(2)]
        b1 = [sb(f"b1{b}", [P, FT0]) for b in range(2)]
        b2 = [sb(f"b2{b}", [P, D]) for b in range(2)]
        xg = sb("xg", [P, 2, D])
        xt = sb("xt", [P, 2, GS])
        ys = sb("ys", [P, 2, D])
        pT = ps("pT", [P, 2, GS])
        p1 = [ps(f"p1{k}", [P, GS]) for k in range(4)]
        p2 = [ps(f"p2{k}", [P, D]) for k in range(2)]
        w_loaded = [st.pool_sem(f"w_loaded{b}") for b in range(2)]
        put = st.pool_sem("put")
        got = sem("got")
        turned = sem("turned")
        xt_put = sem("xt_put")
        up = sem("up")
        bent = sem("bent")
        down = sem("down")
        made = sem("made")
        stored = sem("stored")
        done = sem("done")
        passed = [sem(f"passed{k}") for k in range(5)]

        def experts(eng, body):
            body((0, SHG), 0, 1)
            with eng.Fori(0, E0 // 2) as i:
                body([eng.value_load(group_i[0:1, ds(i * 2 + (1 + j))], min_val=SHG, max_val=MAXG)
                      for j in range(2)], 1, i + 1)
                body([eng.value_load(group_i[0:1, ds(i * 2 + (2 + j))], min_val=SHG, max_val=MAXG)
                      for j in range(2)], 0, i + 2)

        def load_weights(pool, e, b):
            for to, fr in ((w1[b][:, :, :], a["W1all"][e, :, :].rearrange("o (k p) f -> p (o k) f", p=P)),
                           (w2[b][:, :, :], a["W2all"][e, :, :].rearrange("o (f p) d -> p (o f) d", p=P)),
                           (b1[b][:, :], a["b1all"][e, :, :].rearrange("o p f -> p (o f)")),
                           (b2[b][:, :], a["b2all"][e, :].to_broadcast([P, D]))):
                pool.dma_start(to, fr).then_inc(w_loaded[b], 16)

        with nc.Block() as block:
            @block.gpsimd
            def _(pool):
                load_weights(pool, slice(0, 1), 0)
                load_weights(pool, slice(1, 2), 1)
                for t in range(NT):
                    for j in range(2):
                        pool.indirect_dma_start(slots_in, bass.IndirectOffsetOnAxis(ap=slot_i[:, t, j:j + 1], axis=0),
                                                rows[:, t, :], None).then_inc(put, 16)
                with pool.Fori(0, E0 // 2 - 1) as i:
                    for b in range(2):
                        pool.wait_ge(done, i * 2 + (b + 1))
                        pool.sem_inc(passed[0], 1)
                        load_weights(pool, ds(i * 2 + (2 + b)), b)
                pool.wait_ge(done, E0 - 1)
                load_weights(pool, slice(E0, E0 + 1), 0)

            @block.sync
            def _(sp):
                def load(g):
                    sp.wait_ge(turned, g + 1)
                    sp.dma_start(xg[:, :, :], slots_in[ds(g * GS, GS), :].rearrange("(k p) d -> p k d", p=P)
                                 ).then_inc(got, 16)

                def store(g):
                    sp.wait_ge(made, g + 2)
                    sp.dma_start(slots_out[ds(g * GS, GS), :].rearrange("(k p) d -> p k d", p=P), ys[:, :, :]
                                 ).then_inc(stored, 16)

                sp.sem_inc(stored, 16)
                load(0)
                with sp.Fori(0, SHG - 1) as g:
                    load(g + 1)
                    store(g)
                sp.wait_ge(put, 2 * NT * 16)
                load(SHG)
                store(SHG - 1)
                last = sp.value_load(group_i[0:1, E0 + 1:E0 + 2], min_val=SHG + E0, max_val=MAXG)
                with sp.Fori(SHG, last) as g:
                    load(g + 1)
                    store(g)
                sp.wait_ge(stored, last * 16 + 16)
                sp.wait_ge(got, last * 16 + 16)
                sp.sem_inc(passed[4], 1)

            @block.tensor
            def _(pe):
                pe.sem_inc(turned, 1)
                pe.sem_inc(down, 2)

                def turn(g):
                    pe.wait_ge(got, (g + 1) * 16)
                    if not isinstance(g, int):
                        pe.wait_ge(xt_put, g)
                    pe.sem_inc(passed[1], 1)
                    for k in range(2):
                        for j in range(2):
                            ins = nc.tensor.transpose(pT[:, k, j * P:(j + 1) * P], xg[:, j, k * P:(k + 1) * P],
                                                      c.ident[:, :])
                    ins.then_inc(turned, 1)

                def expert(span, b, loads):
                    pe.wait_ge(w_loaded[b], loads * 64)
                    pe.sem_inc(passed[1], 1)
                    with pe.Fori(*span) as g:
                        pe.wait_ge(xt_put, g + 1)
                        for f in range(FT0):
                            pe.wait_ge(bent, g * FT0 + (f + FT0 - 3))
                            pe.sem_inc(passed[1], 1)
                            for k in range(2):
                                ins = nc.tensor.matmul(p1[f % 4][:, :], w1[b][:, k, f * P:(f + 1) * P], xt[:, k, :],
                                                       start=(k == 0), stop=(k == 1))
                            ins.then_inc(up, 1)
                        turn(g + 1)
                        pe.wait_ge(bent, (g + 2) * FT0)
                        pe.wait_ge(made, g + 1)
                        pe.sem_inc(passed[1], 1)
                        for t in range(2):
                            for f in range(FT0):
                                ins = nc.tensor.matmul(p2[t][:, :], hT[:, f, t * P:(t + 1) * P], w2[b][:, f, :],
                                                       start=(f == 0), stop=(f == FT0 - 1))
                            ins.then_inc(down, 1)

                turn(0)
                experts(pe, expert)

            @block.scalar
            def _(act):
                act.sem_inc(bent, FT0)

                def expert(span, b, loads):
                    act.wait_ge(w_loaded[b], loads * 64)
                    act.sem_inc(passed[2], 1)
                    with act.Fori(*span) as g:
                        act.wait_ge(down, g * 2 + 2)
                        for f in range(FT0):
                            act.wait_ge(up, g * FT0 + (f + 1))
                            act.sem_inc(passed[2], 1)
                            nc.scalar.activation(hT[:, f, :], p1[f % 4][:, :], ACT.Gelu, bias=b1[b][:, f:f + 1]
                                                 ).then_inc(bent, 1)

                experts(act, expert)

            @block.vector
            def _(dve):
                v = nc.vector
                dve.sem_inc(made, 1)

                def copy(g):
                    dve.wait_ge(turned, g + 2)
                    dve.sem_inc(passed[3], 1)
                    v.tensor_copy(xt[:, :, :], pT[:, :, :]).then_inc(xt_put, 1)

                def expert(span, b, loads):
                    dve.wait_ge(w_loaded[b], loads * 64)
                    dve.sem_inc(passed[3], 1)
                    with dve.Fori(*span) as g:
                        copy(g + 1)
                        dve.wait_ge(stored, (g + 1) * 16)
                        for t in range(2):
                            dve.wait_ge(down, g * 2 + (3 + t))
                            dve.sem_inc(passed[3], 1)
                            ins = v.tensor_tensor(ys[:, t, :], p2[t][:, :], b2[b][:, :], ALU.add)
                        ins.then_inc(made, 1)
                    dve.wait_ge(made, span[1] + 1)
                    dve.sem_inc(done, 1)

                copy(0)
                experts(dve, expert)


def combine(nc, kit, c, slot_i, w1, w2, slots_out, X, emb, table):
    R = 4
    with kit.stage() as st:
        sb, sem = st.sb, st.sem
        shared = sb("shared", [P, R, D])
        routed = sb("routed", [P, R, 2, D])
        stats = sb("stats", [P, UT, 6])
        mv = sb("mv", [P, UT, 2])
        std, rstd, eps = sb("std", [P, UT]), sb("rstd", [P, UT]), sb("eps", [P, 1])
        loaded = [sem(f"loaded{k}") for k in range(R)]
        got = [st.pool_sem(f"got{k}") for k in range(R)]
        own, added, varied, rooted = sem("own"), sem("added"), sem("varied"), sem("rooted")
        normed, stored = sem("normed"), sem("stored")
        with nc.Block() as block:
            @block.sync
            def _(sp):
                for t in range(NT):
                    if t >= R:
                        sp.wait_ge(added, t - R + 1)
                    sp.dma_start(shared[:, t % R, :], slots_out[t * P:(t + 1) * P, :]).then_inc(loaded[t % R], 16)

            @block.gpsimd
            def _(pool):
                for t in range(NT):
                    if t >= R:
                        pool.wait_ge(added, t - R + 1)
                    for j in range(2):
                        pool.indirect_dma_start(routed[:, t % R, j, :], None, slots_out,
                                                bass.IndirectOffsetOnAxis(ap=slot_i[:, t, j:j + 1], axis=0)
                                                ).then_inc(got[t % R], 16)

            @block.scalar
            def _(act):
                for i in range(NB):
                    act.wait_ge(varied, i + 2)
                    nc.scalar.activation(std[:, :], mv[:, :, 1], ACT.Sqrt, bias=eps[:, :]).then_inc(rooted, 1)
                    act.wait_ge(normed, (i + 1) * UT)
                    act.dma_start(table[i * UT * P:(i + 1) * UT * P, :].rearrange("(k p) d -> p k d", p=P),
                                  emb[:, i * UT:(i + 1) * UT, :]).then_inc(stored, 16)
                act.wait_ge(stored, 16 * NB)

            @block.vector
            def _(dve):
                v = nc.vector
                ch = Chain(dve, own)
                v.memset(eps[:, :], LN_EPS).then_inc(varied, 1)

                def add(t):
                    dve.wait_ge(loaded[t % R], (t // R + 1) * 16)
                    ch.link(v.tensor_tensor(X[:, t, :], X[:, t, :], shared[:, t % R, :], ALU.add))
                    dve.wait_ge(got[t % R], (t // R + 1) * 32)
                    ch.link(v.scalar_tensor_tensor(out=X[:, t, :], in0=routed[:, t % R, 0, :], scalar=w1[:, t, :],
                                                   in1=X[:, t, :], op0=ALU.mult, op1=ALU.add))
                    v.scalar_tensor_tensor(out=X[:, t, :], in0=routed[:, t % R, 1, :], scalar=w2[:, t, :],
                                           in1=X[:, t, :], op0=ALU.mult, op1=ALU.add).then_inc(added, 1)

                for i in range(NB):
                    tiles = range(i * UT, (i + 1) * UT)
                    for t in tiles:
                        add(t)
                    dve.wait_ge(added, tiles.stop)
                    for k, t in enumerate(tiles):
                        ins = v.bn_stats(stats[:, k, :], X[:, t, :])
                    ch.link(ins)
                    for k in range(UT):
                        ins = v.bn_aggr(mv[:, k, :], stats[:, k, :])
                    ins.then_inc(varied, 1)
                    dve.wait_ge(rooted, i + 1)
                    ch.link(v.reciprocal(rstd[:, :], std[:, :]))
                    for k, t in enumerate(tiles):
                        v.tensor_scalar(emb[:, t, :], X[:, t, :], mv[:, k, 0:1], rstd[:, k:k + 1],
                                        ALU.subtract, ALU.mult).then_inc(normed, 1)
                    dve.wait_ge(normed, tiles.stop)


def experts_relu(nc, kit, c, a, xT, gate, X, out):
    with kit.stage() as st:
        sb, ps, sem = st.sb, st.ps, st.sem
        sw1, sw2, sw3 = sb("sw1", [P, 2, D]), sb("sw2", [P, 2, P]), sb("sw3", [P, D])
        ew1, ew2, ew3 = sb("ew1", [P, E1, 2, P]), sb("ew2", [P, E1, 64]), sb("ew3", [64, E1, D])
        sb1, sb2, sb3 = sb("sb1", [P, 2]), sb("sb2", [P, 1]), sb("sb3", [P, D])
        eb1, eb2, eb3 = sb("eb1", [P, E1]), sb("eb2", [64, E1]), sb("eb3", [P, E1, D])
        h1 = sb("h1", [P, 6, UT * P])
        h2 = sb("h2", [P, UT * P])
        g2 = sb("g2", [64, E1, UT * P])
        tmp = sb("tmp", [P, 5, D])
        p1 = [ps(f"p1{k}", [P, 512]) for k in range(4)]
        p3 = [ps(f"p3{k}", [P, 512]) for k in range(4)]
        loaded, up, bent, down, tmp_made, added, stored = (sem(x) for x in (
            "loaded", "up", "bent", "down", "tmpm", "added", "stored"))
        UPS = 2 * (6 + 5)
        NL = 12
        with nc.Block() as block:
            @block.sync
            def _(sp):
                for to, fr in (
                        (sw1[:, :, :], a["L1_ffn_sW1"].rearrange("(k p) f -> p k f", p=P)),
                        (sw2[:, :, :], a["L1_ffn_sW2"].rearrange("(k p) f -> p k f", p=P)),
                        (sw3[:, :], a["L1_ffn_sW3"]),
                        (ew1[:, :, :, :].rearrange("p e k f -> p (e k) f"),
                         a["L1_ffn_eW1"].rearrange("e (k p) f -> p (e k) f", p=P)),
                        (ew2[:, :, :], a["L1_ffn_eW2"].rearrange("e p f -> p e f")),
                        (ew3[:, :, :], a["L1_ffn_eW3"].rearrange("e p f -> p e f")),
                        (sb1[:, :], a["L1_ffn_sb1"]),
                        (sb2[:, :], a["L1_ffn_sb2"]),
                        (sb3[:, :], a["L1_ffn_sb3"].rearrange("(o d) -> o d", o=1).to_broadcast([P, D])),
                        (eb1[:, :], a["L1_ffn_eb1"]),
                        (eb2[:, :], a["L1_ffn_eb2"]),
                        (eb3[:, :, :].rearrange("p e d -> p (e d)"),
                         a["L1_ffn_eb3"].rearrange("(o e) d -> o (e d)", o=1).to_broadcast([P, E1 * D]))):
                    sp.dma_start(to, fr).then_inc(loaded, 16)
                with sp.Fori(0, NB) as i:
                    sp.wait_ge(added, (i + 1) * UT * 5)
                    sp.dma_start(out[ds(i * UT * P, UT * P), :].rearrange("(k p) d -> p k d", p=P),
                                 X[:, ds(i * UT, UT), :]).then_inc(stored, 16)
                sp.wait_ge(stored, 16 * NB)

            @block.tensor
            def _(pe):
                pe.wait_ge(loaded, NL * 16)
                pe.sem_inc(down, 1)
                with pe.Fori(0, NB) as i:
                    o = i * UPS
                    def bank(u):
                        pe.wait_ge(bent, o + (1 + max(u - 3, 0)))
                        return p1[u % 4]
                    for m in range(2):
                        cols = slice(m * CH, (m + 1) * CH)
                        for f in range(6):
                            pb = bank(m * 11 + f)
                            for k in range(2):
                                w = sw1[:, k, f * P:(f + 1) * P] if f < 2 else ew1[:, f - 2, k, :]
                                ins = nc.tensor.matmul(pb[:, 0:CH], w, xT[:, k, ds(i * UT * P + m * CH, CH)],
                                                       start=(k == 0), stop=(k == 1))
                            ins.then_inc(up, 1)
                        pb = bank(m * 11 + 6)
                        pe.wait_ge(bent, o + (m * 11 + 7))
                        for k in range(2):
                            ins = nc.tensor.matmul(pb[:, 0:CH], sw2[:, k, :], h1[:, k, cols],
                                                   start=(k == 0), stop=(k == 1))
                        ins.then_inc(up, 1)
                        for e in range(E1):
                            pb = bank(m * 11 + 7 + e)
                            nc.tensor.matmul(pb[0:64, 0:CH], ew2[:, e, :], h1[:, 2 + e, cols],
                                             start=True, stop=True).then_inc(up, 1)
                    for t in range(UT):
                        pe.wait_ge(bent, o + (12 if (t + 1) * P <= CH else 23))
                        for e in range(5):
                            j = t * 5 + e
                            pe.wait_ge(tmp_made, i * (5 * UT) + (1 + max(j - 3, 0)))
                            lhs = h2[:, t * P:(t + 1) * P] if e == 0 else g2[:, e - 1, t * P:(t + 1) * P]
                            rhs = sw3[:, :] if e == 0 else ew3[:, e - 1, :]
                            nc.tensor.matmul(p3[j % 4][:, 0:D], lhs, rhs, start=True, stop=True).then_inc(down, 1)

            @block.scalar
            def _(act):
                act.wait_ge(loaded, NL * 16)
                act.sem_inc(bent, 1)
                with act.Fori(0, NB) as i:
                    act.wait_ge(down, i * (5 * UT) + 1)
                    for m in range(2):
                        cols = slice(m * CH, (m + 1) * CH)
                        for j in range(11):
                            u = m * 11 + j
                            act.wait_ge(up, i * UPS + (u + 1))
                            pb = p1[u % 4]
                            if j < 6:
                                to, fr = h1[:, j, cols], pb[:, 0:CH]
                                bias = sb1[:, j:j + 1] if j < 2 else eb1[:, j - 2:j - 1]
                            elif j == 6:
                                to, fr, bias = h2[:, cols], pb[:, 0:CH], sb2[:, :]
                            else:
                                to, fr, bias = g2[:, j - 7, cols], pb[0:64, 0:CH], eb2[:, j - 7:j - 6]
                            nc.scalar.activation(to, fr, ACT.Relu, bias=bias).then_inc(bent, 1)

            @block.vector
            def _(dve):
                v = nc.vector
                dve.wait_ge(loaded, NL * 16)
                dve.sem_inc(tmp_made, 1)
                with dve.Fori(0, NB) as i:
                    for t in range(UT):
                        n = ds(i * UT + t)
                        x = X[:, n, :].rearrange("p o d -> p (o d)")
                        for e in range(5):
                            j = t * 5 + e
                            dve.wait_ge(down, i * (5 * UT) + (j + 2))
                            b = sb3[:, :] if e == 0 else eb3[:, e - 1, :]
                            v.tensor_tensor(tmp[:, e, :], p3[j % 4][:, 0:D], b, ALU.add).then_inc(tmp_made, 1)
                            dve.wait_ge(tmp_made, i * (5 * UT) + (j + 2))
                            if j:
                                dve.wait_ge(added, i * (5 * UT) + j)
                            if e == 0:
                                ins = v.tensor_tensor(x, x, tmp[:, e, :], ALU.add)
                            else:
                                ins = v.scalar_tensor_tensor(out=x, in0=tmp[:, e, :],
                                                             scalar=gate[:, n, e - 1:e].rearrange("p o e -> p (o e)"),
                                                             in1=x, op0=ALU.mult, op1=ALU.add)
                            ins.then_inc(added, 1)


class Consts:
    pass


def loads(nc, kit, pairs):
    with kit.stage() as st:
        loaded = st.sem("loaded")
        with nc.Block() as block:
            @block.sync
            def _(sp):
                for to, fr in pairs:
                    sp.dma_start(to, fr).then_inc(loaded, 16)
                sp.wait_ge(loaded, 16 * len(pairs))


def program(nc, a, out):
    kit = Kit(nc)
    c = Consts()

    def dram(name, shape, dt=F32):
        return nc.dram_tensor(name, shape, dt).ap()

    c.t_src, c.t_dst = dram("t_src", [TROWS, P], I32), dram("t_dst", [TROWS, P], I32)
    c.t_w = dram("t_w", [TROWS, P])
    c.pay = dram("pay", [TROWS, P * H])
    c.spread = dram("spread", [EP, 2 * H])
    c.emax = dram("emax", [EP, H])
    slots_in, slots_out = (dram(n, [(MAXG + 1) * GS, D]) for n in ("slots_in", "slots_out"))
    c.slots_in, c.slots_out = slots_in, slots_out
    table = [dram(f"table{k}", [NP, D]) for k in range(2)]
    c.src_logit = dram("src_logit", [NP, H])

    with kit.stage() as whole:
        c.ident, c.ones = whole.sb("ident", [P, P]), whole.sb("ones", [P, P])
        c.iota = whole.sb("iota", [P, P + 1])
        c.far_i = whole.sb("far_i", [P, P], I32)
        c.idx = whole.sb("idx", [P, GMAX], I32)
        c.drel, c.ew = whole.sb("drel", [P, GMAX]), whole.sb("ew", [P, GMAX])
        c.first_step = whole.sb("first_step", [1, NT + 1], I32)
        X = whole.sb("X", [P, NT, D])
        with kit.stage() as gat:
            c.te_i = gat.sb("te_i", [P, GC], I32)
            c.first_edge = gat.sb("first_edge", [P, NT], I32)
            c.goes_on = gat.sb("goes_on", [P, EC])
            c.pen_fwd = gat.sb("pen_fwd", [P, EC])
            c.pen_bwd = gat.sb("pen_bwd", [P, EC])
            c.edge_pen = gat.sb("edge_pen", [P, 3])
            c.src_tile = gat.sb("src_tile", [P, LOOK])
            c.src_within = gat.sb("src_within", [P, LOOK_C, P], BF16)
            c.ident_h = gat.sb("ident_h", [P, P], BF16)
            c.paid = gat.sb("paid", [P, GMAX, H])
            c.self_w = gat.sb("self_w", [P, NT, H])
            c.wps = [gat.sb(f"wp{l}", [P, 2, D + 2 * H]) for l in range(3)]
            c.gbiases = [gat.sb(f"gbias{l}", [P, D]) for l in range(3)]
            c.logit = gat.sb("logit", [P, NT, 2 * H])
            constants(nc, kit, c)
            step_tables(nc, kit, c, a)
            source_parts(nc, kit, c, a)
            attention_weights(nc, kit, c, a)
            c.wp = c.wps[0]
            norm_stage(nc, kit, c, a, None, "input", {"rows": table[0], "logits": c.src_logit}, "project")
            for layer in range(3):
                edge_softmax(nc, kit, c, a, layer)
                with kit.stage() as st:
                    accs = st.sb("accs", [P, NT, RW])
                    edge_pass(nc, kit, c, table[layer % 2], True, accs)
                    c.wp, c.gbias = c.wps[min(layer + 1, 2)], c.gbiases[layer]
                    outs = ({"rows": table[(layer + 1) % 2], "logits": c.src_logit} if layer < 2
                            else {"sbuf": X})
                    attention_end(nc, kit, c, table[layer % 2], accs, outs)
        with kit.stage() as rest:
            xT = rest.sb("xT", [P, 2, NP])
            gate = rest.sb("gate", [P, NT, E1])
            gw, gb = rest.sb("gw", [P, 2, E1]), rest.sb("gb", [E1, 1])
            with kit.stage() as st:
                rows = st.sb("rows", [P, NT, D])
                with kit.stage() as moe:
                    pick = moe.sb("pick", [P, NT, 2])
                    w1, w2 = moe.sb("w1", [P, NT, 1]), moe.sb("w2", [P, NT, 1])
                    slot_i = moe.sb("slot_i", [P, NT, 2], I32)
                    group_i = moe.sb("group_i", [1, E0 + 2], I32)
                    wr = moe.sb("wr", [P, 2, E0])
                    norm_stage(nc, kit, c, a, X, "input", {"sbuf": xT, "rows": slots_in, "rows_sb": rows}, "both")
                    loads(nc, kit, [(wr[:, :, :], a["L0_ffn_Wr"].rearrange("(k p) e -> p k e", p=P))])
                    router(nc, kit, c, xT, wr, E0, None, pick, w1, w2, None)
                    assign_slots(nc, kit, c, pick, slot_i, group_i)
                    hT = xT[:, 0, 0:FT0 * GS].rearrange("p (f s) -> p f s", f=FT0)
                    experts_gelu(nc, kit, c, a, rows, slot_i, group_i, slots_in, slots_out, hT)
                    combine(nc, kit, c, slot_i, w1, w2, slots_out, X, rows, table[0])
                sumsq = st.sb("sumsq", [P, NT])
                w = st.sb("w", [P, 4, D])
                c.gbias = st.sb("gbias", [P, D])
                b = st.sb("b", [P, D])
                loads(nc, kit, [
                    (w[:, 0:2, :], a["W1T"].rearrange("(k p) n -> p k n", p=P)),
                    (w[:, 2:4, :], a["W2T"].rearrange("(k p) n -> p k n", p=P)),
                    (c.gbias[:, :], a["L1_gnn_b1"].rearrange("(o n) -> o n", o=1).to_broadcast([P, D])),
                    (b[:, :], a["L1_gnn_b2"].rearrange("(o n) -> o n", o=1).to_broadcast([P, D])),
                    (gw[:, :, :], a["L1_ffn_gW"].rearrange("(k p) e -> p k e", p=P)),
                    (gb[:, :], a["L1_ffn_gb"])])
                add_into(nc, kit, c.gbias[:, :], b[:, :])
                sums = xT[:, :, :].rearrange("p k n -> p (k n)").rearrange("p (t d) -> p t d", d=D)
                edge_pass(nc, kit, c, table[0], False, sums)
                mix_end(nc, kit, c, lambda t: sums[:, t, :], {"sbuf": rows, "w": w, "sumsq": sumsq})
                inverse_norms(nc, kit, sumsq)
                norm_stage(nc, kit, c, a, X, "scaled", {"sbuf": xT, "adds": rows, "scale": sumsq}, "turned")
            with kit.stage() as st:
                router(nc, kit, c, xT, gw, E1, gb, st.sb("pick", [P, NT, 2]), st.sb("w1", [P, NT, 1]),
                       st.sb("w2", [P, NT, 1]), gate)
            experts_relu(nc, kit, c, a, xT, gate, X, out)


def add_into(nc, kit, to, ap):
    with kit.stage() as st:
        done = st.sem("done")
        with nc.Block() as block:
            @block.vector
            def _(dve):
                nc.vector.tensor_tensor(to, to, ap, ALU.add).then_inc(done, 1)


def inverse_norms(nc, kit, s):
    with kit.stage() as st:
        rooted, own = st.sem("rooted"), st.sem("own")
        with nc.Block() as block:
            @block.scalar
            def _(act):
                nc.scalar.activation(s[:, :], s[:, :], ACT.Sqrt).then_inc(rooted, 1)

            @block.vector
            def _(dve):
                dve.wait_ge(rooted, 1)
                nc.vector.tensor_scalar(s[:, :], s[:, :], 1e-12, None, ALU.max).then_inc(own, 1)
                dve.wait_ge(own, 1)
                nc.vector.reciprocal(s[:, :], s[:, :]).then_inc(own, 1)



def kernel(**inputs):
    import concourse.bacc as bacc
    from concourse.bass_utils import run_bass_kernel_spmd

    nc = bacc.Bacc("TRN2", target_bir_lowering=False, num_devices=1)
    v = {k: np.asarray(x) for k, x in inputs.items()}
    v["x"] = np.concatenate([v["x"], np.zeros((NP - NN, D), v["x"].dtype)])
    v["src"] = np.concatenate([v["src"], np.zeros(EP - NE, v["src"].dtype)])
    v["dst"] = np.concatenate([np.full(1, -1, v["dst"].dtype), v["dst"],
                               np.full(EP - NE + 1, FAR, v["dst"].dtype)])
    v["edge_weight"] = np.concatenate([v["edge_weight"], np.zeros(EP - NE, v["edge_weight"].dtype)])
    v["W1all"] = np.concatenate([v.pop("L0_ffn_W1s")[None], v.pop("L0_ffn_W1p")])
    v["b1all"] = np.concatenate([v.pop("L0_ffn_b1s")[None], v.pop("L0_ffn_b1p")])
    v["b1all"] = v["b1all"].reshape(E0 + 1, FT0, P).transpose(0, 2, 1)
    v["L1_ffn_sb1"] = v["L1_ffn_sb1"].reshape(2, P).T
    v["L1_ffn_sb2"] = v["L1_ffn_sb2"].reshape(P, 1)
    v["L1_ffn_eb1"], v["L1_ffn_eb2"] = v["L1_ffn_eb1"].T, v["L1_ffn_eb2"].T
    v["L1_ffn_gb"] = v["L1_ffn_gb"].reshape(E1, 1)
    v["W2all"] = np.concatenate([v.pop("L0_ffn_W2s")[None], v.pop("L0_ffn_W2p")])
    v["b2all"] = np.concatenate([v.pop("L0_ffn_b2s")[None], v.pop("L0_ffn_b2p")])
    v["W1T"] = v.pop("L1_gnn_W1").T
    v["W2T"] = v.pop("L1_gnn_W2").T
    arrays, aps = {}, {}
    for name, x in v.items():
        arrays[f"in_{name}"] = np.ascontiguousarray(x)
        aps[name] = nc.dram_tensor(f"in_{name}", x.shape, mybir.dt.from_np(x.dtype), kind="ExternalInput").ap()
    out = nc.dram_tensor("out_x", (NP, D), F32, kind="ExternalOutput").ap()
    program(nc, aps, out)
    r = run_bass_kernel_spmd(nc, [arrays], core_ids=[0])
    return r.results[0]["out_x"][0:NN]
```
